# Optimizing a Trainium2 kernel written in Bass

```python
import numpy as np
import jax
import jax.numpy as jnp

def _softmax(x, axis=-1):
    return jax.nn.softmax(x, axis=axis)

def _gelu(x):
    return jax.nn.gelu(x, approximate=True)

def _silu(x):
    return jax.nn.silu(x)

def _sigmoid(x):
    return jax.nn.sigmoid(x)

def _layernorm(x, axis=-1, eps=1e-05):
    m = jnp.mean(x, axis=axis, keepdims=True)
    v = jnp.var(x, axis=axis, keepdims=True)
    return (x - m) / jnp.sqrt(v + eps)

def _scatter_add(tgt, idx, src, axis=0):
    return tgt.at[idx].add(src)

def _segment_sum(src, seg, n):
    return jax.ops.segment_sum(src, seg, n)
kernel_name = 'mk_perceiver_d1_seqx_r2_e9bed4'

def setup_inputs(seed: int=0):
    np.random.seed(seed)
    _w = jnp.asarray

    def _rec_inputs():
        import jax
        import jax.numpy as jnp
        _rk = jax.random.key(seed)
        x = -0.0002928 + 1 * jax.random.normal(jax.random.fold_in(_rk, 1), (4, 128, 512), jnp.float32)
        _lenS = 128 - jax.random.randint(jax.random.fold_in(_rk, 7), (4,), 0, max(1, 128 // 4) + 1, jnp.int32)
        _lenS2 = 2048 - jax.random.randint(jax.random.fold_in(_rk, 8), (4,), 0, max(1, 2048 // 4) + 1, jnp.int32)
        _ctx_1024P = jax.random.normal(jax.random.fold_in(_rk, 11), (4, 16, 512), jnp.float32)
        _ctx_1024c = jax.random.dirichlet(jax.random.fold_in(_rk, 511), 0.3 * jnp.ones((16,), jnp.float32), (4, 2048))
        _ctx_1024t = jnp.einsum('bsk,bkd->bsd', _ctx_1024c, _ctx_1024P)
        _ctx_1024t = _ctx_1024t * jax.lax.rsqrt(jnp.mean(jnp.square(_ctx_1024t)) + 1e-12) * 0.953939
        ctx_1024 = -1.39393e-06 + 0.999914 * (_ctx_1024t + 0.3 * jax.random.normal(jax.random.fold_in(_rk, 611), (4, 2048, 512), jnp.float32))
        return (x, ctx_1024)
    x, ctx_1024 = _rec_inputs()

    def _L0_xattn_setup():
        import jax, jax.numpy as jnp
        import numpy as np
        NUM_HEADS = 16
        KEY_SIZE = 64
        VALUE_SIZE = 64
        MODEL_SIZE = 512
        B, S, D = (2, 1024, 512)

        def _vs_init(key, shape):
            fan_in = shape[0]
            stddev = np.sqrt(1.0 / fan_in) / 0.8796256610342398
            return stddev * jax.random.truncated_normal(key, -2.0, 2.0, shape, dtype=jnp.float32)
        key = jax.random.key(seed)
        ks = jax.random.split(key, 7)
        query = jax.random.normal(ks[0], (B, S, D), dtype=jnp.float32)
        k_in = jax.random.normal(ks[1], (B, S, D), dtype=jnp.float32)
        v_in = jax.random.normal(ks[2], (B, S, D), dtype=jnp.float32)
        Wq = _vs_init(ks[3], (D, NUM_HEADS * KEY_SIZE))
        Wk = _vs_init(ks[4], (D, NUM_HEADS * KEY_SIZE))
        Wv = _vs_init(ks[5], (D, NUM_HEADS * VALUE_SIZE))
        Wo = _vs_init(ks[6], (NUM_HEADS * VALUE_SIZE, MODEL_SIZE))
        bq = jnp.zeros((NUM_HEADS * KEY_SIZE,), jnp.float32)
        bk = jnp.zeros((NUM_HEADS * KEY_SIZE,), jnp.float32)
        bv = jnp.zeros((NUM_HEADS * VALUE_SIZE,), jnp.float32)
        bo = jnp.zeros((MODEL_SIZE,), jnp.float32)
        return {'query': query, 'key': k_in, 'value': v_in, 'Wq': Wq, 'bq': bq, 'Wk': Wk, 'bk': bk, 'Wv': Wv, 'bv': bv, 'Wo': Wo, 'bo': bo}
    _L0_xattn_all = _L0_xattn_setup()
    _L0_xattn_in = {k: v for k, v in _L0_xattn_all.items() if k in ('Wq', 'bq', 'Wk', 'bk', 'Wv', 'bv', 'Wo', 'bo')}
    del _L0_xattn_all

    def _L0_attn_setup():
        import jax, jax.numpy as jnp
        import numpy as np
        EMBED_DIM = 512
        NUM_HEADS = 16
        HEAD_DIM = EMBED_DIM // NUM_HEADS
        BATCH = 2
        SEQ = 1024
        key = jax.random.key(seed)
        k1, k2, k3, k4, k5 = jax.random.split(key, 5)
        scale_in = 1.0 / np.sqrt(EMBED_DIM)
        return {'x': jax.random.normal(k1, (BATCH, SEQ, EMBED_DIM), dtype=jnp.float32), 'head_mask': jnp.ones((NUM_HEADS,), dtype=jnp.float32), 'qkv_w': jax.random.normal(k2, (3 * EMBED_DIM, EMBED_DIM), dtype=jnp.float32) * scale_in, 'qkv_b': jax.random.normal(k3, (3 * EMBED_DIM,), dtype=jnp.float32) * 0.02, 'fc_w': jax.random.normal(k4, (EMBED_DIM, EMBED_DIM), dtype=jnp.float32) * scale_in, 'fc_b': jax.random.normal(k5, (EMBED_DIM,), dtype=jnp.float32) * 0.02}
    _L0_attn_all = _L0_attn_setup()
    _L0_attn_in = {k: v for k, v in _L0_attn_all.items() if k in ('head_mask', 'qkv_w', 'qkv_b', 'fc_w', 'fc_b')}
    del _L0_attn_all

    def _L0_ffn_setup():
        import jax, jax.numpy as jnp
        import numpy as np
        import math
        HID, HD, E, MIN_E = (512, 128, 16, 2)
        B, T = (4, 1024)
        IS_CAUSAL = True

        def _l2norm(x, axis):
            return x / jnp.sqrt(jnp.sum(x * x, axis=axis, keepdims=True) + 1e-12)

        def _gating(hidden_states, sim_matrix, gates):
            b, t, c = hidden_states.shape
            flat = hidden_states.reshape(b * t, c)
            logits = _l2norm(flat, -1) @ _l2norm(sim_matrix, 0) - jax.nn.sigmoid(gates)
            gated = jax.nn.relu(logits)
            mask = (gated > 0).astype(gated.dtype)
            inactive = jnp.sum(mask, axis=1) == 0
            _, top_idx = jax.lax.top_k(logits, MIN_E)
            fb = jnp.sum(jax.nn.one_hot(top_idx, E, dtype=mask.dtype), axis=1)
            mask = mask + inactive[:, None].astype(mask.dtype) * fb
            masked = jnp.where(mask > 0, gated, -jnp.inf)
            probs = jax.nn.softmax(masked, axis=-1)
            return probs
        key = jax.random.key(seed)
        ks = jax.random.split(key, 6)
        a_qkv = math.sqrt(6.0 / (HID + HD))
        a_o = math.sqrt(6.0 / (HD + HID))
        return {'hidden_states': jax.random.normal(ks[0], (B, T, HID), jnp.float32), 'sim_matrix': jax.random.normal(ks[1], (HID, E), jnp.float32), 'gates': jnp.zeros((E,), jnp.float32), 'q_proj': jax.random.uniform(ks[2], (E, HID, HD), jnp.float32, -a_qkv, a_qkv), 'k_proj': jax.random.uniform(ks[3], (E, HID, HD), jnp.float32, -a_qkv, a_qkv), 'v_proj': jax.random.uniform(ks[4], (E, HID, HD), jnp.float32, -a_qkv, a_qkv), 'o_proj': jax.random.uniform(ks[5], (E, HD, HID), jnp.float32, -a_o, a_o)}
    _L0_ffn_all = _L0_ffn_setup()
    _L0_ffn_in = {k: v for k, v in _L0_ffn_all.items() if k in ('sim_matrix', 'gates', 'q_proj', 'k_proj', 'v_proj', 'o_proj')}
    del _L0_ffn_all
    return {'x': x, 'ctx_1024': ctx_1024, 'L0_xattn_Wq': _L0_xattn_in['Wq'], 'L0_xattn_bq': _L0_xattn_in['bq'], 'L0_xattn_Wk': _L0_xattn_in['Wk'], 'L0_xattn_bk': _L0_xattn_in['bk'], 'L0_xattn_Wv': _L0_xattn_in['Wv'], 'L0_xattn_bv': _L0_xattn_in['bv'], 'L0_xattn_Wo': _L0_xattn_in['Wo'], 'L0_xattn_bo': _L0_xattn_in['bo'], 'L0_attn_head_mask': _L0_attn_in['head_mask'], 'L0_attn_qkv_w': _L0_attn_in['qkv_w'], 'L0_attn_qkv_b': _L0_attn_in['qkv_b'], 'L0_attn_fc_w': _L0_attn_in['fc_w'], 'L0_attn_fc_b': _L0_attn_in['fc_b'], 'L0_ffn_sim_matrix': _L0_ffn_in['sim_matrix'], 'L0_ffn_gates': _L0_ffn_in['gates'], 'L0_ffn_q_proj': _L0_ffn_in['q_proj'], 'L0_ffn_k_proj': _L0_ffn_in['k_proj'], 'L0_ffn_v_proj': _L0_ffn_in['v_proj'], 'L0_ffn_o_proj': _L0_ffn_in['o_proj']}

def reference(x, ctx_1024, L0_xattn_Wq, L0_xattn_bq, L0_xattn_Wk, L0_xattn_bk, L0_xattn_Wv, L0_xattn_bv, L0_xattn_Wo, L0_xattn_bo, L0_attn_head_mask, L0_attn_qkv_w, L0_attn_qkv_b, L0_attn_fc_w, L0_attn_fc_b, L0_ffn_sim_matrix, L0_ffn_gates, L0_ffn_q_proj, L0_ffn_k_proj, L0_ffn_v_proj, L0_ffn_o_proj):
    import jax
    import jax.numpy as jnp

    def _L0_xattn_ref(query, key, value, Wq, bq, Wk, bk, Wv, bv, Wo, bo):
        import jax, jax.numpy as jnp
        import numpy as np
        NUM_HEADS = 16
        KEY_SIZE = 64
        VALUE_SIZE = 64
        MODEL_SIZE = 512
        B, S, D = (2, 1024, 512)

        def _vs_init(key, shape):
            fan_in = shape[0]
            stddev = np.sqrt(1.0 / fan_in) / 0.8796256610342398
            return stddev * jax.random.truncated_normal(key, -2.0, 2.0, shape, dtype=jnp.float32)
        b, s, _ = query.shape
        q = (query @ Wq + bq).reshape(b, s, NUM_HEADS, KEY_SIZE)
        k = (key @ Wk + bk).reshape(b, key.shape[1], NUM_HEADS, KEY_SIZE)
        v = (value @ Wv + bv).reshape(b, value.shape[1], NUM_HEADS, VALUE_SIZE)
        logits = jnp.einsum('bshd,bShd->bhsS', q, k) / np.sqrt(KEY_SIZE).astype(np.float32)
        weights = jax.nn.softmax(logits, axis=-1)
        attn = jnp.einsum('bhsS,bShd->bshd', weights, v).reshape(b, s, NUM_HEADS * VALUE_SIZE)
        return attn @ Wo + bo

    def _L0_attn_ref(x, head_mask, qkv_w, qkv_b, fc_w, fc_b):
        import jax, jax.numpy as jnp
        import numpy as np
        EMBED_DIM = 512
        NUM_HEADS = 16
        HEAD_DIM = EMBED_DIM // NUM_HEADS
        BATCH = 2
        SEQ = 1024
        N, S, D = x.shape
        H, hd = (NUM_HEADS, HEAD_DIM)
        qkv = jnp.einsum('nsd,ed->nse', x, qkv_w) + qkv_b
        qkv = qkv.reshape(N, S, H, 3, hd).transpose(3, 0, 2, 1, 4)
        q, k, v = (qkv[0], qkv[1], qkv[2])
        hm = head_mask.reshape(1, H, 1, 1)
        q = q * hm
        k = k * hm
        v = v * hm
        energy = jnp.einsum('nhqd,nhkd->nhqk', q, k)
        attention = jax.nn.softmax(energy / jnp.sqrt(jnp.float32(hd)), axis=-1)
        out = jnp.einsum('nhqk,nhkd->nhqd', attention, v)
        out = out.transpose(0, 2, 1, 3).reshape(N, S, H * hd)
        out = jnp.einsum('nsd,ed->nse', out, fc_w) + fc_b
        return out

    def _L0_ffn_ref(hidden_states, sim_matrix, gates, q_proj, k_proj, v_proj, o_proj):
        import jax, jax.numpy as jnp
        import numpy as np
        import math
        HID, HD, E, MIN_E = (512, 128, 16, 2)
        B, T = (4, 1024)
        IS_CAUSAL = True

        def _l2norm(x, axis):
            return x / jnp.sqrt(jnp.sum(x * x, axis=axis, keepdims=True) + 1e-12)

        def _gating(hidden_states, sim_matrix, gates):
            b, t, c = hidden_states.shape
            flat = hidden_states.reshape(b * t, c)
            logits = _l2norm(flat, -1) @ _l2norm(sim_matrix, 0) - jax.nn.sigmoid(gates)
            gated = jax.nn.relu(logits)
            mask = (gated > 0).astype(gated.dtype)
            inactive = jnp.sum(mask, axis=1) == 0
            _, top_idx = jax.lax.top_k(logits, MIN_E)
            fb = jnp.sum(jax.nn.one_hot(top_idx, E, dtype=mask.dtype), axis=1)
            mask = mask + inactive[:, None].astype(mask.dtype) * fb
            masked = jnp.where(mask > 0, gated, -jnp.inf)
            probs = jax.nn.softmax(masked, axis=-1)
            return probs
        b, t, c = hidden_states.shape
        rw = _gating(hidden_states, sim_matrix, gates).reshape(b, t, E)
        q = jnp.einsum('btc,ech,bte->bth', hidden_states, q_proj, rw)
        k = jnp.einsum('btc,ech,bte->bth', hidden_states, k_proj, rw)
        v = jnp.einsum('btc,ech,bte->bth', hidden_states, v_proj, rw)
        scale = 1.0 / math.sqrt(HD)
        scores = jnp.einsum('bqh,bkh->bqk', q, k) * scale
        if IS_CAUSAL:
            causal = jnp.tril(jnp.ones((t, t), dtype=bool))
            scores = jnp.where(causal[None], scores, -jnp.inf)
        attn = jax.nn.softmax(scores, axis=-1)
        ao = jnp.einsum('bqk,bkh->bqh', attn, v)
        out = jnp.einsum('bth,ehc,bte->btc', ao, o_proj, rw)
        return out
    x = x + _L0_xattn_ref(_layernorm(x, axis=-1), ctx_1024, ctx_1024, L0_xattn_Wq, L0_xattn_bq, L0_xattn_Wk, L0_xattn_bk, L0_xattn_Wv, L0_xattn_bv, L0_xattn_Wo, L0_xattn_bo)
    x = x + _L0_attn_ref(_layernorm(x, axis=-1), L0_attn_head_mask, L0_attn_qkv_w, L0_attn_qkv_b, L0_attn_fc_w, L0_attn_fc_b)
    x = x + _L0_ffn_ref(_layernorm(x, axis=-1), L0_ffn_sim_matrix, L0_ffn_gates, L0_ffn_q_proj, L0_ffn_k_proj, L0_ffn_v_proj, L0_ffn_o_proj)
    return x

_drawn_inputs = setup_inputs


def setup_inputs(seed=0):
    import zlib

    import numpy as np

    out = dict(_drawn_inputs(seed))
    spreads = {'L0_xattn_bq': (0.0, 0.1),
     'L0_xattn_bk': (0.0, 0.1),
     'L0_xattn_bv': (0.0, 0.1),
     'L0_xattn_bo': (0.0, 0.1),
     'L0_ffn_gates': (0.0, 0.1)}
    factors = {}
    for name, (base, spread) in spreads.items():
        noise = np.random.default_rng([zlib.crc32(name.encode()), seed]).standard_normal(out[name].shape)
        drawn = base * np.exp(spread * noise) if base else spread * noise
        out[name] = jnp.asarray(drawn.astype(out[name].dtype))
    for name, factor in factors.items():
        out[name] = (out[name] * factor).astype(out[name].dtype)
    return out
```

```python
from contextlib import ExitStack

import concourse.bass as bass
from concourse import mybir

F32 = mybir.dt.float32
F32R = mybir.dt.float32r
ALU = mybir.AluOpType
ACT = mybir.ActivationFunctionType
AX = mybir.AxisListType

P = 128
BANK = 512
EPS = 1e-5


class Shapes:

    def __init__(self, x, ctx):
        self.NB, self.TQ, self.D = x.shape
        self.S = ctx.shape[1]
        self.C = self.D // P
        self.H, self.HD = 16, 64
        self.HW = self.H * self.HD
        self.NP = self.H // 2
        self.SB = self.S // BANK
        self.NC = self.S // P
        self.HALF = self.NP // 2


def make_identity(nc, pool, ident, sem):
    nc.gpsimd.memset(ident[:], 0.0).then_inc(sem, 1)
    pool.wait_ge(sem, 1)
    nc.gpsimd.affine_select(out=ident[:], in_=ident[:], compare_op=ALU.not_equal, fill=1.0, base=0,
                            pattern=[[-1, P]], channel_multiplier=1).then_inc(sem, 1)


def prepare(nc, Z, ident, x, Wq, bq, Wk, Wv, wk_s, wv_s, q_s):
    NB, C, NP, D, HW = Z.NB, Z.C, Z.NP, Z.D, Z.HW
    TOK = NB * P
    with ExitStack() as ctx:
        sb = lambda name, shape, dt=F32: ctx.enter_context(nc.sbuf_tensor("a_" + name, shape, dt))
        sem = lambda name: ctx.enter_context(nc.semaphore("a_" + name))
        ps = ctx.enter_context(nc.psum_tensor("a_ps", [P, 8, BANK], F32))
        xs = sb("xs", [P, NB, D])
        xn = sb("xn", [P, NB, D])
        xnT = sb("xnT", [P, C, TOK])
        wq = sb("wq", [P, C, HW])
        w = sb("w", [P, 2, C, HW])
        whi = sb("whi", [P, 2, C, HW], F32R)
        wlo = sb("wlo", [P, 2, C, HW], F32R)
        qhi = sb("qhi", [P, 2, TOK], F32R)
        qlo = sb("qlo", [P, 2, TOK], F32R)
        bqT = sb("bqT", [P, NP])
        stats = sb("stats", [P, NB, 6])
        mv = sb("mv", [P, NB, 2])
        var = sb("var", [P, NB])
        std = sb("std", [P, NB])
        rstd = sb("rstd", [P, NB])

        id_ready = sem("id_ready")
        x_in, wq_in, bq_in = sem("x_in"), sem("wq_in"), sem("bq_in")
        w_in = [sem("wk_in"), sem("wv_in")]
        stats_done, mv_done, var_done = sem("stats_done"), sem("mv_done"), sem("var_done")
        std_done, rstd_done, xn_done = sem("std_done"), sem("rstd_done"), sem("xn_done")
        xT_psum, xT_done = sem("xT_psum"), sem("xT_done")
        q_psum, qhi_done, qlo_done = sem("q_psum"), sem("qhi_done"), sem("qlo_done")
        whi_done, wlo_done, w_stored = sem("whi_done"), sem("wlo_done"), sem("w_stored")
        q_stored = [sem("q_stored0"), sem("q_stored1")]
        block = ctx.enter_context(nc.Block())

        @block.sync
        def _(sp):
            sp.dma_start(xs[:], x.rearrange("b t d -> t b d")).then_inc(x_in, 16)
            sp.dma_start(wq[:], Wq.rearrange("(c p) n -> p c n", p=P)).then_inc(wq_in, 16)
            sp.dma_start(bqT[:], bq.rearrange("(j p) -> p j", p=P), allow_slow_non_contiguous=True).then_inc(bq_in, 16)
            for n, W in enumerate((Wk, Wv)):
                sp.dma_start(w[:, n], W.rearrange("(c p) n -> p c n", p=P)).then_inc(w_in[n], 16)
            for j in range(NP):
                sp.wait_ge(qlo_done, j + 1)
                sp.dma_start(q_s[0, j], qhi[:, j % 2].bitcast(F32)).then_inc(q_stored[j % 2], 16)
                sp.dma_start(q_s[1, j], qlo[:, j % 2].bitcast(F32)).then_inc(q_stored[j % 2], 16)
            for q in q_stored:
                sp.wait_ge(q, 16 * NP)
            sp.wait_ge(w_stored, 16 * 2 * C * 2)

        @block.gpsimd
        def _(pool):
            make_identity(nc, pool, ident, id_ready)
            for n in range(2):
                for c in range(C):
                    pool.wait_ge(wlo_done, n * C + c + 1)
                    for hl, src in enumerate((whi, wlo)):
                        dst = wk_s[:, :, hl, c].rearrange("j p n -> p j n") if n == 0 else \
                            wv_s[:, :, hl, c].rearrange("g p n -> p g n")
                        pool.dma_start(dst, src[:, n, c].bitcast(F32).rearrange("p (j n) -> p j n", j=dst.shape[1])).then_inc(w_stored, 16)

        @block.tensor
        def _(pe):
            pe.wait_ge(id_ready, 2)
            for b in range(NB):
                pe.wait_ge(xn_done, b + 1)
                if b >= 2:
                    pe.wait_ge(xT_done, b - 1)
                for c in range(C):
                    mm = nc.tensor.transpose(ps[:, b % 2, c * P:(c + 1) * P], xn[:, b, c * P:(c + 1) * P], ident[:])
                mm.then_inc(xT_psum, 1)
            pe.wait_ge(wq_in, 16)
            pe.wait_ge(xT_done, NB)
            for j in range(NP):
                if j >= 2:
                    pe.wait_ge(qlo_done, j - 1)
                for c in range(C):
                    mm = nc.tensor.matmul(ps[:, 2 + j % 2, :TOK], wq[:, c, j * P:(j + 1) * P], xnT[:, c, :],
                                          start=c == 0, stop=c == C - 1)
                mm.then_inc(q_psum, 1)

        @block.scalar
        def _(act):
            act.wait_ge(var_done, 1)
            nc.scalar.activation(std[:], var[:], ACT.Sqrt).then_inc(std_done, 1)
            act.wait_ge(bq_in, 16)
            for j in range(NP):
                act.wait_ge(q_psum, j + 1)
                if j >= 2:
                    act.wait_ge(q_stored[j % 2], 32 * (j // 2))
                nc.scalar.activation(qhi[:, j % 2], ps[:, 2 + j % 2, :TOK], ACT.Identity,
                                     bias=bqT[:, j:j + 1]).then_inc(qhi_done, 1)
                n, c = divmod(j, C)
                act.wait_ge(w_in[n], 16)
                nc.scalar.copy(whi[:, n, c], w[:, n, c]).then_inc(whi_done, 1)

        @block.vector
        def _(dve):
            dve.wait_ge(x_in, 16)
            for b in range(NB):
                nc.vector.bn_stats(stats[:, b], xs[:, b]).then_inc(stats_done, 1)
            for b in range(NB):
                dve.wait_ge(stats_done, b + 1)
                nc.vector.bn_aggr(mv[:, b], stats[:, b]).then_inc(mv_done, 1)
            dve.wait_ge(mv_done, NB)
            nc.vector.tensor_scalar(var[:], mv[:, :, 1], EPS, None, ALU.add).then_inc(var_done, 1)
            dve.wait_ge(std_done, 1)
            nc.vector.reciprocal(rstd[:], std[:]).then_inc(rstd_done, 1)
            dve.wait_ge(rstd_done, 1)
            for b in range(NB):
                nc.vector.tensor_scalar(xn[:, b], xs[:, b], mv[:, b, 0:1], rstd[:, b:b + 1],
                                        ALU.subtract, ALU.mult).then_inc(xn_done, 1)
            for b in range(NB):
                dve.wait_ge(xT_psum, b + 1)
                nc.vector.tensor_copy(xnT[:, :, b * P:(b + 1) * P],
                                      ps[:, b % 2].rearrange("p (c t) -> p c t", c=C)).then_inc(xT_done, 1)
            dve.wait_ge(bq_in, 16)
            for j in range(NP):
                dve.wait_ge(qhi_done, j + 1)
                if j >= 2:
                    dve.wait_ge(q_stored[j % 2], 32 * (j // 2))
                nc.vector.scalar_tensor_tensor(qlo[:, j % 2], ps[:, 2 + j % 2, :TOK], bqT[:, j:j + 1],
                                               qhi[:, j % 2].bitcast(F32), ALU.add, ALU.subtract).then_inc(qlo_done, 1)
                n, c = divmod(j, C)
                dve.wait_ge(whi_done, j + 1)
                nc.vector.tensor_tensor(wlo[:, n, c], w[:, n, c], whi[:, n, c].bitcast(F32),
                                        ALU.subtract).then_inc(wlo_done, 1)


def cross_attention(nc, Z, ident, ctx_in, bk, bv, wk_s, wv_s, q_s, attn_s):
    NB, C, NP, S, SB, NC, D, HD, HALF = Z.NB, Z.C, Z.NP, Z.S, Z.SB, Z.NC, Z.D, Z.HD, Z.HALF
    SCALE = HD ** -0.5
    STEPS = NP * SB
    LAG_SCORE, LAG_EXP, LAG_WEIGH = 1, 5, 6
    LAST = STEPS + LAG_WEIGH
    ROUNDS = 2 * SB
    KB, QB, TB, OB, VB = 0, 2, 3, 5, 6

    CTX0 = 2 * NC
    issued = {t: [] for t in range(LAST + 1)}
    for c in range(NC):
        issued[c // 2].append(("v", 0, c))
    for c in range(NC):
        issued[HALF * SB + 3 + c // 4].append(("v", 1, c))
    for s in range(SB):
        issued[STEPS - 2 + s] += [("ctx", s, n) for n in range(4)]
    RING = 2 * NC + NC

    def ring_index(kind, g, n):
        return g * NC + n if kind == "v" else CTX0 + 4 * g + n

    with ExitStack() as ctx:
        sb = lambda name, shape, dt=F32: ctx.enter_context(nc.sbuf_tensor("b_" + name, shape, dt))
        ps = ctx.enter_context(nc.psum_tensor("b_ps", [P, 8, BANK], F32))
        ctxT = sb("ctxT", [P, 2, C, S], F32R)
        craw = sb("craw", [P, 2, 4, D])
        V = sb("V", [P, NC, BANK])
        kst = sb("kst", [P, 2, 2, BANK], F32R)
        prob = sb("prob", [P, 2, 2, S])
        wk = sb("wk", [P, 2, 2, C, P], F32R)
        wv = sb("wv", [P, 2, C, BANK], F32R)
        q = sb("q", [P, 2, 2, 2, P], F32R)
        pT = sb("pT", [P, 2, 4, P])
        attnT = sb("attnT", [P, NP, P])
        bkT = sb("bkT", [P, NP])
        bvT = sb("bvT", [P, NP])
        mx = sb("mx", [P, 2, 2, SB])
        mt = sb("mt", [P, 2])
        negm = sb("negm", [P, 2, 2])
        sums = sb("sums", [P, 2, 2, SB])
        total = sb("total", [P, 2])
        rinv = sb("rinv", [P, 2, 2])
        rb = sb("rb", [P, P])
        scaled = sb("scaled", [P, P])

        per, base = {}, {}

        def sem(name, per_batch, start=1):
            s = ctx.enter_context(nc.semaphore("b_" + name))
            per[name], base[name] = per_batch, start
            return name, s

        k_psum = sem("k_psum", STEPS)
        qk_psum = sem("qk_psum", 2 * STEPS)
        t_psum = sem("t_psum", NP * ROUNDS)
        pv_done = sem("pv_done", NP * ROUNDS)
        ring_psum = sem("ring_psum", RING, NC)
        r_psum = sem("r_psum", NP)
        khi_done = sem("khi_done", 2 * STEPS)
        exp_done = sem("exp_done", 2 * STEPS)
        te_done = sem("te_done", NP * ROUNDS // 2)
        chi_done = sem("chi_done", NC, NC)
        klo_done = sem("klo_done", 2 * STEPS)
        qk_out = sem("qk_out", 2 * STEPS)
        mt_done = sem("mt_done", NP)
        negm_done = sem("negm_done", NP)
        to_done = sem("to_done", NP * ROUNDS // 2)
        ring_out = sem("ring_out", RING, NC)
        total_done = sem("total_done", NP)
        rinv_done = sem("rinv_done", NP)
        rb_done = sem("rb_done", NP)
        o_free = sem("o_free", NP)
        attn_done = sem("attn_done", NP)
        wk_in = [sem(f"wk_in{i}", 16 * NP // 2, 0) for i in range(2)]
        q_in = [sem(f"q_in{i}", 4 * 16 * NP // 2, 0) for i in range(2)]
        wv_in = sem("wv_in", 32, 0)
        craw_in = [sem(f"craw_in{i}", 16 * SB // 2, 16 * SB // 2) for i in range(2)]
        bias_in = ctx.enter_context(nc.semaphore("b_bias_in"))
        attn_stored = sem("attn_stored", 16)

        def reach(eng, s, b, k):
            name, semaphore = s
            eng.wait_ge(semaphore, b * per[name] + base[name] + max(k, 0))

        def start(eng, *sems):
            for name, semaphore in sems:
                eng.sem_inc(semaphore, 1)

        block = ctx.enter_context(nc.Block())

        @block.sync
        def _(sp):
            def load_ctx(b, s):
                sp.dma_start(craw[:, s % 2], ctx_in[b, s * BANK:(s + 1) * BANK].rearrange(
                    "(n p) d -> p n d", p=P)).then_inc(craw_in[s % 2][1], 16)

            def load_pair(b, i):
                sp.dma_start(wk[:, i % 2].bitcast(F32), wk_s[i]).then_inc(wk_in[i % 2][1], 16)
                for half in range(2):
                    for h in range(2):
                        sp.dma_start(q[half * HD:(half + 1) * HD, i % 2, h].bitcast(F32),
                                     q_s[:, i, h * HD:(h + 1) * HD, bass.ds(b * P, P)].rearrange("l d t -> d l t")
                                     ).then_inc(q_in[i % 2][1], 16)

            def load_wv(g):
                sp.dma_start(wv[:].bitcast(F32), wv_s[g]).then_inc(wv_in[1], 16)

            def batch(b, following, last):
                for i in range(2, NP):
                    reach(sp, k_psum, b, SB * (i - 1))
                    reach(sp, qk_psum, b, 2 * SB * (i - 1))
                    load_pair(b, i)
                    if i == 3:
                        reach(sp, ring_psum, b, NC)
                        load_wv(1)
                if not last:
                    reach(sp, ring_psum, b, 2 * NC)
                    load_wv(0)
                for s in range(SB):
                    if s >= 2:
                        reach(sp, ring_psum, b, CTX0 + 4 * (s - 1))
                    load_ctx(following, s)
                if not last:
                    reach(sp, qk_psum, b, 2 * STEPS)
                    for i in range(2):
                        load_pair(following, i)
                reach(sp, attn_done, b, NP)
                sp.dma_start(attn_s[b], attnT[:].rearrange("p j t -> p (j t)")).then_inc(attn_stored[1], 16)

            start(sp, attn_stored)
            sp.dma_start(bkT[:], bk.rearrange("(j p) -> p j", p=P), allow_slow_non_contiguous=True).then_inc(bias_in, 16)
            sp.dma_start(bvT[:], bv.rearrange("(j p) -> p j", p=P), allow_slow_non_contiguous=True).then_inc(bias_in, 16)
            for s in range(SB):
                if s >= 2:
                    sp.wait_ge(ring_psum[1], 4 * (s - 1))
                load_ctx(0, s)
                if s == 1:
                    load_pair(0, 0)
                    load_pair(0, 1)
                    load_wv(0)
            for b in range(NB):
                batch(b, min(b + 1, NB - 1), b == NB - 1)
            reach(sp, attn_stored, NB, 0)

        @block.tensor
        def _(pe):
            def ctx_transpose(s, n, bank):
                for c in range(C):
                    mm = nc.tensor.transpose(ps[:, bank, c * P:(c + 1) * P], craw[:, s % 2, n, c * P:(c + 1) * P], ident[:])
                mm.then_inc(ring_psum[1], 1)

            def v_chunk(c, bank):
                pairs = [(0, 0), (0, 1), (1, 0)]
                for m, (a, w) in enumerate(pairs):
                    for k in range(C):
                        mm = nc.tensor.matmul(ps[:, bank], ctxT[:, a, k, c * P:(c + 1) * P], wv[:, w, k],
                                              start=m == 0 and k == 0, stop=m == 2 and k == C - 1)
                mm.then_inc(ring_psum[1], 1)

            def project(t, first, last):
                i, s = divmod(t, SB)
                terms = [(a, w, k) for a, w in ((0, 0), (1, 0), (0, 1)) for k in range(C)]
                for m in range(first, last):
                    a, w, k = terms[m]
                    mm = nc.tensor.matmul(ps[:, KB + t % 2], wk[:, i % 2, w, k], ctxT[:, a, k, s * BANK:(s + 1) * BANK],
                                          start=m == 0, stop=m == len(terms) - 1)
                if last == len(terms):
                    mm.then_inc(k_psum[1], 1)

            def score(b, t, h):
                i = t // SB
                if t % SB == 0 and h == 0:
                    reach(pe, q_in[i % 2], b, 64 * (i // 2 + 1))
                reach(pe, klo_done, b, 2 * t + h + 1)
                reach(pe, qk_out, b, 2 * t + h)
                for l in range(2):
                    mm = nc.tensor.matmul(ps[:, QB], q[:, i % 2, h, l], kst[:, t % 2, h], start=l == 0, stop=l == 1)
                mm.then_inc(qk_psum[1], 1)

            def transpose_round(b, i, r):
                n = i * ROUNDS + r
                reach(pe, exp_done, b, 2 * (i * SB + r // 2) + 2)
                reach(pe, (te_done, to_done)[r % 2], b, n // 2)
                for m in range(4):
                    c, h = 2 * r + m // 2, m % 2
                    mm = nc.tensor.transpose(ps[:, TB + r % 2, m * P:(m + 1) * P],
                                             prob[:, i % 2, h, c * P:(c + 1) * P], ident[:])
                mm.then_inc(t_psum[1], 1)

            def weigh_round(b, i, r):
                n = i * ROUNDS + r
                if r == 0:
                    reach(pe, o_free, b, i)
                reach(pe, (te_done, to_done)[r % 2], b, n // 2 + 1)
                reach(pe, ring_out, b, i // HALF * NC + 2 * r + 2)
                for m in range(4):
                    c, h = 2 * r + m // 2, m % 2
                    col = (i % HALF * 2 + h) * HD
                    mm = nc.tensor.matmul(ps[h * HD:(h + 1) * HD, OB, 0:P], V[:, c, col:col + HD], pT[:, r % 2, m],
                                          start=c == 0, stop=c == NC - 1)
                mm.then_inc(pv_done[1], 1)

            def spread_rinv(b, i):
                reach(pe, rinv_done, b, i + 1)
                reach(pe, pv_done, b, (i + 1) * ROUNDS)
                for h in range(2):
                    mm = nc.tensor.matmul(ps[h * HD:(h + 1) * HD, OB, P:2 * P],
                                          rinv[:, i % 2, h:h + 1].broadcast_to([P, HD]), ident[:], start=True, stop=True)
                mm.then_inc(r_psum[1], 1)

            start(pe, k_psum, qk_psum, t_psum, pv_done, r_psum)
            for n in range(NC):
                if n % 4 == 0:
                    pe.wait_ge(craw_in[n // 4 % 2][1], 16 * (n // 8 + 1))
                if n >= 2:
                    pe.wait_ge(ring_out[1], n - 1)
                ctx_transpose(n // 4, n % 4, VB + n % 2)
            with pe.Fori(0, NB) as b:
                reach(pe, ring_out, b, 0)
                for t in range(LAST):
                    w = t - LAG_WEIGH
                    if w >= 0:
                        transpose_round(b, w // SB, w % SB * 2)
                        transpose_round(b, w // SB, w % SB * 2 + 1)
                    if t < STEPS:
                        if t % SB == 0:
                            reach(pe, wk_in[t // SB % 2], b, 16 * (t // SB // 2 + 1))
                        reach(pe, klo_done, b, 2 * (t - 1))
                        project(t, 0, 6)
                    if 0 <= t - LAG_SCORE < STEPS:
                        score(b, t - LAG_SCORE, 0)
                    if t < STEPS:
                        project(t, 6, 3 * C)
                    if 0 <= t - LAG_SCORE < STEPS:
                        score(b, t - LAG_SCORE, 1)
                    if w >= 0:
                        weigh_round(b, w // SB, w % SB * 2)
                        weigh_round(b, w // SB, w % SB * 2 + 1)
                        if w % SB == SB - 1:
                            spread_rinv(b, w // SB)
                    for kind, g, n in issued[t]:
                        at = ring_index(kind, g, n)
                        reach(pe, ring_out, b, at - 1)
                        if kind == "v":
                            if n == 0:
                                reach(pe, wv_in, b, 16 * (g + 1))
                            v_chunk(n, VB + at % 2)
                        else:
                            if n == 0:
                                reach(pe, craw_in[g % 2], b, 16 * (g // 2 + 1))
                            ctx_transpose(g, n, VB + at % 2)

        @block.scalar
        def _(act):
            def ctx_hi(s, n, bank):
                at = (4 * s + n) * P
                nc.scalar.copy(ctxT[:, 0, :, at:at + P], ps[:, bank].rearrange("p (c t) -> p c t", c=C)
                               ).then_inc(chi_done[1], 1)

            start(act, khi_done, exp_done, te_done)
            act.wait_ge(bias_in, 32)
            for n in range(NC):
                act.wait_ge(ring_psum[1], n + 1)
                ctx_hi(n // 4, n % 4, VB + n % 2)
            with act.Fori(0, NB) as b:
                for t in range(LAST):
                    w = t - LAG_WEIGH
                    if w >= 0:
                        n = w // SB * ROUNDS + w % SB * 2
                        reach(act, t_psum, b, n + 1)
                        reach(act, pv_done, b, n - 1)
                        nc.scalar.copy(pT[:, 0], ps[:, TB].rearrange("p (m t) -> p m t", m=4)).then_inc(te_done[1], 1)
                    e = t - LAG_EXP
                    if 0 <= e < STEPS:
                        i, s = divmod(e, SB)
                        if s == 0:
                            reach(act, negm_done, b, i + 1)
                            reach(act, rinv_done, b, i - 1)
                        for h in range(2):
                            p = prob[:, i % 2, h, s * BANK:(s + 1) * BANK]
                            nc.scalar.activation(p, p, ACT.Exp, bias=negm[:, i % 2, h:h + 1], scale=SCALE,
                                                 accum_out=sums[:, i % 2, h, s:s + 1]).then_inc(exp_done[1], 1)
                    if t < STEPS:
                        reach(act, k_psum, b, t + 1)
                        reach(act, qk_psum, b, 2 * (t - 1))
                        for h in range(2):
                            rows = slice(h * HD, (h + 1) * HD)
                            nc.scalar.activation(kst[rows, t % 2, h], ps[rows, KB + t % 2], ACT.Identity,
                                                 bias=bkT[rows, t // SB:t // SB + 1]).then_inc(khi_done[1], 1)
                    for kind, g, n in issued[t]:
                        if kind == "ctx":
                            at = ring_index(kind, g, n)
                            reach(act, ring_psum, b, at + 1)
                            ctx_hi(g, n, VB + at % 2)

        @block.vector
        def _(dve):
            def ctx_lo(s, n, bank):
                at = (4 * s + n) * P
                nc.vector.tensor_tensor(ctxT[:, 1, :, at:at + P], ps[:, bank].rearrange("p (c t) -> p c t", c=C),
                                        ctxT[:, 0, :, at:at + P].bitcast(F32), ALU.subtract).then_inc(ring_out[1], 1)

            start(dve, klo_done, qk_out, mt_done, negm_done, to_done, total_done, rinv_done, rb_done, o_free, attn_done)
            dve.wait_ge(bias_in, 32)
            for n in range(NC):
                dve.wait_ge(chi_done[1], n + 1)
                ctx_lo(n // 4, n % 4, VB + n % 2)
            with dve.Fori(0, NB) as b:
                for t in range(LAST + 1):
                    w = t - LAG_WEIGH
                    if w >= SB and w % SB == 0:
                        i = w // SB - 1
                        reach(dve, r_psum, b, i + 1)
                        if i == 0:
                            reach(dve, attn_stored, b, 0)
                        nc.vector.tensor_copy(rb[:], ps[:, OB, P:2 * P]).then_inc(rb_done[1], 1)
                        reach(dve, rb_done, b, i + 1)
                        reach(dve, attn_done, b, i)
                        nc.vector.tensor_tensor(scaled[:], ps[:, OB, 0:P], rb[:], ALU.mult).then_inc(o_free[1], 1)
                        reach(dve, o_free, b, i + 1)
                        nc.vector.tensor_scalar(attnT[:, i], scaled[:], bvT[:, i:i + 1], None, ALU.add).then_inc(attn_done[1], 1)
                    if 0 <= w < STEPS:
                        n = w // SB * ROUNDS + w % SB * 2 + 1
                        reach(dve, t_psum, b, n + 1)
                        reach(dve, pv_done, b, n - 1)
                        nc.vector.tensor_copy(pT[:, 1], ps[:, TB + 1].rearrange("p (m t) -> p m t", m=4)).then_inc(to_done[1], 1)
                    if 0 <= w < STEPS and w % SB == SB - 1:
                        i = w // SB
                        reach(dve, exp_done, b, 2 * SB * (i + 1))
                        nc.vector.tensor_reduce(total[:], sums[:, i % 2], AX.X, ALU.add).then_inc(total_done[1], 1)
                        reach(dve, total_done, b, i + 1)
                        reach(dve, r_psum, b, i - 1)
                        nc.vector.reciprocal(rinv[:, i % 2], total[:]).then_inc(rinv_done[1], 1)
                        reach(dve, rinv_done, b, i + 1)
                    e = t - LAG_SCORE
                    if 0 <= e < STEPS:
                        i, s = divmod(e, SB)
                        for h in range(2):
                            reach(dve, qk_psum, b, 2 * e + h + 1)
                            reach(dve, t_psum, b, ROUNDS * (i - 2) + 2 * (s + 1))
                            if s == 0:
                                reach(dve, negm_done, b, i - 1)
                            nc.vector.tensor_scalar(prob[:, i % 2, h, s * BANK:(s + 1) * BANK], ps[:, QB], 1.0, None,
                                                    ALU.mult, ALU.max, accum_out=mx[:, i % 2, h, s:s + 1]).then_inc(qk_out[1], 1)
                        if s == SB - 1:
                            reach(dve, qk_out, b, 2 * (e + 1))
                            nc.vector.tensor_reduce(mt[:], mx[:, i % 2], AX.X, ALU.max).then_inc(mt_done[1], 1)
                            reach(dve, mt_done, b, i + 1)
                            nc.vector.tensor_scalar(negm[:, i % 2], mt[:], -SCALE, None, ALU.mult).then_inc(negm_done[1], 1)
                            reach(dve, negm_done, b, i + 1)
                    if t < STEPS:
                        for h in range(2):
                            rows, other = slice(h * HD, (h + 1) * HD), slice((1 - h) * HD, (2 - h) * HD)
                            reach(dve, khi_done, b, 2 * t + h + 1)
                            nc.vector.scalar_tensor_tensor(kst[other, t % 2, h], ps[rows, KB + t % 2],
                                                           bkT[rows, t // SB:t // SB + 1], kst[rows, t % 2, h].bitcast(F32),
                                                           ALU.add, ALU.subtract).then_inc(klo_done[1], 1)
                    for kind, g, n in issued[t] if t < LAST else []:
                        at = ring_index(kind, g, n)
                        if kind == "v":
                            reach(dve, ring_psum, b, at + 1)
                            reach(dve, pv_done, b, 0 if g == 0 else (HALF - 1) * ROUNDS + n // 2 + 1)
                            nc.vector.tensor_copy(V[:, n], ps[:, VB + at % 2]).then_inc(ring_out[1], 1)
                        else:
                            reach(dve, chi_done, b, 4 * g + n + 1)
                            ctx_lo(g, n, VB + at % 2)


def layer_norm_steps(nc, dve, xs, xn, b_ready, tiles, sems, NB, D):
    stats, mv, var, std, rstd = tiles
    stats_done, mv_done, var_done, std_done, rstd_done, xn_done = sems
    for b in range(NB):
        b_ready(b)
        nc.vector.bn_stats(stats[:, b], xs[:, b]).then_inc(stats_done, 1)
        dve.wait_ge(stats_done, b + 1)
        nc.vector.bn_aggr(mv[:, b], stats[:, b]).then_inc(mv_done, 1)
    dve.wait_ge(mv_done, NB)
    nc.vector.tensor_scalar(var[:], mv[:, :, 1], EPS, None, ALU.add).then_inc(var_done, 1)
    dve.wait_ge(std_done, 1)
    nc.vector.reciprocal(rstd[:], std[:]).then_inc(rstd_done, 1)
    dve.wait_ge(rstd_done, 1)
    for b in range(NB):
        nc.vector.tensor_scalar(xn[:, b], xs[:, b], mv[:, b, 0:1], rstd[:, b:b + 1],
                                ALU.subtract, ALU.mult).then_inc(xn_done, 1)


def self_attention(nc, Z, ident, x, attn_s, Wo, bo, head_mask, qkv_w, qkv_b, fc_w, fc_b, x2):
    NB, C, NP, D = Z.NB, Z.C, Z.NP, Z.D
    H, HD = 16, 32
    G = P // HD
    E3 = 3 * D
    WT = E3 // P
    TOK = NB * P
    U = NB * G
    LAG = 3
    with ExitStack() as ctx:
        sb = lambda name, shape, dt=F32: ctx.enter_context(nc.sbuf_tensor("c_" + name, shape, dt))
        sem = lambda name: ctx.enter_context(nc.semaphore("c_" + name))
        ps = ctx.enter_context(nc.psum_tensor("c_ps", [P, 8, BANK], F32))
        WB, OB2, LB, PB, AB, FB = 0, 2, 2, 4, 6, 7
        attnT = sb("attnT", [P, NB, NP, P])
        wo = sb("wo", [P, NP, D])
        wraw = sb("wraw", [P, WT, D])
        fraw = sb("fraw", [P, C, D])
        wT = sb("wT", [P, C, E3])
        fT = sb("fT", [P, C, D])
        xb = sb("xb", [P, NB, D])
        bo_b = sb("bo_b", [P, D])
        fb_b = sb("fb_b", [P, D])
        bv_b = sb("bv_b", [P, H, HD])
        hm_b = sb("hm_b", [P, H])
        bqk = sb("bqk", [P, 2, G])
        hmT = sb("hmT", [P, G])
        xn = sb("xn", [P, NB, D])
        xnT = sb("xnT", [P, C, TOK])
        qkT = sb("qkT", [P, 2, G, TOK])
        v = sb("v", [P, NB, H, HD])
        vb = sb("vb", [P, 2, H, HD])
        prob = sb("prob", [P, 4, G, P])
        mx = sb("mx", [P, U, G])
        sums = sb("sums", [P, NB, G, G])
        rinv = sb("rinv", [P, NB, H])
        pT = sb("pT", [P, 2, G, P])
        ao = sb("ao", [P, 2, H, HD])
        aoT = sb("aoT", [P, 2, C, P])
        stats, mv = sb("stats", [P, NB, 6]), sb("mv", [P, NB, 2])
        var, std, rstd = sb("var", [P, NB]), sb("std", [P, NB]), sb("rstd", [P, NB])

        w_in = [sem("wq_in"), sem("wk_in"), sem("wv_in")]
        f_in, wo_in, at_in, x_in = sem("f_in"), sem("wo_in"), sem("at_in"), sem("x_in")
        small_in = sem("small_in")
        xb_done = sem("xb_done")
        wt_psum, wt_done = sem("wt_psum"), [sem("wt_act"), sem("wt_dve")]
        wo_psum, x1_done = sem("wo_psum"), sem("x1_done")
        ln = [sem(n) for n in ("stats_done", "mv_done", "var_done", "std_done", "rstd_done", "xn_done")]
        xT_psum, xT_done = sem("xT_psum"), sem("xT_done")
        qk_psum, qk_done, v_psum, vb_done, v_done = sem("qk_psum"), sem("qk_done"), sem("v_psum"), sem("vb_done"), sem("v_done")
        l_psum, mx_done, sub_done, exp_done = sem("l_psum"), sem("mx_done"), sem("sub_done"), sem("exp_done")
        sum_done, rinv_done = sem("sum_done"), sem("rinv_done")
        t_psum, t_done, pv_psum = sem("t_psum"), sem("t_done"), sem("pv_psum")
        ao_done, aoT_psum, aoT_done = sem("ao_done"), sem("aoT_psum"), sem("aoT_done")
        fc_psum, x1b_done, x2_done = sem("fc_psum"), sem("x1b_done"), sem("x2_done")
        block = ctx.enter_context(nc.Block())
        SMALL = 16 * (4 + 3 * G)
        xT_at = 2

        @block.sync
        def _(sp):
            for t in range(3):
                for r in range(G):
                    sp.dma_start(wraw[r * HD:(r + 1) * HD, t * G:(t + 1) * G],
                                 qkv_w.rearrange("(g r t d) c -> r t d g c", g=G, r=G, t=3)[r, t]).then_inc(w_in[t], 16)
            sp.dma_start(attnT[:], attn_s.rearrange("b p (j t) -> p b j t", j=NP)).then_inc(at_in, 16)
            sp.dma_start(fraw[:], fc_w.rearrange("(m p) c -> p m c", p=P)).then_inc(f_in, 16)

        @block.gpsimd
        def _(pool):
            pool.dma_start(xb[:], x.rearrange("b t d -> t b d")).then_inc(x_in, 16)
            pool.dma_start(bo_b[:], bo.rearrange("(a d) -> a d", a=1).broadcast_to([P, D])).then_inc(small_in, 16)
            pool.dma_start(fb_b[:], fc_b.rearrange("(a d) -> a d", a=1).broadcast_to([P, D])).then_inc(small_in, 16)
            pool.dma_start(hm_b[:], head_mask.rearrange("(a d) -> a d", a=1).broadcast_to([P, H])).then_inc(small_in, 16)
            bias = qkv_b.rearrange("(a h t d) -> a h t d", a=1, t=3, d=HD)
            pool.dma_start(bv_b[:], bias[:, :, 2].broadcast_to([P, H, HD])).then_inc(small_in, 16)
            for r in range(G):
                rows = slice(r * HD, (r + 1) * HD)
                for t in range(2):
                    pool.dma_start(bqk[rows, t], qkv_b.rearrange("(g r t d) -> r t d g", g=G, r=G, t=3)[r, t],
                                   allow_slow_non_contiguous=True).then_inc(small_in, 16)
                pool.dma_start(hmT[rows], head_mask.rearrange("(g r) -> r g", g=G)[r:r + 1].broadcast_to([HD, G]),
                               allow_slow_non_contiguous=True).then_inc(small_in, 16)
            pool.wait_ge(small_in, SMALL)
            pool.wait_ge(x_in, 16)
            for b in range(NB):
                nc.gpsimd.tensor_tensor(xb[:, b], xb[:, b], bo_b[:], ALU.add).then_inc(xb_done, 1)
            for b in range(NB):
                pool.wait_ge(ln[5], b + 1)
                nc.gpsimd.tensor_tensor(x2[:, b], x2[:, b], fb_b[:], ALU.add).then_inc(x1b_done, 1)

        @block.tensor
        def _(pe):
            for m in range(WT + C):
                pe.wait_ge(*(w_in[m // G], 16 * G) if m < WT else (f_in, 16))
                if m >= 2:
                    pe.wait_ge(wt_done[m % 2], m // 2)
                src = wraw[:, m] if m < WT else fraw[:, m - WT]
                for c in range(C):
                    mm = nc.tensor.transpose(ps[:, WB + m % 2, c * P:(c + 1) * P], src[:, c * P:(c + 1) * P], ident[:])
                mm.then_inc(wt_psum, 1)
            pe.wait_ge(at_in, 16)
            pe.wait_ge(wo_in, 16)
            for b in range(NB):
                for j in range(NP):
                    mm = nc.tensor.matmul(ps[:, 2 + b], attnT[:, b, j], wo[:, j], start=j == 0, stop=j == NP - 1)
                mm.then_inc(wo_psum, 1)
            for b in range(NB):
                pe.wait_ge(ln[5], b + 1)
                for c in range(C):
                    mm = nc.tensor.transpose(ps[:, xT_at + b, c * P:(c + 1) * P], xn[:, b, c * P:(c + 1) * P], ident[:])
                mm.then_inc(xT_psum, 1)
            pe.wait_ge(xT_done, NB)
            pe.wait_ge(wt_done[0], (WT + C) // 2)
            pe.wait_ge(wt_done[1], (WT + C) // 2)
            for m in range(2 * G):
                g, t = divmod(m, 2)
                if m >= 2:
                    pe.wait_ge(qk_done, m - 1)
                for c in range(C):
                    mm = nc.tensor.matmul(ps[:, WB + m % 2], wT[:, c, (t * G + g) * P:(t * G + g + 1) * P], xnT[:, c], start=c == 0, stop=c == C - 1)
                mm.then_inc(qk_psum, 1)

            def project_v(b):
                if b >= 2:
                    pe.wait_ge(vb_done, b - 1)
                for c in range(C):
                    mm = nc.tensor.matmul(ps[:, WB + b % 2], xnT[:, c, b * P:(b + 1) * P], wT[:, c, 2 * D:],
                                          start=c == 0, stop=c == C - 1)
                mm.then_inc(v_psum, 1)

            def logits(u):
                b, r = divmod(u, G)
                rows = slice(r * HD, (r + 1) * HD)
                if u == 0:
                    pe.wait_ge(qk_done, 2 * G)
                if u >= 2:
                    pe.wait_ge(sub_done, u - 1)
                for g in range(G):
                    mm = nc.tensor.matmul(ps[:, LB + u % 2, g * P:(g + 1) * P], qkT[rows, 0, g, b * P:(b + 1) * P],
                                          qkT[rows, 1, g, b * P:(b + 1) * P], start=True, stop=True)
                mm.then_inc(l_psum, 1)

            def transpose_probs(u):
                pe.wait_ge(exp_done, u + 1)
                if u >= 2:
                    pe.wait_ge(t_done, u - 1)
                for g in range(G):
                    mm = nc.tensor.transpose(ps[:, PB + u % 2, g * P:(g + 1) * P], prob[:, u % 4, g], ident[:])
                mm.then_inc(t_psum, 1)

            def weigh(u):
                b, r = divmod(u, G)
                pe.wait_ge(t_done, u + 1)
                if r == 0:
                    pe.wait_ge(v_done, b + 1)
                    if b >= 1:
                        pe.wait_ge(ao_done, b)
                for g in range(G):
                    h = G * g + r
                    mm = nc.tensor.matmul(ps[:, AB, h * HD:(h + 1) * HD], pT[:, u % 2, g], v[:, b, h], start=True, stop=True)
                mm.then_inc(pv_psum, 1)

            def transpose_out(b):
                pe.wait_ge(ao_done, b + 1)
                if b >= 1:
                    pe.wait_ge(x2_done, b)
                for c in range(C):
                    mm = nc.tensor.transpose(ps[:, FB, c * P:(c + 1) * P],
                                             ao[:, b % 2].rearrange("p h d -> p (h d)")[:, c * P:(c + 1) * P], ident[:])
                mm.then_inc(aoT_psum, 1)

            def out_product(b):
                pe.wait_ge(aoT_done, b + 1)
                for c in range(C):
                    mm = nc.tensor.matmul(ps[:, FB], aoT[:, b % 2, c], fT[:, c], start=c == 0, stop=c == C - 1)
                mm.then_inc(fc_psum, 1)

            for s in range(U + LAG + 3):
                if s < U:
                    logits(s)
                if s < NB:
                    project_v(s)
                if 0 <= s - LAG < U:
                    transpose_probs(s - LAG)
                if 0 <= s - LAG - 1 < U:
                    weigh(s - LAG - 1)
                b, at = divmod(s - LAG - 1 - G, G)
                if 0 <= b < NB and at == 0:
                    transpose_out(b)
                if 0 <= b < NB and at == 1:
                    out_product(b)

        @block.scalar
        def _(act):
            act.dma_start(wo[:], Wo.rearrange("(j p) n -> p j n", p=P)).then_inc(wo_in, 16)
            for m in range(0, WT + C, 2):
                act.wait_ge(wt_psum, m + 1)
                dst = wT[:, :, m * P:(m + 1) * P] if m < WT else fT[:, :, (m - WT) * P:(m - WT + 1) * P]
                nc.scalar.copy(dst, ps[:, WB].rearrange("p (c e) -> p c e", c=C)).then_inc(wt_done[0], 1)
            act.wait_ge(ln[2], 1)
            nc.scalar.activation(std[:], var[:], ACT.Sqrt).then_inc(ln[3], 1)
            for b in range(0, NB):
                act.wait_ge(xT_psum, b + 1)
                nc.scalar.copy(xnT[:, :, b * P:(b + 1) * P], ps[:, xT_at + b].rearrange("p (c t) -> p c t", c=C)).then_inc(xT_done, 1)
            for s in range(U + LAG + 3):
                if s < U:
                    act.wait_ge(sub_done, s + 1)
                    nc.scalar.activation(prob[:, s % 4], prob[:, s % 4], ACT.Exp, scale=HD ** -0.5).then_inc(exp_done, 1)
                u = s - LAG
                if 0 <= u < U:
                    act.wait_ge(t_psum, u + 1)
                    if u >= 2:
                        act.wait_ge(pv_psum, u - 1)
                    nc.scalar.copy(pT[:, u % 2], ps[:, PB + u % 2].rearrange("p (g q) -> p g q", g=G)).then_inc(t_done, 1)
                b, at = divmod(s - LAG - 1 - G, G)
                if 0 <= b < NB and at == 0:
                    act.wait_ge(aoT_psum, b + 1)
                    if b >= 2:
                        act.wait_ge(fc_psum, b - 1)
                    nc.scalar.copy(aoT[:, b % 2], ps[:, FB].rearrange("p (c q) -> p c q", c=C)).then_inc(aoT_done, 1)

        @block.vector
        def _(dve):
            for m in range(1, WT + C, 2):
                dve.wait_ge(wt_psum, m + 1)
                dst = wT[:, :, m * P:(m + 1) * P] if m < WT else fT[:, :, (m - WT) * P:(m - WT + 1) * P]
                nc.vector.tensor_copy(dst, ps[:, WB + 1].rearrange("p (c e) -> p c e", c=C)).then_inc(wt_done[1], 1)

            def x1_tile(b):
                dve.wait_ge(wo_psum, b + 1)
                dve.wait_ge(xb_done, b + 1)
                nc.vector.tensor_tensor(x2[:, b], ps[:, 2 + b], xb[:, b], ALU.add).then_inc(x1_done, 1)
                dve.wait_ge(x1_done, b + 1)

            layer_norm_steps(nc, dve, x2, xn, x1_tile, (stats, mv, var, std, rstd), ln, NB, D)
            dve.wait_ge(small_in, SMALL)
            for m in range(2 * G):
                g, t = divmod(m, 2)
                dve.wait_ge(qk_psum, m + 1)
                nc.vector.tensor_scalar(qkT[:, t, g], ps[:, WB + m % 2], bqk[:, t, g:g + 1], hmT[:, g:g + 1],
                                        ALU.add, ALU.mult).then_inc(qk_done, 1)

            def v_tile(b):
                dve.wait_ge(v_psum, b + 1)
                if b >= 2:
                    dve.wait_ge(v_done, b - 1)
                nc.vector.tensor_tensor(vb[:, b % 2], ps[:, WB + b % 2].rearrange("p (h d) -> p h d", h=H), bv_b[:],
                                        ALU.add).then_inc(vb_done, 1)
                dve.wait_ge(vb_done, b + 1)
                nc.vector.tensor_tensor(v[:, b], vb[:, b % 2], hm_b[:, :, None].broadcast_to([P, H, HD]),
                                        ALU.mult).then_inc(v_done, 1)

            for s in range(U + LAG + 5):
                if s < U:
                    u = s
                    lg = ps[:, LB + u % 2].rearrange("p (g k) -> p g k", g=G)
                    dve.wait_ge(l_psum, u + 1)
                    nc.vector.tensor_reduce(mx[:, u], lg, AX.X, ALU.max).then_inc(mx_done, 1)
                    dve.wait_ge(mx_done, u + 1)
                    if u >= 4:
                        dve.wait_ge(t_psum, u - 3)
                        dve.wait_ge(sum_done, u - 3)
                    nc.vector.tensor_tensor(prob[:, u % 4], lg, mx[:, u, :, None].broadcast_to([P, G, P]),
                                            ALU.subtract).then_inc(sub_done, 1)
                if s < NB:
                    v_tile(s)
                u = s - 2
                if 0 <= u < U:
                    b, r = divmod(u, G)
                    dve.wait_ge(exp_done, u + 1)
                    nc.vector.tensor_reduce(sums[:, b, :, r], prob[:, u % 4], AX.X, ALU.add).then_inc(sum_done, 1)
                    if r == G - 1:
                        dve.wait_ge(sum_done, u + 1)
                        nc.vector.reciprocal(rinv[:, b], sums[:, b].rearrange("p g r -> p (g r)")).then_inc(rinv_done, 1)
                u = s - LAG - 1
                if 0 <= u < U and u % G == G - 1:
                    b = u // G
                    dve.wait_ge(pv_psum, u + 1)
                    dve.wait_ge(rinv_done, b + 1)
                    if b >= 2:
                        dve.wait_ge(aoT_psum, b - 1)
                    nc.vector.tensor_tensor(ao[:, b % 2], ps[:, AB].rearrange("p (h d) -> p h d", h=H),
                                            rinv[:, b, :, None].broadcast_to([P, H, HD]), ALU.mult).then_inc(ao_done, 1)
                b, at = divmod(s - LAG - 1 - G, G)
                if 0 <= b < NB and at == 1:
                    dve.wait_ge(fc_psum, b + 1)
                    dve.wait_ge(x1b_done, b + 1)
                    nc.vector.tensor_tensor(x2[:, b], ps[:, FB], x2[:, b], ALU.add).then_inc(x2_done, 1)


def expert_attention(nc, Z, ident, x2, sim_matrix, gates, q_proj, k_proj, v_proj, o_proj, out):
    NB, C, D = Z.NB, Z.C, Z.D
    E, HD = q_proj.shape[0], q_proj.shape[2]
    EG = BANK // HD
    NG = E // EG
    TILES = 3 * NG
    TOK = NB * P
    SCALE = HD ** -0.5
    NORM_EPS = 1e-12
    NEG = -3e38
    RAW = 3
    WP = (0, 1)
    with ExitStack() as ctx:
        sb = lambda name, shape, dt=F32: ctx.enter_context(nc.sbuf_tensor("d_" + name, shape, dt))
        sem = lambda name: ctx.enter_context(nc.semaphore("d_" + name))
        ps = ctx.enter_context(nc.psum_tensor("d_ps", [P, 8, BANK], F32))
        raw = sb("raw", [P, RAW, C, EG, HD])
        whi = sb("whi", [P, 2, C, EG * HD], F32R)
        wlo = sb("wlo", [P, 2, C, EG * HD], F32R)
        wo = sb("wo", [P, E, D])
        xn = sb("xn", [P, NB, D])
        hT = sb("hT", [P, C, TOK])
        hhi = sb("hhi", [P, C, TOK], F32R)
        hlo = sb("hlo", [P, C, TOK], F32R)
        acc = sb("acc", [P, 3, NB, EG, HD])
        qkv = sb("qkv", [P, 3, NB, HD])
        qkT = sb("qkT", [P, 2, TOK])
        prob = sb("prob", [P, NB, P])
        probT = sb("probT", [P, NB, P])
        aoT = sb("aoT", [P, NB, P])
        cmask = sb("cmask", [P, P])
        sm = sb("sm", [P, C, E])
        sq = sb("sq", [P, C, E])
        snorm = sb("snorm", [P, 3, E])
        simn = sb("simn", [P, C, E])
        ones = sb("ones", [P, P])
        gt = sb("gt", [P, 4, E])
        junk = sb("junk", [P, D])
        n2 = sb("n2", [P, 4, NB])
        lg = sb("lg", [P, NB, E])
        rev = sb("rev", [P, E])
        g = sb("g", [P, 16, NB, E])
        g1 = sb("g1", [P, 8, NB])
        rw = sb("rw", [P, NB, E])
        mx, nmx, sums, rinv = sb("mx", [P, NB]), sb("nmx", [P, NB]), sb("sums", [P, NB]), sb("rinv", [P, NB])
        stats, mv = sb("stats", [P, NB, 6]), sb("mv", [P, NB, 2])
        var, std, rstd = sb("var", [P, NB]), sb("std", [P, NB]), sb("rstd", [P, NB])

        raw_in = [sem(f"raw_in{i}") for i in range(RAW)]
        wo_in, small_in = sem("wo_in"), sem("small_in")
        const_done, sq_done = sem("const_done"), sem("sq_done")
        ln = [sem(n) for n in ("stats_done", "mv_done", "var_done", "std_done", "rstd_done", "xn_done")]
        hT_psum, hT_done, hhi_done, hlo_done = sem("hT_psum"), sem("hT_done"), sem("hhi_done"), sem("hlo_done")
        whi_done, wlo_done = sem("whi_done"), sem("wlo_done")
        sim_psum, gate_psum, root_done, egate_done, gexp_done = sem("sim_psum"), sem("gate_psum"), sem("root_done"), sem("egate_done"), sem("gexp_done")
        chain = sem("chain")
        n2_done, gate_in_done, gsub_done, simn_done = sem("n2_done"), sem("gate_in_done"), sem("gsub_done"), sem("simn_done")
        y_psum, y_used = sem("y_psum"), sem("y_used")
        qkv_done, qkT_psum, qkT_done = sem("qkv_done"), sem("qkT_psum"), sem("qkT_done")
        s_psum, max_done, exp_done, prob_done = sem("s_psum"), sem("max_done"), sem("exp_done"), sem("prob_done")
        pT_psum, pT_done, ao_psum, ao_done = sem("pT_psum"), sem("pT_done"), sem("ao_psum"), sem("ao_done")
        o_psum, o_used, stored = sem("o_psum"), sem("o_used"), sem("stored")
        YB = 2
        block = ctx.enter_context(nc.Block())

        @block.sync
        def _(sp):
            for m in range(TILES):
                t, eg = divmod(m, NG)
                if m >= RAW:
                    sp.wait_ge(wlo_done, m - RAW + 1)
                W = (q_proj, k_proj, v_proj)[t]
                for c in range(C):
                    sp.dma_start(raw[:, m % RAW, c], W[eg * EG:(eg + 1) * EG, c * P:(c + 1) * P].rearrange("e p h -> p e h")
                                 ).then_inc(raw_in[m % RAW], 16)
            for b in range(NB):
                sp.wait_ge(o_used, E * (b + 1))
                sp.dma_start(out[b], x2[:, b]).then_inc(stored, 16)
            sp.wait_ge(stored, 16 * NB)

        @block.gpsimd
        def _(pool):
            pool.dma_start(sm[:], sim_matrix.rearrange("(c p) e -> p c e", p=P)).then_inc(small_in, 16)
            pool.dma_start(gt[:, 0], gates.rearrange("(a e) -> a e", a=1).broadcast_to([P, E])).then_inc(small_in, 16)
            pool.dma_start(wo[:], o_proj.rearrange("e h c -> h e c")).then_inc(wo_in, 16)
            nc.gpsimd.memset(ones[:], 1.0).then_inc(const_done, 1)
            nc.gpsimd.memset(cmask[:], 0.0).then_inc(const_done, 1)
            nc.gpsimd.iota(rev[:], pattern=[[-1, E]], base=E, channel_multiplier=0,
                           allow_small_or_imprecise_dtypes=True).then_inc(const_done, 1)
            pool.wait_ge(const_done, 3)
            nc.gpsimd.affine_select(out=cmask[:], in_=cmask[:], compare_op=ALU.is_ge, fill=NEG, base=0,
                                    pattern=[[-1, P]], channel_multiplier=1).then_inc(const_done, 1)

        @block.tensor
        def _(pe):
            pe.wait_ge(const_done, 4)
            pe.wait_ge(sq_done, 1)
            for c in range(C):
                mm = nc.tensor.matmul(ps[:, 6, :E], ones[:], sq[:, c], start=c == 0, stop=c == C - 1)
            mm.then_inc(sim_psum, 1)
            for b in range(NB):
                pe.wait_ge(ln[5], b + 1)
                if b >= 2:
                    pe.wait_ge(hlo_done, b - 1)
                for c in range(C):
                    mm = nc.tensor.transpose(ps[:, b % 2, c * P:(c + 1) * P], xn[:, b, c * P:(c + 1) * P], ident[:])
                mm.then_inc(hT_psum, 1)
            pe.wait_ge(hT_done, NB)
            pe.wait_ge(simn_done, 1)
            for b in range(NB):
                for c in range(C):
                    mm = nc.tensor.matmul(ps[:, 7, b * E:(b + 1) * E], hT[:, c, b * P:(b + 1) * P], simn[:, c],
                                          start=c == 0, stop=c == C - 1)
            mm.then_inc(gate_psum, 1)
            pe.wait_ge(hlo_done, NB)
            for m in range(TILES):
                pe.wait_ge(wlo_done, m + 1)
                for b in range(NB):
                    n = m * NB + b
                    if n >= 4:
                        pe.wait_ge(y_used, (n - 3) * EG)
                    terms = [(hh, ww, c) for hh, ww in ((hhi, whi), (hhi, wlo), (hlo, whi)) for c in range(C)]
                    for i, (hh, ww, c) in enumerate(terms):
                        mm = nc.tensor.matmul(ps[:, YB + n % 4], hh[:, c, b * P:(b + 1) * P], ww[:, m % 2, c],
                                              start=i == 0, stop=i == len(terms) - 1)
                    mm.then_inc(y_psum, 1)
            for t in range(2):
                pe.wait_ge(qkv_done, t + 1)
                for b in range(NB):
                    mm = nc.tensor.transpose(ps[:, t, b * P:(b + 1) * P], qkv[:, t, b], ident[:])
                mm.then_inc(qkT_psum, 1)
            pe.wait_ge(qkT_done, 2)
            for b in range(NB):
                mm = nc.tensor.matmul(ps[:, 6, b * P:(b + 1) * P], qkT[:, 0, b * P:(b + 1) * P], qkT[:, 1, b * P:(b + 1) * P],
                                      start=True, stop=True)
            mm.then_inc(s_psum, 1)
            for b in range(NB):
                pe.wait_ge(prob_done, b + 1)
                mm = nc.tensor.transpose(ps[:, 7, b * P:(b + 1) * P], prob[:, b], ident[:])
            mm.then_inc(pT_psum, 1)
            pe.wait_ge(pT_done, 1)
            for b in range(NB):
                mm = nc.tensor.matmul(ps[:, 1, b * P:(b + 1) * P], qkv[:, 2, b], probT[:, b], start=True, stop=True)
            mm.then_inc(ao_psum, 1)
            pe.wait_ge(ao_done, 1)
            pe.wait_ge(wo_in, 16)
            for b in range(NB):
                for e in range(E):
                    n = b * E + e
                    if n >= 4:
                        pe.wait_ge(o_used, n - 3)
                    nc.tensor.matmul(ps[:, YB + n % 4], aoT[:, b], wo[:, e], start=True, stop=True).then_inc(o_psum, 1)

        @block.scalar
        def _(act):
            act.wait_ge(small_in, 32)
            nc.scalar.activation(gt[:, 1], gt[:, 0], ACT.Exp, scale=-1.0).then_inc(egate_done, 1)
            act.wait_ge(ln[2], 1)
            nc.scalar.activation(std[:], var[:], ACT.Sqrt).then_inc(ln[3], 1)
            act.wait_ge(chain, 3)
            nc.scalar.activation(snorm[:, 1], snorm[:, 0], ACT.Sqrt).then_inc(root_done, 1)
            act.wait_ge(n2_done, 1)
            nc.scalar.activation(n2[:, 2], n2[:, 1], ACT.Sqrt).then_inc(root_done, 1)
            for b in range(NB):
                act.wait_ge(hT_psum, b + 1)
                src = ps[:, b % 2].rearrange("p (c t) -> p c t", c=C)
                nc.scalar.copy(hhi[:, :, b * P:(b + 1) * P], src).then_inc(hhi_done, 1)
                nc.scalar.copy(hT[:, :, b * P:(b + 1) * P], src).then_inc(hT_done, 1)

            def weight_hi(m):
                act.wait_ge(raw_in[m % RAW], 16 * C * (m // RAW + 1))
                if m >= 2:
                    act.wait_ge(y_psum, (m - 1) * NB)
                nc.scalar.copy(whi[:, m % 2], raw[:, m % RAW].rearrange("p c e h -> p c (e h)")).then_inc(whi_done, 1)

            for m in range(TILES):
                weight_hi(m)
                if m == 0:
                    act.wait_ge(gsub_done, 1)
                    nc.scalar.activation(g[:, 11], g[:, 10], ACT.Exp).then_inc(gexp_done, 1)
            for b in range(NB):
                act.wait_ge(max_done, b + 1)
                nc.scalar.activation(prob[:, b], prob[:, b], ACT.Exp, bias=nmx[:, b:b + 1], scale=SCALE,
                                     accum_out=sums[:, b:b + 1]).then_inc(exp_done, 1)
            act.wait_ge(pT_psum, 1)
            nc.scalar.copy(probT[:], ps[:, 7].rearrange("p (b t) -> p b t", b=NB)).then_inc(pT_done, 1)
            act.wait_ge(ao_psum, 1)
            nc.scalar.copy(aoT[:], ps[:, 1].rearrange("p (b t) -> p b t", b=NB)).then_inc(ao_done, 1)

        @block.vector
        def _(dve):
            V = nc.vector
            count = [0]

            def step(ins):
                count[0] += 1
                ins.then_inc(chain, 1)
                dve.wait_ge(chain, count[0])

            dve.wait_ge(small_in, 32)
            V.tensor_tensor(sq[:], sm[:], sm[:], ALU.mult).then_inc(sq_done, 1)
            dve.wait_ge(egate_done, 1)
            step(V.tensor_scalar(gt[:, 2], gt[:, 1], 1.0, None, ALU.add))
            step(V.reciprocal(gt[:, 3], gt[:, 2]))
            dve.wait_ge(sim_psum, 1)
            step(V.tensor_scalar(snorm[:, 0], ps[:, 6, :E], NORM_EPS, None, ALU.add))
            layer_norm_steps(nc, dve, x2, xn, lambda b: None, (stats, mv, var, std, rstd), ln, NB, D)
            dve.wait_ge(root_done, 1)
            step(V.reciprocal(snorm[:, 2], snorm[:, 1]))
            V.tensor_tensor(simn[:], sm[:], snorm[:, 2, None, :].broadcast_to([P, C, E]), ALU.mult).then_inc(simn_done, 1)
            dve.wait_ge(ln[5], NB)
            for b in range(NB):
                step(V.tensor_tensor_reduce(junk[:], xn[:, b], xn[:, b], 1.0, 0.0, ALU.mult, ALU.add, n2[:, 0, b:b + 1]))
            V.tensor_scalar(n2[:, 1], n2[:, 0], NORM_EPS, None, ALU.add).then_inc(n2_done, 1)
            for b in range(NB):
                dve.wait_ge(hhi_done, b + 1)
                dve.wait_ge(hT_done, b + 1)
                V.tensor_tensor(hlo[:, :, b * P:(b + 1) * P], ps[:, b % 2].rearrange("p (c t) -> p c t", c=C),
                                hhi[:, :, b * P:(b + 1) * P].bitcast(F32), ALU.subtract).then_inc(hlo_done, 1)

            def weight_lo(m):
                dve.wait_ge(whi_done, m + 1)
                V.tensor_tensor(wlo[:, m % 2], raw[:, m % RAW].rearrange("p c e h -> p c (e h)"), whi[:, m % 2].bitcast(F32),
                                ALU.subtract).then_inc(wlo_done, 1)

            weight_lo(0)
            dve.wait_ge(root_done, 2)
            step(V.reciprocal(n2[:, 3], n2[:, 2]))
            dve.wait_ge(gate_psum, 1)
            for b in range(NB):
                ins = V.scalar_tensor_tensor(lg[:, b], ps[:, 7, b * E:(b + 1) * E], n2[:, 3, b:b + 1], gt[:, 3],
                                             ALU.mult, ALU.subtract)
                step(ins)
            wide = lambda a: a[:, :, None].broadcast_to([P, NB, E])
            revb = rev[:, None, :].broadcast_to([P, NB, E])
            dve.wait_ge(const_done, 4)
            left, top = lg, []
            for k in range(2):
                o = 3 * k
                step(V.tensor_reduce(g1[:, 2 * k], left if k else left[:], AX.X, ALU.max))
                step(V.tensor_tensor(g[:, o], left if k else left[:], wide(g1[:, 2 * k]), ALU.is_equal))
                step(V.tensor_tensor(g[:, o + 1], g[:, o], revb, ALU.mult))
                step(V.tensor_reduce(g1[:, 2 * k + 1], g[:, o + 1], AX.X, ALU.max))
                step(V.tensor_tensor(g[:, o + 2], revb, wide(g1[:, 2 * k + 1]), ALU.is_equal))
                top.append(g[:, o + 2])
                if k == 0:
                    step(V.scalar_tensor_tensor(g[:, 6], g[:, 2], -16.0, lg[:], ALU.mult, ALU.add))
                    left = g[:, 6]
            step(V.tensor_tensor(g[:, 7], top[0], top[1], ALU.add))
            step(V.tensor_scalar(g[:, 8], lg[:], 0.0, None, ALU.is_gt))
            step(V.tensor_scalar(g1[:, 4], g1[:, 0], 0.0, None, ALU.is_le))
            step(V.tensor_tensor(g[:, 9], g[:, 7], wide(g1[:, 4]), ALU.mult))
            step(V.tensor_tensor(g[:, 13], g[:, 8], g[:, 9], ALU.add))
            step(V.tensor_scalar(g[:, 12], lg[:], 0.0, None, ALU.max))
            step(V.tensor_reduce(g1[:, 5], g[:, 12], AX.X, ALU.max))
            V.tensor_tensor(g[:, 10], g[:, 12], wide(g1[:, 5]), ALU.subtract).then_inc(gsub_done, 1)
            weight_lo(1)
            dve.wait_ge(gexp_done, 1)
            step(V.tensor_tensor(g[:, 14], g[:, 11], g[:, 13], ALU.mult))
            step(V.tensor_reduce(g1[:, 6], g[:, 14], AX.X, ALU.add))
            step(V.reciprocal(g1[:, 7], g1[:, 6]))
            step(V.tensor_tensor(rw[:], g[:, 14], wide(g1[:, 7]), ALU.mult))
            for m in range(TILES):
                t, eg = divmod(m, NG)
                for b in range(NB):
                    n = m * NB + b
                    dve.wait_ge(y_psum, n + 1)
                    if eg > 0:
                        dve.wait_ge(y_used, EG * (n - NB + 1))
                    for j in range(EG):
                        e = eg * EG + j
                        y, w = ps[:, YB + n % 4, j * HD:(j + 1) * HD], rw[:, b, e:e + 1]
                        if eg == 0:
                            ins = V.tensor_scalar(acc[:, t, b, j], y, w, None, ALU.mult)
                        else:
                            ins = V.scalar_tensor_tensor(acc[:, t, b, j], y, w, acc[:, t, b, j], ALU.mult, ALU.add)
                        ins.then_inc(y_used, 1)
                if m + 2 < TILES:
                    weight_lo(m + 2)
                if eg == NG - 1:
                    dve.wait_ge(y_used, EG * NB * (m + 1))
                    V.tensor_reduce(qkv[:, t], acc[:, t].rearrange("p b j h -> p b h j"), AX.X, ALU.add).then_inc(qkv_done, 1)
            for t in range(2):
                dve.wait_ge(qkT_psum, t + 1)
                V.tensor_copy(qkT[:, t], ps[:, t]).then_inc(qkT_done, 1)
            dve.wait_ge(s_psum, 1)
            step(V.tensor_tensor(prob[:], ps[:, 6].rearrange("p (b t) -> p b t", b=NB),
                                 cmask[:, None, :].broadcast_to([P, NB, P]), ALU.add))
            step(V.tensor_reduce(mx[:], prob[:], AX.X, ALU.max))
            V.tensor_scalar(nmx[:], mx[:], -SCALE, None, ALU.mult).then_inc(max_done, NB)
            for b in range(NB):
                dve.wait_ge(exp_done, b + 1)
                step(V.reciprocal(rinv[:, b:b + 1], sums[:, b:b + 1]))
                V.tensor_scalar(prob[:, b], prob[:, b], rinv[:, b:b + 1], None, ALU.mult).then_inc(prob_done, 1)
            for b in range(NB):
                for e in range(E):
                    n = b * E + e
                    dve.wait_ge(o_psum, n + 1)
                    if e > 0:
                        dve.wait_ge(o_used, n)
                    V.scalar_tensor_tensor(x2[:, b], ps[:, YB + n % 4], rw[:, b, e:e + 1], x2[:, b],
                                           ALU.mult, ALU.add).then_inc(o_used, 1)


NAMES = ['x', 'ctx_1024', 'L0_xattn_Wq', 'L0_xattn_bq', 'L0_xattn_Wk', 'L0_xattn_bk', 'L0_xattn_Wv', 'L0_xattn_bv',
         'L0_xattn_Wo', 'L0_xattn_bo', 'L0_attn_head_mask', 'L0_attn_qkv_w', 'L0_attn_qkv_b', 'L0_attn_fc_w',
         'L0_attn_fc_b', 'L0_ffn_sim_matrix', 'L0_ffn_gates', 'L0_ffn_q_proj', 'L0_ffn_k_proj', 'L0_ffn_v_proj',
         'L0_ffn_o_proj']


def perceiver_layer(nc, x, ctx_1024, Wq, bq, Wk, bk, Wv, bv, Wo, bo, head_mask, qkv_w, qkv_b, fc_w, fc_b,
                    sim_matrix, gates, q_proj, k_proj, v_proj, o_proj, out):
    Z = Shapes(x, ctx_1024)
    scratch = lambda name, shape: nc.dram_tensor(name, shape, F32, kind="Internal").ap()
    wk_s = scratch("wk_s", [Z.NP, P, 2, Z.C, P])
    wv_s = scratch("wv_s", [2, P, 2, Z.C, BANK])
    q_s = scratch("q_s", [2, Z.NP, P, Z.NB * P])
    attn_s = scratch("attn_s", [Z.NB, P, Z.NP * P])
    with ExitStack() as ctx:
        ident = ctx.enter_context(nc.sbuf_tensor("ident", [P, P], F32))
        prepare(nc, Z, ident, x, Wq, bq, Wk, Wv, wk_s, wv_s, q_s)
        cross_attention(nc, Z, ident, ctx_1024, bk, bv, wk_s, wv_s, q_s, attn_s)
        x2 = ctx.enter_context(nc.sbuf_tensor("x2", [P, Z.NB, Z.D], F32))
        self_attention(nc, Z, ident, x, attn_s, Wo, bo, head_mask, qkv_w, qkv_b, fc_w, fc_b, x2)
        expert_attention(nc, Z, ident, x2, sim_matrix, gates, q_proj, k_proj, v_proj, o_proj, out)


def kernel(**inputs):
    import numpy as np
    import concourse.bacc as bacc
    from concourse.bass_utils import run_bass_kernel_spmd

    nc = bacc.Bacc("TRN2", target_bir_lowering=False, num_devices=1)
    arrays, args = {}, []
    for name in NAMES:
        a = np.ascontiguousarray(inputs[name])
        arrays[f"in_{name}"] = a
        args.append(nc.dram_tensor(f"in_{name}", a.shape, mybir.dt.from_np(a.dtype), kind="ExternalInput").ap())
    out = nc.dram_tensor("out", inputs["x"].shape, F32, kind="ExternalOutput").ap()
    perceiver_layer(nc, *args, out)
    r = run_bass_kernel_spmd(nc, [arrays], core_ids=[0])
    return r.results[0]["out"]
```

```python
from contextlib import ExitStack

import concourse.bass as bass
from concourse import mybir

F32 = mybir.dt.float32
F32R = mybir.dt.float32r
ALU = mybir.AluOpType
ACT = mybir.ActivationFunctionType
AX = mybir.AxisListType

P = 128
BANK = 512
EPS = 1e-5


class Shapes:

    def __init__(self, x, ctx, gates):
        self.NB, self.TQ, self.D = x.shape
        self.S = ctx.shape[1]
        self.C = self.D // P
        self.E = gates.shape[0]
        self.H, self.HD = 16, 64
        self.HW = self.H * self.HD
        self.NP = self.H // 2
        self.SB = self.S // BANK
        self.NC = self.S // P
        self.HALF = self.NP // 2


LN_STEPS = ("stats_done", "mv_done", "var_done", "std_done", "rstd_done", "xn_done")


def make_identity(nc, pool, ident, sem):
    nc.gpsimd.memset(ident[:], 0.0).then_inc(sem, 1)
    pool.wait_ge(sem, 1)
    nc.gpsimd.affine_select(out=ident[:], in_=ident[:], compare_op=ALU.not_equal, fill=1.0, base=0,
                            pattern=[[-1, P]], channel_multiplier=1).then_inc(sem, 1)


def alias(nc, name, shape, at):
    return nc.alloc_sbuf_tensor_at(name, shape, F32, offset=at)


def reach(eng, s, b, k):
    eng.wait_ge(s.sem, b * s.per + s.base + (k if s.base + k > 0 else 0))


class Count:

    def __init__(self, ctx, nc, name, per, base=1):
        self.sem, self.per, self.base = ctx.enter_context(nc.semaphore(name)), per, base


class Shared:

    def __init__(self, ctx, nc, Z):
        sb = lambda name, shape, dt=F32: ctx.enter_context(nc.sbuf_tensor(name, shape, dt))
        self.ident = sb("ident", [P, P])
        self.x2 = sb("x2", [P, Z.NB * Z.D])
        self.wv_at = nc.sbuf_base
        self.wv = sb("wv", [P, 2, Z.C, BANK], F32R)
        self.wk_at = nc.sbuf_base
        self.wk = sb("wk", [P, 2, 2, Z.C, P], F32R)
        self.stage = sb("stage", [P, STAGE_SLOTS, Z.D])
        self.w_rows = alias(nc, "w_rows", [P, 4 * Z.C, Z.D], self.wv_at)
        self.w_tiles = alias(nc, "w_tiles", [P, 4, Z.C, BANK], self.wv_at)
        assert nc.sbuf_base == self.wv_at + 4 * 4 * Z.C * Z.D
        self.rows_in = [ctx.enter_context(nc.semaphore(f"rows_in{i}")) for i in range(3)]
        self.tile_in = [ctx.enter_context(nc.semaphore(f"tile_in{i}")) for i in range(4)]
        self.gate = sb("gate", [P, 4, Z.E])
        self.stats, self.mv = sb("stats", [P, Z.NB, 6]), sb("mv", [P, Z.NB, 2])
        self.ln = [ctx.enter_context(nc.semaphore("e_" + n)) for n in LN_STEPS]


STAGE_SLOTS = 4


class Stage:

    def __init__(self, ctx, nc, Z):
        wv = lambda g: [("wv", g, c) for c in range(Z.C)]
        self.items = ([("wk", 2), ("wk", 3)] + wv(1) + [("wk", i) for i in range(4, Z.NP)] + wv(0)
                      + [("ctx", n) for n in range(Z.NC // 2)] + [("wk", 0), ("wk", 1)])
        self.pos, self.owner, self.count, loads = {}, [], {}, [0] * STAGE_SLOTS
        for item in self.items:
            self.pos[item] = len(self.owner)
            self.owner += [item] * (2 if item[0] == "ctx" else 1)
            slot = self.slot(item)
            loads[slot] += 16
            self.count[item] = loads[slot]
        assert len(self.owner) % STAGE_SLOTS == 0
        self.filled = [Count(ctx, nc, f"stage_in{i}", loads[i], 0) for i in range(STAGE_SLOTS)]
        splits = [item for item in self.items if item[0] != "ctx"]
        self.split_at = {item: n for n, item in enumerate(splits)}
        self.SPLITS = len(splits)
        self.hi_done = Count(ctx, nc, "split_hi", self.SPLITS)
        self.lo_done = Count(ctx, nc, "split_lo", self.SPLITS)

    def slot(self, item):
        return self.pos[item] % STAGE_SLOTS

    def split_count(self, item):
        early = item in (("wk", 0), ("wk", 1)) or item[:2] == ("wv", 0)
        return self.split_at[item] + 1 - (self.SPLITS if early else 0)


class CrossShared:
    def __init__(self, ctx, nc, Z):
        sb = lambda name, shape, dt=F32: ctx.enter_context(nc.sbuf_tensor(name, shape, dt))
        count = lambda name, per, base: Count(ctx, nc, name, per, base)
        self.ctxT = sb("ctxT", [P, 2, Z.C, Z.S], F32R)
        self.q = sb("q", [P, 2, 2, 2, P], F32R)
        self.wo = sb("wo", [P, Z.NP, Z.D])
        self.RING = 3 * Z.NC + 4
        self.ring_psum = count("ring_psum", self.RING, Z.NC)
        self.ring_out = count("ring_out", self.RING, Z.NC)
        self.chi_done = count("chi_done", Z.NC, Z.NC)
        self.q_in = [count(f"q_in{i}", 4 * 16 * Z.NP // 2, 0) for i in range(2)]
        self.stage = Stage(ctx, nc, Z)
        self.wo_in = count("wo_in", 0, 0)


VB = 6


def load_ctx(sp, Z, M, ctx_in, b, n, sem):
    sp.dma_start(M.stage[:, ctx_slot(n):ctx_slot(n) + 2], ctx_in[b, n * 2 * P:(n + 1) * 2 * P].rearrange("(n p) d -> p n d", p=P)
                 ).then_inc(sem, 16)


def ctx_slot(n):
    return 2 * ((n + 1) % 2)


def load_q(sp, Z, X, q_s, b, i):
    for half in range(2):
        for h in range(2):
            sp.dma_start(X.q[half * Z.HD:(half + 1) * Z.HD, i % 2, h].bitcast(F32),
                         q_s[:, i, h * Z.HD:(h + 1) * Z.HD, b * P:(b + 1) * P].rearrange("l d t -> d l t")
                         ).then_inc(X.q_in[i % 2].sem, 16)


def split_parts(Z, M, item, raw):
    if item[0] == "wk":
        return raw.rearrange("p (k n) -> p k n", k=Z.C), M.wk[:, item[1] % 2, 0], M.wk[:, item[1] % 2, 1]
    return raw, M.wv[:, 0, item[2]], M.wv[:, 1, item[2]]


def ctx_transpose(nc, Z, M, X, ps, s, n, bank):
    for c in range(Z.C):
        mm = nc.tensor.transpose(ps[:, bank, c * P:(c + 1) * P], M.stage[:, ctx_slot(2 * s + n // 2) + n % 2, c * P:(c + 1) * P], M.ident[:])
    mm.then_inc(X.ring_psum.sem, 1)


def ctx_hi(nc, Z, X, ps, s, n, bank):
    at = (4 * s + n) * P
    nc.scalar.copy(X.ctxT[:, 0, :, at:at + P], ps[:, bank].rearrange("p (c t) -> p c t", c=Z.C)).then_inc(X.chi_done.sem, 1)


def ctx_lo(nc, Z, X, ps, s, n, bank):
    at = (4 * s + n) * P
    nc.vector.tensor_tensor(X.ctxT[:, 1, :, at:at + P], ps[:, bank].rearrange("p (c t) -> p c t", c=Z.C),
                            X.ctxT[:, 0, :, at:at + P].bitcast(F32), ALU.subtract).then_inc(X.ring_out.sem, 1)


def prepare(nc, Z, M, X, x, ctx_in, Wq, bq, Wk, Wv, bo, q_s):
    NB, C, NP, D, HW, NC = Z.NB, Z.C, Z.NP, Z.D, Z.HW, Z.NC
    TOK = NB * P
    SPLITS = [("wk", 0), ("wk", 1)] + [("wv", 0, c) for c in range(C)]
    XB, QB, CB = 0, 2, 4
    QBUFS = 4
    with ExitStack() as ctx:
        sb = lambda name, shape, dt=F32: ctx.enter_context(nc.sbuf_tensor("a_" + name, shape, dt))
        sem = lambda name: ctx.enter_context(nc.semaphore("a_" + name))
        ps = ctx.enter_context(nc.psum_tensor("a_ps", [P, 8, BANK], F32))
        xs = M.x2[:].rearrange("p (b d) -> p b d", b=NB)
        xn = sb("xn", [P, NB, D])
        xnT = sb("xnT", [P, C, TOK])
        wq = sb("wq", [P, C, HW])
        w = sb("w", [P, len(SPLITS), BANK])
        qhi = sb("qhi", [P, QBUFS, TOK], F32R)
        qlo = sb("qlo", [P, QBUFS, TOK], F32R)
        bqT = sb("bqT", [P, NP])
        bo_b = sb("bo_b", [P, D])
        stats, mv = sb("stats", [P, NB, 6]), sb("mv", [P, NB, 2])
        var, std, rstd = sb("var", [P, NB]), sb("std", [P, NB]), sb("rstd", [P, NB])

        id_ready = sem("id_ready")
        x_in, bq_in, bo_in = sem("x_in"), sem("bq_in"), sem("bo_in")
        wq_in = [sem(f"wq_in{c}") for c in range(C)]
        wk_in, wv_in, ctx_sem = sem("wk_in"), sem("wv_in"), [sem("ctx_in0"), sem("ctx_in1")]
        ln = [sem(n) for n in ("stats_done", "mv_done", "var_done", "std_done", "rstd_done", "xn_done")]
        xT_psum, xT_done = sem("xT_psum"), sem("xT_done")
        q_psum, qhi_done, qlo_done = sem("q_psum"), sem("qhi_done"), sem("qlo_done")
        whi_done, wlo_done = sem("whi_done"), sem("wlo_done")
        q_stored = [sem(f"q_stored{i}") for i in range(QBUFS)]
        block = ctx.enter_context(nc.Block())

        TURNS = [([], [], [0]), ([0], [0, 1], [1]), ([1], [2, 3], [2]), ([2], [4, 5], [3]), ([3], [6, 7], [4]),
                 ([4], [8, 9], [5]), ([5], [10, 11, 12], [6]), ([], [13, 14, 15], [7])]

        @block.sync
        def _(sp):
            sp.dma_start(xs, x.rearrange("b t d -> t b d")).then_inc(x_in, 16)
            for c in range(C):
                sp.dma_start(wq[:, c], Wq[c * P:(c + 1) * P]).then_inc(wq_in[c], 16)
            load_ctx(sp, Z, M, ctx_in, 0, 0, ctx_sem[0])
            for j in range(2):
                sp.dma_start(w[:, j].rearrange("p (k n) -> p k n", k=C),
                             Wk[:, j * P:(j + 1) * P].rearrange("(k p) n -> p k n", p=P)).then_inc(wk_in, 16)
            load_ctx(sp, Z, M, ctx_in, 0, 1, ctx_sem[1])
            sp.dma_start(w[:, 2:], Wv[:, :BANK].rearrange("(c p) n -> p c n", p=P)).then_inc(wv_in, 16)
            for n in range(2, NC // 2):
                sp.wait_ge(X.ring_psum.sem, 2 * (n - 1))
                load_ctx(sp, Z, M, ctx_in, 0, n, ctx_sem[n % 2])
            for i in range(2):
                sp.wait_ge(q_stored[i], 32)
                load_q(sp, Z, X, q_s, 0, i)
            for s in q_stored:
                sp.wait_ge(s, 32 * NP // QBUFS)

        @block.gpsimd
        def _(pool):
            pool.dma_start(bqT[:], bq.rearrange("(j p) -> p j", p=P), allow_slow_non_contiguous=True).then_inc(bq_in, 16)
            pool.dma_start(bo_b[:], bo.rearrange("(a d) -> a d", a=1).broadcast_to([P, D])).then_inc(bo_in, 16)
            make_identity(nc, pool, M.ident, id_ready)

            pool.wait_ge(bo_in, 16)
            for b in range(NB):
                pool.wait_ge(ln[5], b + 1)
                nc.gpsimd.tensor_tensor(xs[:, b], xs[:, b], bo_b[:], ALU.add)
            for j in range(NP):
                pool.wait_ge(qlo_done, j + 1)
                for hl, src in enumerate((qhi, qlo)):
                    pool.dma_start(q_s[hl, j], src[:, j % QBUFS].bitcast(F32)).then_inc(q_stored[j % QBUFS], 16)

        @block.tensor
        def _(pe):
            pe.wait_ge(id_ready, 2)
            for b in range(NB):
                pe.wait_ge(ln[5], b + 1)
                if b >= 2:
                    pe.wait_ge(xT_done, b - 1)
                for c in range(C):
                    mm = nc.tensor.transpose(ps[:, XB + b % 2, c * P:(c + 1) * P], xn[:, b, c * P:(c + 1) * P], M.ident[:])
                mm.then_inc(xT_psum, 1)
            for _, chunks, pairs in TURNS:
                for n in chunks:
                    if n % 2 == 0:
                        pe.wait_ge(ctx_sem[n // 2 % 2], 16 * (n // 4 + 1))
                    if n >= 4:
                        pe.wait_ge(X.ring_out.sem, n - 3)
                    ctx_transpose(nc, Z, M, X, ps, n // 4, n % 4, CB + n % 4)
                for j in pairs:
                    if j == 0:
                        pe.wait_ge(xT_done, NB)
                        for c in range(C):
                            pe.wait_ge(wq_in[c], 16)
                    if j >= 2:
                        pe.wait_ge(qlo_done, j - 1)
                    for c in range(C):
                        mm = nc.tensor.matmul(ps[:, QB + j % 2, :TOK], wq[:, c, j * P:(j + 1) * P], xnT[:, c, :],
                                              start=c == 0, stop=c == C - 1)
                    mm.then_inc(q_psum, 1)

        @block.scalar
        def _(act):
            act.wait_ge(ln[2], 1)
            nc.scalar.activation(std[:], var[:], ACT.Sqrt).then_inc(ln[3], 1)
            act.wait_ge(bq_in, 16)
            for units, chunks, pairs in TURNS:
                for n in chunks:
                    act.wait_ge(X.ring_psum.sem, n + 1)
                    ctx_hi(nc, Z, X, ps, n // 4, n % 4, CB + n % 4)
                for j in pairs:
                    act.wait_ge(q_psum, j + 1)
                    if j >= QBUFS:
                        act.wait_ge(q_stored[j % QBUFS], 32 * (j // QBUFS))
                    nc.scalar.activation(qhi[:, j % QBUFS], ps[:, QB + j % 2, :TOK], ACT.Identity,
                                         bias=bqT[:, j:j + 1]).then_inc(qhi_done, 1)
                for m in units:
                    act.wait_ge(*(wk_in, 32) if SPLITS[m][0] == "wk" else (wv_in, 16))
                    raw, hi, _ = split_parts(Z, M, SPLITS[m], w[:, m])
                    nc.scalar.copy(hi, raw).then_inc(whi_done, 1)

        @block.vector
        def _(dve):
            layer_norm_stats(nc, dve, xs, lambda b: dve.wait_ge(x_in, 16), stats, mv, ln, NB)
            layer_norm_apply(nc, dve, xs, xn, (mv, var, std, rstd), ln, NB)
            for b in range(NB):
                dve.wait_ge(xT_psum, b + 1)
                nc.vector.tensor_copy(xnT[:, :, b * P:(b + 1) * P],
                                      ps[:, XB + b % 2].rearrange("p (c t) -> p c t", c=C)).then_inc(xT_done, 1)
            dve.wait_ge(bq_in, 16)
            for units, chunks, pairs in TURNS:
                for n in chunks:
                    dve.wait_ge(X.chi_done.sem, n + 1)
                    ctx_lo(nc, Z, X, ps, n // 4, n % 4, CB + n % 4)
                for j in pairs:
                    dve.wait_ge(qhi_done, j + 1)
                    nc.vector.scalar_tensor_tensor(qlo[:, j % QBUFS], ps[:, QB + j % 2, :TOK], bqT[:, j:j + 1],
                                                   qhi[:, j % QBUFS].bitcast(F32), ALU.add, ALU.subtract).then_inc(qlo_done, 1)
                for m in units:
                    dve.wait_ge(whi_done, m + 1)
                    raw, hi, lo = split_parts(Z, M, SPLITS[m], w[:, m])
                    nc.vector.tensor_tensor(lo, raw, hi.bitcast(F32), ALU.subtract).then_inc(wlo_done, 1)


def layer_norm_stats(nc, dve, xs, ready, stats, mv, sems, NB):
    stats_done, mv_done = sems[:2]
    for b in range(NB):
        ready(b)
        nc.vector.bn_stats(stats[:, b], xs[:, b]).then_inc(stats_done, 1)
    for b in range(NB):
        dve.wait_ge(stats_done, b + 1)
        nc.vector.bn_aggr(mv[:, b], stats[:, b]).then_inc(mv_done, 1)


def layer_norm_apply(nc, dve, xs, xn, tiles, sems, NB):
    mv, var, std, rstd = tiles
    _, mv_done, var_done, std_done, rstd_done, xn_done = sems
    dve.wait_ge(mv_done, NB)
    nc.vector.tensor_scalar(var[:], mv[:, :, 1], EPS, None, ALU.add).then_inc(var_done, 1)
    dve.wait_ge(std_done, 1)
    nc.vector.reciprocal(rstd[:], std[:]).then_inc(rstd_done, 1)
    dve.wait_ge(rstd_done, 1)
    for b in range(NB):
        nc.vector.tensor_scalar(xn[:, b], xs[:, b], mv[:, b, 0:1], rstd[:, b:b + 1],
                                ALU.subtract, ALU.mult).then_inc(xn_done, 1)


def cross_attention(nc, Z, M, X, ctx_in, Wk, bk, Wv, bv, Wo, q_s, late_loads):
    NB, C, NP, S, SB, NC, D, HD, HALF = Z.NB, Z.C, Z.NP, Z.S, Z.SB, Z.NC, Z.D, Z.HD, Z.HALF
    SCALE = HD ** -0.5
    STEPS = NP * SB
    LAG_SCORE, LAG_EXP, LAG_WEIGH = 1, 5, 6
    LAST = STEPS + LAG_WEIGH
    ROUNDS = 2 * SB
    KB, QB, TB, OB = 0, 2, 3, 5

    issued = {t: [] for t in range(LAST + 1)}
    for c in range(NC):
        issued[c // 2].append(("v", 0, c))
        issued[HALF * SB + 3 + c // 4].append(("v", 1, c))
    chunks = iter([("ctx", s, n) for s in range(SB) for n in range(4)])
    for t, n in zip(range(STEPS - 3, LAST + 1), (3, 3, 3, 3, 2, 2)):
        issued[t] += [next(chunks) for _ in range(n)]
    issued[STEPS - 1].append(("wo", 0, 4))
    issued[STEPS + 1].append(("wo", 4, 6))
    issued[STEPS + 4].append(("wo", 6, 7))
    issued[LAST].append(("wo", 7, 8))
    ring_at = {item: at for at, item in enumerate(x for t in range(LAST + 1) for x in issued[t])}
    RING = X.RING
    assert len(ring_at) == RING and RING % 2 == 0
    ctx_index = lambda s, n: ring_at[("ctx", s, n)]
    T = X.stage
    splits = {t: [] for t in range(LAST + 1)}
    for i in range(2, NP):
        splits[SB * (i - 1) + 1].append(("wk", i))
    for c in range(C):
        splits[2 * SB + 1 + c].append(("wv", 1, c))
        splits[STEPS - 6 + c // 2].append(("wv", 0, c))
    splits[LAST - 2].append(("wk", 0))
    splits[LAST - 1].append(("wk", 1))
    assert [x for t in splits for x in splits[t]] == list(T.split_at)

    with ExitStack() as ctx:
        sb = lambda name, shape, dt=F32: ctx.enter_context(nc.sbuf_tensor("b_" + name, shape, dt))
        ps = ctx.enter_context(nc.psum_tensor("b_ps", [P, 8, BANK], F32))
        ctxT, wk, wv, q, wo, ident = X.ctxT, M.wk, M.wv, X.q, X.wo, M.ident
        V = sb("V", [P, NC, BANK])
        kst = sb("kst", [P, 2, 2, BANK], F32R)
        prob = sb("prob", [P, 2, 2, S])
        pT = sb("pT", [P, 2, 4, P])
        attnT = sb("attnT", [P, NP, P])
        bkT = sb("bkT", [P, NP])
        bvT = sb("bvT", [P, NP])
        mx = sb("mx", [P, 2, 2, SB])
        mt = sb("mt", [P, 2])
        negm = sb("negm", [P, 2, 2])
        sums = sb("sums", [P, 2, 2, SB])
        total = sb("total", [P, 2])
        rinv = sb("rinv", [P, 2, 2])
        rb = sb("rb", [P, P])
        scaled = sb("scaled", [P, P])

        sem = lambda name, per: Count(ctx, nc, "b_" + name, per)

        k_psum = sem("k_psum", STEPS)
        qk_psum = sem("qk_psum", 2 * STEPS)
        t_psum = sem("t_psum", NP * ROUNDS)
        pv_done = sem("pv_done", NP * ROUNDS)
        r_psum = sem("r_psum", NP)
        khi_done = sem("khi_done", 2 * STEPS)
        exp_done = sem("exp_done", 2 * STEPS)
        te_done = sem("te_done", NP * ROUNDS // 2)
        klo_done = sem("klo_done", 2 * STEPS)
        qk_out = sem("qk_out", 2 * STEPS)
        mt_done = sem("mt_done", NP)
        negm_done = sem("negm_done", NP)
        to_done = sem("to_done", NP * ROUNDS // 2)
        total_done = sem("total_done", NP)
        rinv_done = sem("rinv_done", NP)
        rb_done = sem("rb_done", NP)
        o_free = sem("o_free", NP)
        attn_done = sem("attn_done", NP)
        bias_in = ctx.enter_context(nc.semaphore("b_bias_in"))

        ring_psum, ring_out, chi_done = X.ring_psum, X.ring_out, X.chi_done

        def start(eng, *counts):
            for s in counts:
                eng.sem_inc(s.sem, 1)

        block = ctx.enter_context(nc.Block())

        @block.sync
        def _(sp):
            sp.dma_start(wo[:], Wo.rearrange("(j p) n -> p j n", p=P)).then_inc(X.wo_in.sem, 16)
            sp.dma_start(bkT[:], bk.rearrange("(j p) -> p j", p=P), allow_slow_non_contiguous=True).then_inc(bias_in, 16)
            sp.dma_start(bvT[:], bv.rearrange("(j p) -> p j", p=P), allow_slow_non_contiguous=True).then_inc(bias_in, 16)
            def free_slots(b, item):
                at, width = T.pos[item], 2 if item[0] == "ctx" else 1
                for p in range(at - STAGE_SLOTS, at - STAGE_SLOTS + width):
                    old, ago = T.owner[p], 1 if p < 0 else 0
                    if old[0] == "ctx":
                        reach(sp, ring_psum, b, ctx_index(old[1] // 2, old[1] % 2 * 2 + 1) + 1 - ago * RING)
                    else:
                        reach(sp, T.lo_done, b, T.split_at[old] + 1 - ago * T.SPLITS)

            def load_stage(b, item):
                free_slots(b, item)
                slot = T.slot(item)
                if item[0] == "ctx":
                    load_ctx(sp, Z, M, ctx_in, min(b + 1, NB - 1), item[1], T.filled[slot].sem)
                elif item[0] == "wk":
                    src = Wk[:, item[1] * P:(item[1] + 1) * P].rearrange("(k p) n -> p k n", p=P)
                    sp.dma_start(M.stage[:, slot].rearrange("p (k n) -> p k n", k=C), src).then_inc(T.filled[slot].sem, 16)
                else:
                    _, g, c = item
                    sp.dma_start(M.stage[:, slot], Wv[c * P:(c + 1) * P, g * BANK:(g + 1) * BANK]
                                 ).then_inc(T.filled[slot].sem, 16)

            q_after = {("wv", 1, 1): 2, ("wv", 1, 2): 3, ("wk", 5): 4, ("wk", 7): 5, ("wv", 0, 1): 6, ("wv", 0, 2): 7,
                       ("ctx", 1): 8, ("ctx", 5): 9}
            for b in range(NB):
                last = b == NB - 1
                for item in T.items:
                    load_stage(b, item)
                    i = q_after.get(item)
                    if i is not None and not (last and i >= NP):
                        reach(sp, qk_psum, b, 2 * SB * (i - 1))
                        load_q(sp, Z, X, q_s, b + i // NP, i % NP)
                    if item == ("ctx", 1) and last:
                        reach(sp, T.lo_done, b, T.split_at["wv", 0, C - 1] + 1)
                        late_loads(sp, 0)
            reach(sp, T.lo_done, NB - 1, T.SPLITS)
            reach(sp, ring_psum, NB - 1, ctx_index(SB - 1, 3) + 1)
            late_loads(sp, 1)
            late_loads(sp, 2)

        @block.tensor
        def _(pe):
            def v_chunk(c, bank):
                pairs = [(0, 0), (0, 1), (1, 0)]
                for m, (a, w) in enumerate(pairs):
                    for k in range(C):
                        mm = nc.tensor.matmul(ps[:, bank], ctxT[:, a, k, c * P:(c + 1) * P], wv[:, w, k],
                                              start=m == 0 and k == 0, stop=m == 2 and k == C - 1)
                mm.then_inc(ring_psum.sem, 1)

            def project(t, first, last):
                i, s = divmod(t, SB)
                terms = [(a, w, k) for a, w in ((0, 0), (1, 0), (0, 1)) for k in range(C)]
                for m in range(first, last):
                    a, w, k = terms[m]
                    mm = nc.tensor.matmul(ps[:, KB + t % 2], wk[:, i % 2, w, k], ctxT[:, a, k, s * BANK:(s + 1) * BANK],
                                          start=m == 0, stop=m == len(terms) - 1)
                if last == len(terms):
                    mm.then_inc(k_psum.sem, 1)

            def score(b, t, h):
                i = t // SB
                if t % SB == 0 and h == 0:
                    reach(pe, X.q_in[i % 2], b, 64 * (i // 2 + 1))
                reach(pe, klo_done, b, 2 * t + h + 1)
                reach(pe, qk_out, b, 2 * t + h)
                for l in range(2):
                    mm = nc.tensor.matmul(ps[:, QB], q[:, i % 2, h, l], kst[:, t % 2, h], start=l == 0, stop=l == 1)
                mm.then_inc(qk_psum.sem, 1)

            def transpose_round(b, i, r):
                n = i * ROUNDS + r
                reach(pe, exp_done, b, 2 * (i * SB + r // 2) + 2)
                reach(pe, (te_done, to_done)[r % 2], b, n // 2)
                for m in range(4):
                    c, h = 2 * r + m // 2, m % 2
                    mm = nc.tensor.transpose(ps[:, TB + r % 2, m * P:(m + 1) * P],
                                             prob[:, i % 2, h, c * P:(c + 1) * P], ident[:])
                mm.then_inc(t_psum.sem, 1)

            def weigh_round(b, i, r):
                n = i * ROUNDS + r
                if r == 0:
                    reach(pe, o_free, b, i)
                reach(pe, (te_done, to_done)[r % 2], b, n // 2 + 1)
                reach(pe, ring_out, b, i // HALF * NC + 2 * r + 2)
                for m in range(4):
                    c, h = 2 * r + m // 2, m % 2
                    col = (i % HALF * 2 + h) * HD
                    mm = nc.tensor.matmul(ps[h * HD:(h + 1) * HD, OB, 0:P], V[:, c, col:col + HD], pT[:, r % 2, m],
                                          start=c == 0, stop=c == NC - 1)
                mm.then_inc(pv_done.sem, 1)

            def spread_rinv(b, i):
                reach(pe, rinv_done, b, i + 1)
                reach(pe, pv_done, b, (i + 1) * ROUNDS)
                for h in range(2):
                    mm = nc.tensor.matmul(ps[h * HD:(h + 1) * HD, OB, P:2 * P],
                                          rinv[:, i % 2, h:h + 1].broadcast_to([P, HD]), ident[:], start=True, stop=True)
                mm.then_inc(r_psum.sem, 1)

            def ring_item(b, item):
                (kind, g, n), at = item, ring_at[item]
                bank = VB + at % 2
                reach(pe, ring_out, b, at - 1)
                if kind == "v":
                    if n == 0:
                        reach(pe, T.lo_done, b, T.split_count(("wv", g, C - 1)))
                    if g == 0 and n % 4 == 0:
                        reach(pe, ring_out, b, ctx_index(n // 4, 3) + 1 - RING)
                    v_chunk(n, bank)
                elif kind == "ctx":
                    if n % 2 == 0:
                        half = ("ctx", 2 * g + n // 2)
                        reach(pe, T.filled[T.slot(half)], b, T.count[half])
                    ctx_transpose(nc, Z, M, X, ps, g, n, bank)
                else:
                    pe.wait_ge(X.wo_in.sem, 16)
                    reach(pe, attn_done, b, n)
                    for i in range(g, n):
                        mm = nc.tensor.matmul(ps[:, bank], attnT[:, i], wo[:, i], start=i == g, stop=i == n - 1)
                    mm.then_inc(ring_psum.sem, 1)

            start(pe, k_psum, qk_psum, t_psum, pv_done, r_psum)
            with pe.Fori(0, NB) as b:
                for t in range(LAST + 1):
                    w = t - LAG_WEIGH
                    tail = t > STEPS
                    if 0 <= w < STEPS and not tail:
                        transpose_round(b, w // SB, w % SB * 2)
                        transpose_round(b, w // SB, w % SB * 2 + 1)
                    if t < STEPS:
                        if t < SB:
                            reach(pe, ring_out, b, ctx_index(t, 3) + 1 - RING)
                        if t % SB == 0:
                            reach(pe, T.lo_done, b, T.split_count(("wk", t // SB)))
                        reach(pe, klo_done, b, 2 * (t - 1))
                        project(t, 0, 6)
                    if 0 <= t - LAG_SCORE < STEPS:
                        score(b, t - LAG_SCORE, 0)
                    if t < STEPS:
                        project(t, 6, 3 * C)
                    if 0 <= t - LAG_SCORE < STEPS:
                        score(b, t - LAG_SCORE, 1)
                    items = list(issued[t])
                    if 0 <= w < STEPS:
                        for half in range(2):
                            weigh_round(b, w // SB, w % SB * 2 + half)
                            if t >= STEPS:
                                if w + 1 < STEPS:
                                    transpose_round(b, (w + 1) // SB, (w + 1) % SB * 2 + half)
                                for item in items[:(len(items) + 1) // 2]:
                                    ring_item(b, item)
                                items = items[(len(items) + 1) // 2:]
                        if w % SB == SB - 1:
                            spread_rinv(b, w // SB)
                    for item in items:
                        ring_item(b, item)

        @block.scalar
        def _(act):
            def split_hi(b, item):
                slot = T.slot(item)
                reach(act, T.filled[slot], b, T.count[item])
                if item[0] == "wk":
                    reach(act, k_psum, b, SB * (item[1] - 1 if item[1] >= 2 else NP - 1 + item[1]))
                else:
                    reach(act, ring_psum, b, ring_at["v", 1 - item[1], NC - 1] + 1)
                raw, hi, _ = split_parts(Z, M, item, M.stage[:, slot])
                nc.scalar.copy(hi, raw).then_inc(T.hi_done.sem, 1)

            start(act, khi_done, exp_done, te_done, T.hi_done)
            act.wait_ge(bias_in, 32)
            with act.Fori(0, NB) as b:
                for t in range(LAST + 1):
                    w = t - LAG_WEIGH
                    if 0 <= w < STEPS:
                        n = w // SB * ROUNDS + w % SB * 2
                        reach(act, t_psum, b, n + 1)
                        reach(act, pv_done, b, n - 1)
                        nc.scalar.copy(pT[:, 0], ps[:, TB].rearrange("p (m t) -> p m t", m=4)).then_inc(te_done.sem, 1)
                    e = t - LAG_EXP
                    if 0 <= e < STEPS:
                        i, s = divmod(e, SB)
                        if s == 0:
                            reach(act, negm_done, b, i + 1)
                            reach(act, rinv_done, b, i - 1)
                        for h in range(2):
                            p = prob[:, i % 2, h, s * BANK:(s + 1) * BANK]
                            nc.scalar.activation(p, p, ACT.Exp, bias=negm[:, i % 2, h:h + 1], scale=SCALE,
                                                 accum_out=sums[:, i % 2, h, s:s + 1]).then_inc(exp_done.sem, 1)
                    if t < STEPS:
                        reach(act, k_psum, b, t + 1)
                        reach(act, qk_psum, b, 2 * (t - 1))
                        for h in range(2):
                            rows = slice(h * HD, (h + 1) * HD)
                            nc.scalar.activation(kst[rows, t % 2, h], ps[rows, KB + t % 2], ACT.Identity,
                                                 bias=bkT[rows, t // SB:t // SB + 1]).then_inc(khi_done.sem, 1)
                    for kind, g, n in issued[t]:
                        if kind == "ctx":
                            at = ctx_index(g, n)
                            reach(act, ring_psum, b, at + 1)
                            ctx_hi(nc, Z, X, ps, g, n, VB + at % 2)
                    for item in splits[t]:
                        split_hi(b, item)

        @block.vector
        def _(dve):
            start(dve, klo_done, qk_out, mt_done, negm_done, to_done, total_done, rinv_done, rb_done, o_free, attn_done,
                  T.lo_done)
            dve.wait_ge(bias_in, 32)
            with dve.Fori(0, NB) as b:
                for t in range(LAST + 1):
                    w = t - LAG_WEIGH
                    if w >= SB and w % SB == 0:
                        i = w // SB - 1
                        reach(dve, r_psum, b, i + 1)
                        if i == 0:
                            reach(dve, ring_psum, b, 0)
                        nc.vector.tensor_copy(rb[:], ps[:, OB, P:2 * P]).then_inc(rb_done.sem, 1)
                        reach(dve, rb_done, b, i + 1)
                        reach(dve, attn_done, b, i)
                        nc.vector.tensor_tensor(scaled[:], ps[:, OB, 0:P], rb[:], ALU.mult).then_inc(o_free.sem, 1)
                        reach(dve, o_free, b, i + 1)
                        nc.vector.tensor_scalar(attnT[:, i], scaled[:], bvT[:, i:i + 1], None, ALU.add).then_inc(attn_done.sem, 1)
                    if 0 <= w < STEPS:
                        n = w // SB * ROUNDS + w % SB * 2 + 1
                        reach(dve, t_psum, b, n + 1)
                        reach(dve, pv_done, b, n - 1)
                        nc.vector.tensor_copy(pT[:, 1], ps[:, TB + 1].rearrange("p (m t) -> p m t", m=4)).then_inc(to_done.sem, 1)
                    if 0 <= w < STEPS and w % SB == SB - 1:
                        i = w // SB
                        reach(dve, exp_done, b, 2 * SB * (i + 1))
                        nc.vector.tensor_reduce(total[:], sums[:, i % 2], AX.X, ALU.add).then_inc(total_done.sem, 1)
                        reach(dve, total_done, b, i + 1)
                        reach(dve, r_psum, b, i - 1)
                        nc.vector.reciprocal(rinv[:, i % 2], total[:]).then_inc(rinv_done.sem, 1)
                        reach(dve, rinv_done, b, i + 1)
                    e = t - LAG_SCORE
                    if 0 <= e < STEPS:
                        i, s = divmod(e, SB)
                        for h in range(2):
                            reach(dve, qk_psum, b, 2 * e + h + 1)
                            reach(dve, t_psum, b, ROUNDS * (i - 2) + 2 * (s + 1))
                            if s == 0:
                                reach(dve, negm_done, b, i - 1)
                            nc.vector.tensor_scalar(prob[:, i % 2, h, s * BANK:(s + 1) * BANK], ps[:, QB], 1.0, None,
                                                    ALU.mult, ALU.max, accum_out=mx[:, i % 2, h, s:s + 1]).then_inc(qk_out.sem, 1)
                        if s == SB - 1:
                            reach(dve, qk_out, b, 2 * (e + 1))
                            nc.vector.tensor_reduce(mt[:], mx[:, i % 2], AX.X, ALU.max).then_inc(mt_done.sem, 1)
                            reach(dve, mt_done, b, i + 1)
                            nc.vector.tensor_scalar(negm[:, i % 2], mt[:], -SCALE, None, ALU.mult).then_inc(negm_done.sem, 1)
                            reach(dve, negm_done, b, i + 1)
                    if t < STEPS:
                        for h in range(2):
                            rows, other = slice(h * HD, (h + 1) * HD), slice((1 - h) * HD, (2 - h) * HD)
                            reach(dve, khi_done, b, 2 * t + h + 1)
                            nc.vector.scalar_tensor_tensor(kst[other, t % 2, h], ps[rows, KB + t % 2],
                                                           bkT[rows, t // SB:t // SB + 1], kst[rows, t % 2, h].bitcast(F32),
                                                           ALU.add, ALU.subtract).then_inc(klo_done.sem, 1)
                    for item in issued[t]:
                        (kind, g, n), at = item, ring_at[item]
                        bank = VB + at % 2
                        if kind == "ctx":
                            reach(dve, chi_done, b, 4 * g + n + 1)
                            ctx_lo(nc, Z, X, ps, g, n, bank)
                            continue
                        reach(dve, ring_psum, b, at + 1)
                        if kind == "v":
                            reach(dve, pv_done, b, 0 if g == 0 else (HALF - 1) * ROUNDS + n // 2 + 1)
                            nc.vector.tensor_copy(V[:, n], ps[:, bank]).then_inc(ring_out.sem, 1)
                        else:
                            reach(dve, ring_out, b, at)
                            rows = M.x2[:, bass.ds(b * D, D)]
                            nc.vector.tensor_tensor(rows, ps[:, bank], rows, ALU.add).then_inc(ring_out.sem, 1)
                    for item in splits[t]:
                        reach(dve, T.hi_done, b, T.split_at[item] + 1)
                        raw, hi, lo = split_parts(Z, M, item, M.stage[:, T.slot(item)])
                        nc.vector.tensor_tensor(lo, raw, hi.bitcast(F32), ALU.subtract).then_inc(T.lo_done.sem, 1)


SELF_HD = 32


def load_rows(sp, Z, M, qkv_w, fc_w, part):
    G = P // SELF_HD
    for t in ((0, 1), (2,), ())[part]:
        for r in range(G):
            sp.dma_start(M.w_rows[r * SELF_HD:(r + 1) * SELF_HD, t * G:(t + 1) * G],
                         qkv_w.rearrange("(g r t d) c -> r t d g c", g=G, r=G, t=3)[r, t]).then_inc(M.rows_in[part], 16)
    if part == 2:
        sp.dma_start(M.w_rows[:, 3 * G:], fc_w.rearrange("(m p) c -> p m c", p=P)).then_inc(M.rows_in[part], 16)


def load_tile(sp, Z, M, projections, m):
    t, eg = divmod(m, 4)
    for i in range(4):
        if t < 3:
            dst = M.w_tiles[:, m % 4, i].rearrange("p (e h) -> p e h", e=4)
            src = projections[t][eg * 4:(eg + 1) * 4, i * P:(i + 1) * P].rearrange("e p h -> p e h")
        else:
            dst, src = M.w_tiles[:, m % 4, i], projections[t][eg * 4 + i]
        sp.dma_start(dst, src).then_inc(M.tile_in[m % 4], 16)


def self_attention(nc, Z, M, head_mask, qkv_b, fc_b, gates, projections):
    NB, C, D = Z.NB, Z.C, Z.D
    H, HD = 16, SELF_HD
    G = P // HD
    TILES = 4 * G
    ORDER = [t * G + g for g in range(G) for t in range(2)] + list(range(2 * G, TILES))
    TOK = NB * P
    U = NB * G
    LAG = 4
    BUFS = 6
    WB, XB, LB, PB, AB, VB, FB = 0, 4, 0, 2, 4, 6, 7
    with ExitStack() as ctx:
        sb = lambda name, shape, dt=F32: ctx.enter_context(nc.sbuf_tensor("c_" + name, shape, dt))
        sem = lambda name: ctx.enter_context(nc.semaphore("c_" + name))
        ps = ctx.enter_context(nc.psum_tensor("c_ps", [P, 8, BANK], F32))
        x2 = M.x2[:].rearrange("p (b d) -> p b d", b=NB)
        ident = M.ident
        whi, wlo = sb("whi", [P, C, 4 * D], F32R), sb("wlo", [P, C, 4 * D], F32R)
        fb_b = sb("fb_b", [P, D])
        bv_b = sb("bv_b", [P, H, HD])
        hm_b = sb("hm_b", [P, H])
        bqk = sb("bqk", [P, 2, G])
        hmT = sb("hmT", [P, 2, G])
        xn = sb("xn", [P, NB, D])
        xhi, xlo = sb("xhi", [P, C, TOK], F32R), sb("xlo", [P, C, TOK], F32R)
        qkT = sb("qkT", [P, 2, G, TOK])
        v = sb("v", [P, NB, H, HD])
        vb = sb("vb", [P, 2, H, HD])
        prob = sb("prob", [P, BUFS, G, P])
        negm = sb("negm", [P, U, G])
        sums = sb("sums", [P, U, G])
        rinv = sb("rinv", [P, U, G])
        pT = sb("pT", [P, 2 * G, G, P])
        aohi, aolo = sb("aohi", [P, 2, C, P], F32R), sb("aolo", [P, 2, C, P], F32R)
        stats, mv = sb("stats", [P, NB, 6]), sb("mv", [P, NB, 2])
        var, std, rstd = sb("var", [P, NB]), sb("std", [P, NB]), sb("rstd", [P, NB])

        small_in = sem("small_in")
        ln = [sem(n) for n in LN_STEPS]
        wt_psum, whi_done, wlo_done = sem("wt_psum"), sem("whi_done"), sem("wlo_done")
        xT_psum, xhi_done, xlo_done = sem("xT_psum"), sem("xhi_done"), sem("xlo_done")
        hm_done, qk_psum, qk_done = sem("hm_done"), sem("qk_psum"), sem("qk_done")
        egate_done, gate_done = sem("egate_done"), sem("gate_done")
        v_psum, vb_done, v_done = sem("v_psum"), sem("vb_done"), sem("v_done")
        l_psum, max_done, exp_done = sem("l_psum"), sem("max_done"), sem("exp_done")
        rinv_done, norm_done = sem("rinv_done"), sem("norm_done")
        t_psum, t_done, pv_psum = sem("t_psum"), sem("t_done"), sem("pv_psum")
        aohi_done, aolo_done = sem("aohi_done"), sem("aolo_done")
        fc_psum, x1b_done, x2_done = sem("fc_psum"), sem("x1b_done"), sem("x2_done")
        block = ctx.enter_context(nc.Block())
        SMALL = 16 * (4 + 3 * G)

        @block.sync
        def _(sp):
            for m, rows in enumerate((2 * G, 2 * G, 3 * G, 4 * G)):
                sp.wait_ge(wt_psum, rows)
                load_tile(sp, Z, M, projections, m)

        @block.gpsimd
        def _(pool):
            for r in range(G):
                rows = slice(r * HD, (r + 1) * HD)
                for t in range(2):
                    pool.dma_start(bqk[rows, t], qkv_b.rearrange("(g r t d) -> r t d g", g=G, r=G, t=3)[r, t],
                                   allow_slow_non_contiguous=True).then_inc(small_in, 16)
                pool.dma_start(hmT[rows, 1], head_mask.rearrange("(g r) -> r g", g=G)[r:r + 1].broadcast_to([HD, G]),
                               allow_slow_non_contiguous=True).then_inc(small_in, 16)
            pool.dma_start(fb_b[:], fc_b.rearrange("(a d) -> a d", a=1).broadcast_to([P, D])).then_inc(small_in, 16)
            pool.dma_start(hm_b[:], head_mask.rearrange("(a d) -> a d", a=1).broadcast_to([P, H])).then_inc(small_in, 16)
            bias = qkv_b.rearrange("(a h t d) -> a h t d", a=1, t=3, d=HD)
            pool.dma_start(bv_b[:], bias[:, :, 2].broadcast_to([P, H, HD])).then_inc(small_in, 16)
            pool.dma_start(M.gate[:, 0], gates.rearrange("(a e) -> a e", a=1).broadcast_to([P, Z.E])).then_inc(small_in, 16)
            pool.wait_ge(small_in, SMALL)
            for b in range(NB):
                pool.wait_ge(ln[5], b + 1)
                nc.gpsimd.tensor_tensor(x2[:, b], x2[:, b], fb_b[:], ALU.add).then_inc(x1b_done, 1)
            for u in range(U):
                pool.wait_ge(rinv_done, u + 1)
                p = prob[:, u % BUFS]
                nc.gpsimd.tensor_tensor(p, p, rinv[:, u, :, None].broadcast_to([P, G, P]), ALU.mult).then_inc(norm_done, 1)

        @block.tensor
        def _(pe):
            def weight_tile(m):
                if m in (0, 2 * G, 3 * G):
                    part = max(m // G - 1, 0)
                    pe.wait_ge(M.rows_in[part], (16 * 2 * G, 16 * G, 16)[part])
                if m >= 4:
                    pe.wait_ge(wlo_done, m - 3)
                for c in range(C):
                    mm = nc.tensor.transpose(ps[:, WB + m % 4, c * P:(c + 1) * P],
                                             M.w_rows[:, ORDER[m], c * P:(c + 1) * P], ident[:])
                mm.then_inc(wt_psum, 1)

            def passes(out, a, w):
                terms = [(i, j, c) for i, j in ((0, 0), (0, 1), (1, 0)) for c in range(C)]
                for n, (i, j, c) in enumerate(terms):
                    mm = nc.tensor.matmul(out, a(i, c), w(j, c), start=n == 0, stop=n == len(terms) - 1)
                return mm

            W, XT = (whi, wlo), (xhi, xlo)

            def project_qk(j):
                g, t = divmod(j, 2)
                pe.wait_ge(wlo_done, j + 1)
                if j >= 2:
                    pe.wait_ge(qk_done, j - 1)
                tile = (t * G + g) * P
                passes(ps[:, XB + j % 2], lambda i, c: W[i][:, c, tile:tile + P], lambda i, c: XT[i][:, c]
                       ).then_inc(qk_psum, 1)

            def project_v(b):
                pe.wait_ge(wlo_done, 3 * G)
                if b >= 2:
                    pe.wait_ge(vb_done, b - 1)
                passes(ps[:, VB + b % 2], lambda i, c: XT[i][:, c, b * P:(b + 1) * P],
                       lambda i, c: W[i][:, c, 2 * D:3 * D]).then_inc(v_psum, 1)

            def logits(u):
                b, r = divmod(u, G)
                rows = slice(r * HD, (r + 1) * HD)
                if u == 0:
                    pe.wait_ge(qk_done, 2 * G)
                    pe.wait_ge(wlo_done, TILES)
                if u >= 2:
                    pe.wait_ge(exp_done, u - 1)
                for g in range(G):
                    mm = nc.tensor.matmul(ps[:, LB + u % 2, g * P:(g + 1) * P], qkT[rows, 0, g, b * P:(b + 1) * P],
                                          qkT[rows, 1, g, b * P:(b + 1) * P], start=True, stop=True)
                mm.then_inc(l_psum, 1)

            def transpose_probs(u):
                pe.wait_ge(norm_done, u + 1)
                if u >= 2:
                    pe.wait_ge(t_done, u - 1)
                for g in range(G):
                    mm = nc.tensor.transpose(ps[:, PB + u % 2, g * P:(g + 1) * P], prob[:, u % BUFS, g], ident[:])
                mm.then_inc(t_psum, 1)

            def weigh(b):
                pe.wait_ge(t_done, G * (b + 1))
                pe.wait_ge(v_done, b + 1)
                if b >= 2:
                    pe.wait_ge(aolo_done, b - 1)
                for g in range(G):
                    for r in range(G):
                        mm = nc.tensor.matmul(ps[r * HD:(r + 1) * HD, AB + b % 2, g * P:(g + 1) * P], v[:, b, G * g + r],
                                              pT[:, (b * G + r) % (2 * G), g], start=True, stop=True)
                mm.then_inc(pv_psum, 1)

            def out_product(b):
                pe.wait_ge(aolo_done, b + 1)
                pe.wait_ge(*(x2_done, b) if b >= 1 else (vb_done, NB))
                A = (aohi, aolo)
                passes(ps[:, FB], lambda i, c: A[i][:, b % 2, c], lambda i, c: W[i][:, c, 3 * D:]).then_inc(fc_psum, 1)

            for m in range(4):
                weight_tile(m)
            for b in range(NB):
                pe.wait_ge(ln[5], b + 1)
                if b >= 2:
                    pe.wait_ge(xlo_done, b - 1)
                for c in range(C):
                    mm = nc.tensor.transpose(ps[:, XB + b % 2, c * P:(c + 1) * P], xn[:, b, c * P:(c + 1) * P], ident[:])
                mm.then_inc(xT_psum, 1)
            for m in range(4, 2 * G):
                weight_tile(m)
            pe.wait_ge(xlo_done, NB)
            for j in range(2 * G):
                project_qk(j)
                weight_tile(2 * G + j)
            for s in range(U + LAG + 2):
                if s < U:
                    logits(s)
                if s < NB:
                    project_v(s)
                if 0 <= s - LAG < U:
                    transpose_probs(s - LAG)
                if 0 <= s - LAG - 1 < U and (s - LAG - 1) % G == G - 1:
                    weigh((s - LAG - 1) // G)
                b, at = divmod(s - LAG - 1 - G, G)
                if 0 <= b < NB and at == 0:
                    out_product(b)

        @block.scalar
        def _(act):
            def weight_hi(m):
                act.wait_ge(wt_psum, m + 1)
                tile = ORDER[m] * P
                nc.scalar.copy(whi[:, :, tile:tile + P], ps[:, WB + m % 4].rearrange("p (c e) -> p c e", c=C)
                               ).then_inc(whi_done, 1)

            for m in range(4):
                weight_hi(m)
            act.wait_ge(ln[2], 1)
            nc.scalar.activation(std[:], var[:], ACT.Sqrt).then_inc(ln[3], 1)
            for b in range(NB):
                act.wait_ge(xT_psum, b + 1)
                nc.scalar.copy(xhi[:, :, b * P:(b + 1) * P], ps[:, XB + b % 2].rearrange("p (c t) -> p c t", c=C)
                               ).then_inc(xhi_done, 1)
            for m in range(4, TILES):
                weight_hi(m)
            for s in range(U + LAG + 2):
                if s < U:
                    act.wait_ge(max_done, s + 1)
                    if s >= BUFS:
                        act.wait_ge(t_psum, s - BUFS + 1)
                    for g in range(G):
                        ins = nc.scalar.activation(prob[:, s % BUFS, g], ps[:, LB + s % 2, g * P:(g + 1) * P], ACT.Exp,
                                                   bias=negm[:, s, g:g + 1], accum_out=sums[:, s, g:g + 1])
                    ins.then_inc(exp_done, 1)
                u = s - LAG - 1
                if 0 <= u < U and u % G == G - 1:
                    b = u // G
                    act.wait_ge(pv_psum, b + 1)
                    if b >= 2:
                        act.wait_ge(fc_psum, b - 1)
                    nc.scalar.copy(aohi[:, b % 2], ps[:, AB + b % 2].rearrange("p (c q) -> p c q", c=C)).then_inc(aohi_done, 1)
                if s == U:
                    act.wait_ge(small_in, SMALL)
                    nc.scalar.activation(M.gate[:, 1], M.gate[:, 0], ACT.Exp, scale=-1.0).then_inc(egate_done, 1)

        @block.vector
        def _(dve):
            def weight_lo(m):
                dve.wait_ge(whi_done, m + 1)
                tile = ORDER[m] * P
                nc.vector.tensor_tensor(wlo[:, :, tile:tile + P], ps[:, WB + m % 4].rearrange("p (c e) -> p c e", c=C),
                                        whi[:, :, tile:tile + P].bitcast(F32), ALU.subtract).then_inc(wlo_done, 1)

            def v_tile(b):
                dve.wait_ge(v_psum, b + 1)
                if b >= 2:
                    dve.wait_ge(v_done, b - 1)
                nc.vector.tensor_tensor(vb[:, b % 2], ps[:, VB + b % 2].rearrange("p (h d) -> p h d", h=H), bv_b[:],
                                        ALU.add).then_inc(vb_done, 1)
                dve.wait_ge(vb_done, b + 1)
                nc.vector.tensor_tensor(v[:, b], vb[:, b % 2], hm_b[:, :, None].broadcast_to([P, H, HD]),
                                        ALU.mult).then_inc(v_done, 1)

            layer_norm_stats(nc, dve, x2, lambda b: None, stats, mv, ln, NB)
            layer_norm_apply(nc, dve, x2, xn, (mv, var, std, rstd), ln, NB)
            for m in range(4):
                weight_lo(m)
            for b in range(NB):
                dve.wait_ge(xhi_done, b + 1)
                nc.vector.tensor_tensor(xlo[:, :, b * P:(b + 1) * P], ps[:, XB + b % 2].rearrange("p (c t) -> p c t", c=C),
                                        xhi[:, :, b * P:(b + 1) * P].bitcast(F32), ALU.subtract).then_inc(xlo_done, 1)
            for m in range(4, 2 * G):
                weight_lo(m)
            dve.wait_ge(small_in, SMALL)
            nc.vector.tensor_scalar(hmT[:, 0], hmT[:, 1], HD ** -0.5, None, ALU.mult).then_inc(hm_done, 1)
            dve.wait_ge(hm_done, 1)
            for j in range(2 * G):
                g, t = divmod(j, 2)
                dve.wait_ge(qk_psum, j + 1)
                nc.vector.tensor_scalar(qkT[:, t, g], ps[:, XB + j % 2], bqk[:, t, g:g + 1], hmT[:, t, g:g + 1],
                                        ALU.add, ALU.mult).then_inc(qk_done, 1)
                weight_lo(2 * G + j)
            for s in range(U + LAG + 2):
                if s < U:
                    dve.wait_ge(l_psum, s + 1)
                    nc.vector.tensor_reduce(negm[:, s], ps[:, LB + s % 2].rearrange("p (g k) -> p g k", g=G), AX.X, ALU.max,
                                            negate=True).then_inc(max_done, 1)
                if 1 <= s <= U:
                    dve.wait_ge(exp_done, s)
                    nc.vector.reciprocal(rinv[:, s - 1], sums[:, s - 1]).then_inc(rinv_done, 1)
                if s < NB:
                    v_tile(s)
                u = s - LAG
                if 0 <= u < U:
                    dve.wait_ge(t_psum, u + 1)
                    if u >= 2 * G:
                        dve.wait_ge(pv_psum, u // G - 1)
                    nc.vector.tensor_copy(pT[:, u % (2 * G)], ps[:, PB + u % 2].rearrange("p (g q) -> p g q", g=G)
                                          ).then_inc(t_done, 1)
                u = s - LAG - 1
                if 0 <= u < U and u % G == G - 1:
                    b = u // G
                    dve.wait_ge(aohi_done, b + 1)
                    nc.vector.tensor_tensor(aolo[:, b % 2], ps[:, AB + b % 2].rearrange("p (c q) -> p c q", c=C),
                                            aohi[:, b % 2].bitcast(F32), ALU.subtract).then_inc(aolo_done, 1)
                b, at = divmod(s - LAG - 1 - G, G)
                if 0 <= b < NB and at == 0:
                    dve.wait_ge(fc_psum, b + 1)
                    dve.wait_ge(x1b_done, b + 1)
                    nc.vector.tensor_tensor(x2[:, b], ps[:, FB], x2[:, b], ALU.add).then_inc(x2_done, 1)
                    dve.wait_ge(x2_done, b + 1)
                    nc.vector.bn_stats(M.stats[:, b], x2[:, b]).then_inc(M.ln[0], 1)
                    dve.wait_ge(M.ln[0], b + 1)
                    nc.vector.bn_aggr(M.mv[:, b], M.stats[:, b]).then_inc(M.ln[1], 1)
                if s == U + 1:
                    dve.wait_ge(egate_done, 1)
                    nc.vector.tensor_scalar(M.gate[:, 2], M.gate[:, 1], 1.0, None, ALU.add).then_inc(gate_done, 1)
                    dve.wait_ge(gate_done, 1)
                    nc.vector.reciprocal(M.gate[:, 3], M.gate[:, 2]).then_inc(gate_done, 1)


def expert_attention(nc, Z, M, sim_matrix, projections, out):
    NB, C, D = Z.NB, Z.C, Z.D
    E, HD = projections[0].shape[0], projections[0].shape[2]
    EG = BANK // HD
    NG = E // EG
    TILES = 3 * NG
    ALL = 4 * NG
    TOK = NB * P
    SCALE = HD ** -0.5
    NORM_EPS = 1e-12
    NEG = -3e38
    ATTEND = 2 * NG
    YB = 2
    HB = (0, 1, 6, 7)
    SIMB, GATEB, SB_, PTB = 5, 0, 6, 7
    OUTS = [(m, b, e) for m in range(TILES, ALL) for pair in range(0, NB, 2) for e in range(EG) for b in (pair, pair + 1)]
    with ExitStack() as ctx:
        sb = lambda name, shape, dt=F32: ctx.enter_context(nc.sbuf_tensor("d_" + name, shape, dt))
        sem = lambda name: ctx.enter_context(nc.semaphore("d_" + name))
        ps = ctx.enter_context(nc.psum_tensor("d_ps", [P, 8, BANK], F32))
        x2 = M.x2[:].rearrange("p (b d) -> p b d", b=NB)
        raw, ident, ln, mv = M.w_tiles, M.ident, M.ln, M.mv
        whi = sb("whi", [P, 2, C, BANK], F32R)
        wlo = sb("wlo", [P, 2, C, BANK], F32R)
        xn = sb("xn", [P, NB, D])
        hhi = sb("hhi", [P, C, TOK], F32R)
        hlo = sb("hlo", [P, C, TOK], F32R)
        acc = sb("acc", [P, 3, NB, EG, HD])
        qkv = sb("qkv", [P, 3, NB, HD])
        qkT = sb("qkT", [P, 2, TOK])
        prob = sb("prob", [P, NB, P])
        probT = sb("probT", [P, NB, P])
        aohi, aolo = sb("aohi", [P, NB, P], F32R), sb("aolo", [P, NB, P], F32R)
        cmask = sb("cmask", [P, P])
        sm = sb("sm", [P, C, E])
        sm_split = sb("sm_split", [P, C, 2 * E], F32R)
        sq = sb("sq", [P, C, E])
        ones = sb("ones", [P, P])
        junk = sb("junk", [P, D])
        norm = sb("norm", [P, 4, NB + E])
        lgs, lg0 = sb("lgs", [P, NB, E]), sb("lg0", [P, NB, E])
        lg = sb("lg", [P, NB, E])
        rev = sb("rev", [P, E])
        g = sb("g", [P, 16, NB, E])
        g1 = sb("g1", [P, 8, NB])
        rw = sb("rw", [P, NB, E])
        mx, nmx, sums, rinv = sb("mx", [P, NB]), sb("nmx", [P, NB]), sb("sums", [P, NB]), sb("rinv", [P, NB])
        var, std, rstd = sb("var", [P, NB]), sb("std", [P, NB]), sb("rstd", [P, NB])

        small_in, const_done, sq_done = sem("small_in"), sem("const_done"), sem("sq_done")
        hT_psum, hhi_done, hlo_done = sem("hT_psum"), sem("hhi_done"), sem("hlo_done")
        smhi_done, smlo_done = sem("smhi_done"), sem("smlo_done")
        whi_done, wlo_done = sem("whi_done"), sem("wlo_done")
        sim_psum, gate_psum, root_done, gexp_done = sem("sim_psum"), sem("gate_psum"), sem("root_done"), sem("gexp_done")
        chain = sem("chain")
        square_done, norm_done, gsub_done = sem("square_done"), sem("norm_done"), sem("gsub_done")
        y_psum, y_used = sem("y_psum"), sem("y_used")
        qkv_done, qkT_psum, qkT_done = sem("qkv_done"), sem("qkT_psum"), sem("qkT_done")
        s_psum, max_done, exp_done, prob_done = sem("s_psum"), sem("max_done"), sem("exp_done"), sem("prob_done")
        pT_psum, pT_done, ao_psum = sem("pT_psum"), sem("pT_done"), sem("ao_psum")
        aohi_done, aolo_done = sem("aohi_done"), sem("aolo_done")
        o_psum, o_used, stored = sem("o_psum"), sem("o_used"), sem("stored")
        block = ctx.enter_context(nc.Block())

        @block.sync
        def _(sp):
            for m in range(4, ALL):
                sp.wait_ge(wlo_done, m - 3)
                load_tile(sp, Z, M, projections, m)
            for b in range(NB):
                sp.wait_ge(o_used, max(n for n, o in enumerate(OUTS) if o[1] == b) + 1)
                sp.dma_start(out[b], x2[:, b]).then_inc(stored, 16)
            sp.wait_ge(stored, 16 * NB)

        @block.gpsimd
        def _(pool):
            pool.dma_start(sm[:], sim_matrix.rearrange("(c p) e -> p c e", p=P)).then_inc(small_in, 16)
            nc.gpsimd.memset(ones[:], 1.0).then_inc(const_done, 1)
            nc.gpsimd.memset(cmask[:], 0.0).then_inc(const_done, 1)
            nc.gpsimd.iota(rev[:], pattern=[[-1, E]], base=E, channel_multiplier=0,
                           allow_small_or_imprecise_dtypes=True).then_inc(const_done, 1)
            pool.wait_ge(const_done, 3)
            nc.gpsimd.affine_select(out=cmask[:], in_=cmask[:], compare_op=ALU.is_ge, fill=NEG, base=0,
                                    pattern=[[-1, P]], channel_multiplier=1).then_inc(const_done, 1)
            for m in range(TILES + 1, ALL):
                pool.wait_ge(whi_done, m + 1)
                nc.gpsimd.tensor_tensor(wlo[:, m % 2], raw[:, m % 4], whi[:, m % 2].bitcast(F32), ALU.subtract
                                        ).then_inc(wlo_done, 1)

        @block.tensor
        def _(pe):
            def product(m, b):
                n = m * NB + b
                if n >= 4:
                    pe.wait_ge(y_used, (n - 3) * EG)
                elif YB + n == SIMB:
                    pe.wait_ge(norm_done, 1)
                pe.wait_ge(whi_done, m + 1)
                pe.wait_ge(hhi_done, b + 1)
                terms = [(hh, ww, c) for hh, ww in ((hhi, whi), (hlo, whi), (hhi, wlo)) for c in range(C)]
                for i, (hh, ww, c) in enumerate(terms):
                    if i == C:
                        pe.wait_ge(hlo_done, b + 1)
                    if i == 2 * C:
                        pe.wait_ge(wlo_done, m + 1)
                    mm = nc.tensor.matmul(ps[:, YB + n % 4], hh[:, c, b * P:(b + 1) * P], ww[:, m % 2, c],
                                          start=i == 0, stop=i == len(terms) - 1)
                mm.then_inc(y_psum, 1)

            def gate_logits():
                pe.wait_ge(hlo_done, NB)
                pe.wait_ge(smlo_done, 1)
                terms = [(hh, c) for hh in (hhi, hlo) for c in range(C)]
                for b in range(NB):
                    for i, (hh, c) in enumerate(terms):
                        mm = nc.tensor.matmul(ps[:, GATEB, b * 2 * E:(b + 1) * 2 * E], hh[:, c, b * P:(b + 1) * P],
                                              sm_split[:, c], start=i == 0, stop=i == len(terms) - 1)
                mm.then_inc(gate_psum, 1)

            def transpose_qk():
                for t in range(2):
                    pe.wait_ge(qkv_done, t + 1)
                    for b in range(NB):
                        mm = nc.tensor.transpose(ps[:, t, b * P:(b + 1) * P], qkv[:, t, b], ident[:])
                    mm.then_inc(qkT_psum, 1)

            def scores():
                pe.wait_ge(qkT_done, 2)
                for b in range(NB):
                    mm = nc.tensor.matmul(ps[:, SB_, b * P:(b + 1) * P], qkT[:, 0, b * P:(b + 1) * P],
                                          qkT[:, 1, b * P:(b + 1) * P], start=True, stop=True)
                mm.then_inc(s_psum, 1)

            def transpose_probs():
                for b in range(NB):
                    pe.wait_ge(prob_done, b + 1)
                    mm = nc.tensor.transpose(ps[:, PTB, b * P:(b + 1) * P], prob[:, b], ident[:])
                mm.then_inc(pT_psum, 1)

            def attend(b):
                pe.wait_ge(pT_done, 1)
                pe.wait_ge(qkv_done, 2 + b + 1)
                nc.tensor.matmul(ps[:, HB[b], :P], qkv[:, 2, b], probT[:, b], start=True, stop=True).then_inc(ao_psum, 1)

            def output(n):
                m, b, e = OUTS[n]
                pe.wait_ge(*(y_used, (TILES * NB + n - 3) * EG) if n < 4 else (o_used, n - 3))
                if e == 0:
                    pe.wait_ge(wlo_done, m + 1)
                pe.wait_ge(aolo_done, b + 1)
                terms = ((aohi, whi), (aolo, whi), (aohi, wlo))
                for i, (aa, ww) in enumerate(terms):
                    mm = nc.tensor.matmul(ps[:, YB + n % 4], aa[:, b], ww[:, m % 2, e], start=i == 0, stop=i == 2)
                mm.then_inc(o_psum, 1)

            for b in range(NB):
                pe.wait_ge(ln[5], b + 1)
                for c in range(C):
                    mm = nc.tensor.transpose(ps[:, HB[b], c * P:(c + 1) * P], xn[:, b, c * P:(c + 1) * P], ident[:])
                mm.then_inc(hT_psum, 1)
            pe.wait_ge(const_done, 4)
            pe.wait_ge(sq_done, 1)
            for c in range(C):
                mm = nc.tensor.matmul(ps[:, SIMB, :E], ones[:], sq[:, c], start=c == 0, stop=c == C - 1)
            mm.then_inc(sim_psum, 1)
            after = {(0, 0): gate_logits, (ATTEND, 1): transpose_qk, (ATTEND, 3): scores, (ATTEND + 2, 1): transpose_probs}
            for m in range(TILES):
                for b in range(NB):
                    product(m, b)
                    if (m, b) in after:
                        after[m, b]()
                    if m == TILES - 1 and b >= 1:
                        attend(b - 1)
            for n in range(len(OUTS)):
                output(n)
                if n == 1:
                    attend(NB - 1)

        @block.scalar
        def _(act):
            def weight_hi(m):
                act.wait_ge(M.tile_in[m % 4], 16 * 4 * (m // 4 + 1))
                if m >= TILES + 2:
                    act.wait_ge(o_psum, (m - 1 - TILES) * EG * NB)
                elif m >= 2:
                    act.wait_ge(y_psum, (m - 1) * NB)
                nc.scalar.copy(whi[:, m % 2], raw[:, m % 4]).then_inc(whi_done, 1)

            act.wait_ge(ln[2], 1)
            nc.scalar.activation(std[:], var[:], ACT.Sqrt).then_inc(ln[3], 1)
            weight_hi(0)
            act.wait_ge(small_in, 16)
            nc.scalar.copy(sm_split[:, :, :E], sm[:]).then_inc(smhi_done, 1)
            for b in range(NB):
                act.wait_ge(hT_psum, b + 1)
                nc.scalar.copy(hhi[:, :, b * P:(b + 1) * P], ps[:, HB[b]].rearrange("p (c t) -> p c t", c=C)
                               ).then_inc(hhi_done, 1)
            for b in range(NB):
                if b >= 1:
                    act.wait_ge(square_done, b)
                nc.scalar.activation(junk[:], xn[:, b], ACT.Square, accum_out=norm[:, 0, b:b + 1]).then_inc(square_done, 1)
            act.wait_ge(norm_done, 2)
            nc.scalar.activation(norm[:, 2], norm[:, 1], ACT.Sqrt).then_inc(root_done, 1)
            weight_hi(1)
            act.wait_ge(gsub_done, 1)
            nc.scalar.activation(g[:, 11], g[:, 10], ACT.Exp).then_inc(gexp_done, 1)
            for m in range(2, ALL):
                if m == ATTEND + 3:
                    for b in range(NB):
                        act.wait_ge(max_done, b + 1)
                        nc.scalar.activation(prob[:, b], prob[:, b], ACT.Exp, bias=nmx[:, b:b + 1], scale=SCALE,
                                             accum_out=sums[:, b:b + 1]).then_inc(exp_done, 1)
                if m == TILES:
                    act.wait_ge(pT_psum, 1)
                    nc.scalar.copy(probT[:], ps[:, PTB].rearrange("p (b t) -> p b t", b=NB)).then_inc(pT_done, 1)
                if m == TILES + 1:
                    for b in range(NB):
                        act.wait_ge(ao_psum, b + 1)
                        nc.scalar.copy(aohi[:, b], ps[:, HB[b], :P]).then_inc(aohi_done, 1)
                weight_hi(m)

        @block.vector
        def _(dve):
            V = nc.vector
            count = [0]

            def step(ins):
                count[0] += 1
                ins.then_inc(chain, 1)
                dve.wait_ge(chain, count[0])

            def weight_lo(m):
                dve.wait_ge(whi_done, m + 1)
                V.tensor_tensor(wlo[:, m % 2], raw[:, m % 4], whi[:, m % 2].bitcast(F32), ALU.subtract).then_inc(wlo_done, 1)

            def tokens_lo(b):
                dve.wait_ge(hhi_done, b + 1)
                V.tensor_tensor(hlo[:, :, b * P:(b + 1) * P], ps[:, HB[b]].rearrange("p (c t) -> p c t", c=C),
                                hhi[:, :, b * P:(b + 1) * P].bitcast(F32), ALU.subtract).then_inc(hlo_done, 1)

            layer_norm_apply(nc, dve, x2, xn, (mv, var, std, rstd), ln, NB)
            dve.wait_ge(small_in, 16)
            V.tensor_tensor(sq[:], sm[:], sm[:], ALU.mult).then_inc(sq_done, 1)
            tokens_lo(0)
            weight_lo(0)
            dve.wait_ge(smhi_done, 1)
            V.tensor_tensor(sm_split[:, :, E:], sm[:], sm_split[:, :, :E].bitcast(F32), ALU.subtract).then_inc(smlo_done, 1)
            for b in range(1, NB):
                tokens_lo(b)
            dve.wait_ge(sim_psum, 1)
            V.tensor_scalar(norm[:, 1, NB:], ps[:, SIMB, :E], NORM_EPS, None, ALU.add).then_inc(norm_done, 1)
            dve.wait_ge(square_done, NB)
            V.tensor_scalar(norm[:, 1, :NB], norm[:, 0, :NB], NORM_EPS, None, ALU.add).then_inc(norm_done, 1)
            dve.wait_ge(root_done, 1)
            step(V.reciprocal(norm[:, 3], norm[:, 2]))
            dve.wait_ge(gate_psum, 1)
            step(V.tensor_reduce(lgs[:], ps[:, GATEB, :NB * 2 * E].rearrange("p (b i e) -> p b e i", b=NB, i=2), AX.X, ALU.add))
            for b in range(NB):
                ins = V.scalar_tensor_tensor(lg0[:, b], lgs[:, b], norm[:, 3, b:b + 1],
                                             norm[:, 3, NB:], ALU.mult, ALU.mult)
            step(ins)
            step(V.tensor_tensor(lg[:], lg0[:], M.gate[:, 3, None, :].broadcast_to([P, NB, E]), ALU.subtract))
            wide = lambda a: a[:, :, None].broadcast_to([P, NB, E])
            revb = rev[:, None, :].broadcast_to([P, NB, E])
            dve.wait_ge(const_done, 4)
            left, top = lg[:], []
            for k in range(2):
                o = 3 * k
                step(V.tensor_reduce(g1[:, 2 * k], left, AX.X, ALU.max))
                step(V.tensor_tensor(g[:, o], left, wide(g1[:, 2 * k]), ALU.is_equal))
                step(V.tensor_tensor(g[:, o + 1], g[:, o], revb, ALU.mult))
                step(V.tensor_reduce(g1[:, 2 * k + 1], g[:, o + 1], AX.X, ALU.max))
                step(V.tensor_tensor(g[:, o + 2], revb, wide(g1[:, 2 * k + 1]), ALU.is_equal))
                top.append(g[:, o + 2])
                if k == 0:
                    step(V.scalar_tensor_tensor(g[:, 6], g[:, 2], -16.0, lg[:], ALU.mult, ALU.add))
                    left = g[:, 6]
            step(V.tensor_tensor(g[:, 7], top[0], top[1], ALU.add))
            step(V.tensor_scalar(g[:, 8], lg[:], 0.0, None, ALU.is_gt))
            step(V.tensor_scalar(g1[:, 4], g1[:, 0], 0.0, None, ALU.is_le))
            step(V.tensor_tensor(g[:, 9], g[:, 7], wide(g1[:, 4]), ALU.mult))
            step(V.tensor_tensor(g[:, 13], g[:, 8], g[:, 9], ALU.add))
            step(V.tensor_scalar(g[:, 12], lg[:], 0.0, None, ALU.max))
            step(V.tensor_reduce(g1[:, 5], g[:, 12], AX.X, ALU.max))
            V.tensor_tensor(g[:, 10], g[:, 12], wide(g1[:, 5]), ALU.subtract).then_inc(gsub_done, 1)
            weight_lo(1)
            dve.wait_ge(gexp_done, 1)
            step(V.tensor_tensor(g[:, 14], g[:, 11], g[:, 13], ALU.mult))
            step(V.tensor_reduce(g1[:, 6], g[:, 14], AX.X, ALU.add))
            step(V.reciprocal(g1[:, 7], g1[:, 6]))
            step(V.tensor_tensor(rw[:], g[:, 14], wide(g1[:, 7]), ALU.mult))

            def use_product(m, b):
                t, eg = divmod(m, NG)
                n = m * NB + b
                dve.wait_ge(y_psum, n + 1)
                if eg > 0:
                    dve.wait_ge(y_used, EG * (n - NB + 1))
                for j in range(EG):
                    e = eg * EG + j
                    y, w = ps[:, YB + n % 4, j * HD:(j + 1) * HD], rw[:, b, e:e + 1]
                    if eg == 0:
                        ins = V.tensor_scalar(acc[:, t, b, j], y, w, None, ALU.mult)
                    else:
                        ins = V.scalar_tensor_tensor(acc[:, t, b, j], y, w, acc[:, t, b, j], ALU.mult, ALU.add)
                    ins.then_inc(y_used, 1)

            def attention_lo(b):
                dve.wait_ge(aohi_done, b + 1)
                V.tensor_tensor(aolo[:, b], ps[:, HB[b], :P], aohi[:, b].bitcast(F32), ALU.subtract).then_inc(aolo_done, 1)

            def copy_qkT():
                for t in range(2):
                    dve.wait_ge(qkT_psum, t + 1)
                    V.tensor_copy(qkT[:, t], ps[:, t]).then_inc(qkT_done, 1)

            def score_maxima():
                dve.wait_ge(s_psum, 1)
                step(V.tensor_tensor(prob[:], ps[:, SB_].rearrange("p (b t) -> p b t", b=NB),
                                     cmask[:, None, :].broadcast_to([P, NB, P]), ALU.add))
                step(V.tensor_reduce(mx[:], prob[:], AX.X, ALU.max))
                V.tensor_scalar(nmx[:], mx[:], -SCALE, None, ALU.mult).then_inc(max_done, NB)

            def normalise():
                dve.wait_ge(exp_done, NB)
                step(V.reciprocal(rinv[:], sums[:]))
                for b in range(NB):
                    V.tensor_scalar(prob[:, b], prob[:, b], rinv[:, b:b + 1], None, ALU.mult).then_inc(prob_done, 1)

            after = {(ATTEND, 2): copy_qkT, (ATTEND + 1, 0): score_maxima, (ATTEND + 1, 3): normalise}
            for m in range(TILES):
                t, eg = divmod(m, NG)
                for b in range(NB):
                    use_product(m, b)
                    if (m, b) in after:
                        after[m, b]()
                    if m == TILES - 1:
                        dve.wait_ge(y_used, EG * (m * NB + b + 1))
                        V.tensor_reduce(qkv[:, t, b], acc[:, t, b].rearrange("p j h -> p h j"), AX.X, ALU.add
                                        ).then_inc(qkv_done, 1)
                        if b >= 1:
                            attention_lo(b - 1)
                if m < TILES - 1:
                    weight_lo(m + 2)
                if eg == NG - 1 and t < 2:
                    dve.wait_ge(y_used, EG * NB * (m + 1))
                    V.tensor_reduce(qkv[:, t], acc[:, t].rearrange("p b j h -> p b h j"), AX.X, ALU.add).then_inc(qkv_done, 1)
            for n, (m, b, e) in enumerate(OUTS):
                dve.wait_ge(o_psum, n + 1)
                before = [i for i in range(n) if OUTS[i][1] == b]
                if before:
                    dve.wait_ge(o_used, before[-1] + 1)
                w = (m - TILES) * EG + e
                V.scalar_tensor_tensor(x2[:, b], ps[:, YB + n % 4], rw[:, b, w:w + 1], x2[:, b],
                                       ALU.mult, ALU.add).then_inc(o_used, 1)
                if n == 1:
                    attention_lo(NB - 1)


NAMES = ['x', 'ctx_1024', 'L0_xattn_Wq', 'L0_xattn_bq', 'L0_xattn_Wk', 'L0_xattn_bk', 'L0_xattn_Wv', 'L0_xattn_bv',
         'L0_xattn_Wo', 'L0_xattn_bo', 'L0_attn_head_mask', 'L0_attn_qkv_w', 'L0_attn_qkv_b', 'L0_attn_fc_w',
         'L0_attn_fc_b', 'L0_ffn_sim_matrix', 'L0_ffn_gates', 'L0_ffn_q_proj', 'L0_ffn_k_proj', 'L0_ffn_v_proj',
         'L0_ffn_o_proj']


def perceiver_layer(nc, x, ctx_1024, Wq, bq, Wk, bk, Wv, bv, Wo, bo, head_mask, qkv_w, qkv_b, fc_w, fc_b,
                    sim_matrix, gates, q_proj, k_proj, v_proj, o_proj, out):
    Z = Shapes(x, ctx_1024, gates)
    scratch = lambda name, shape: nc.dram_tensor(name, shape, F32, kind="Internal").ap()
    q_s = scratch("q_s", [2, Z.NP, P, Z.NB * P])
    projections = (q_proj, k_proj, v_proj, o_proj)
    with ExitStack() as ctx:
        M = Shared(ctx, nc, Z)
        with ExitStack() as inner:
            X = CrossShared(inner, nc, Z)
            prepare(nc, Z, M, X, x, ctx_1024, Wq, bq, Wk, Wv, bo, q_s)
            cross_attention(nc, Z, M, X, ctx_1024, Wk, bk, Wv, bv, Wo, q_s,
                            lambda sp, part: load_rows(sp, Z, M, qkv_w, fc_w, part))
        self_attention(nc, Z, M, head_mask, qkv_b, fc_b, gates, projections)
        expert_attention(nc, Z, M, sim_matrix, projections, out)


def kernel(**inputs):
    import numpy as np
    import concourse.bacc as bacc
    from concourse.bass_utils import run_bass_kernel_spmd

    nc = bacc.Bacc("TRN2", target_bir_lowering=False, num_devices=1)
    arrays, args = {}, []
    for name in NAMES:
        a = np.ascontiguousarray(inputs[name])
        arrays[f"in_{name}"] = a
        args.append(nc.dram_tensor(f"in_{name}", a.shape, mybir.dt.from_np(a.dtype), kind="ExternalInput").ap())
    out = nc.dram_tensor("out", inputs["x"].shape, F32, kind="ExternalOutput").ap()
    perceiver_layer(nc, *args, out)
    r = run_bass_kernel_spmd(nc, [arrays], core_ids=[0])
    return r.results[0]["out"]
```

```python
from contextlib import ExitStack

import concourse.bass as bass
from concourse import mybir

F32 = mybir.dt.float32
F32R = mybir.dt.float32r
ALU = mybir.AluOpType
ACT = mybir.ActivationFunctionType
AX = mybir.AxisListType

P = 128
BANK = 512
EPS = 1e-5
STAGE_SLOTS = 4


class Shapes:

    def __init__(self, x, ctx, gates):
        self.NB, self.TQ, self.D = x.shape
        self.S = ctx.shape[1]
        self.C = self.D // P
        self.E = gates.shape[0]
        self.H, self.HD = 16, 64
        self.HW = self.H * self.HD
        self.NP = self.H // 2
        self.SB = self.S // BANK
        self.NC = self.S // P
        self.HALF = self.NP // 2


LN_STEPS = ("stats_done", "mv_done", "var_done", "std_done", "rstd_done", "xn_done")


def make_identity(nc, pool, ident, sem):
    nc.gpsimd.memset(ident[:], 0.0).then_inc(sem, 1)
    pool.wait_ge(sem, 1)
    nc.gpsimd.affine_select(out=ident[:], in_=ident[:], compare_op=ALU.not_equal, fill=1.0, base=0,
                            pattern=[[-1, P]], channel_multiplier=1).then_inc(sem, 1)


def alias(nc, name, shape, at):
    return nc.alloc_sbuf_tensor_at(name, shape, F32, offset=at)


def reach(eng, s, batch, k):
    b, later = batch
    eng.wait_ge(s.sem, b * s.per + later * s.per + s.base + (k if later or s.base + k > 0 else 0))


class Count:

    def __init__(self, ctx, nc, name, per, base=1):
        self.sem, self.per, self.base = ctx.enter_context(nc.semaphore(name)), per, base


class Shared:

    def __init__(self, ctx, nc, Z):
        sb = lambda name, shape, dt=F32: ctx.enter_context(nc.sbuf_tensor(name, shape, dt))
        self.ident = sb("ident", [P, P])
        self.x2 = sb("x2", [P, Z.NB * Z.D])
        self.wv_at = nc.sbuf_base
        self.wv = sb("wv", [P, 2, Z.C, BANK], F32R)
        self.wk = sb("wk", [P, 2, 2, Z.C, P], F32R)
        self.stage = sb("stage", [P, STAGE_SLOTS, Z.D])
        self.w_rows = alias(nc, "w_rows", [P, 4 * Z.C, Z.D], self.wv_at)
        self.w_tiles = alias(nc, "w_tiles", [P, 4, Z.C, BANK], self.wv_at)
        assert nc.sbuf_base == self.wv_at + 4 * 4 * Z.C * Z.D
        self.rows_in = [ctx.enter_context(nc.semaphore(f"rows_in{i}")) for i in range(3)]
        self.tile_in = [ctx.enter_context(nc.semaphore(f"tile_in{i}")) for i in range(4)]
        self.gate = sb("gate", [P, 4, Z.E])
        self.stats, self.mv = sb("stats", [P, Z.NB * 6]), sb("mv", [P, Z.NB * 2])
        self.ln = [ctx.enter_context(nc.semaphore("e_" + n)) for n in LN_STEPS]


class Stage:

    def __init__(self, ctx, nc, Z):
        wv = lambda g: [("wv", g, c) for c in range(Z.C)]
        half_blocks = [("ctx", n) for n in range(Z.NC // 2)]
        self.items = ([("wk", 2), ("wk", 3)] + wv(1) + [("wk", i) for i in range(4, Z.NP)] + wv(0)[:3] + [("wk", 0)]
                      + half_blocks[:4] + wv(0)[3:] + [("wk", 1)] + half_blocks[4:])
        self.pos, self.owner, self.count, loads = {}, [], {}, [0] * STAGE_SLOTS
        for item in self.items:
            self.pos[item] = len(self.owner)
            self.owner += [item] * (2 if item[0] == "ctx" else 1)
            slot = self.slot(item)
            loads[slot] += 16
            self.count[item] = loads[slot]
        assert len(self.owner) % STAGE_SLOTS == 0
        self.filled = [Count(ctx, nc, f"stage_in{i}", loads[i], 0) for i in range(STAGE_SLOTS)]
        splits = [item for item in self.items if item[0] != "ctx"]
        self.split_at = {item: n for n, item in enumerate(splits)}
        self.SPLITS = len(splits)
        self.hi_done = Count(ctx, nc, "split_hi", self.SPLITS)
        self.lo_done = Count(ctx, nc, "split_lo", self.SPLITS)

    def slot(self, item):
        return self.pos[item] % STAGE_SLOTS

    def early(self, item):
        return item[0] == "ctx" or item in (("wk", 0), ("wk", 1)) or item[:2] == ("wv", 0)

    def split_count(self, item):
        return self.split_at[item] + 1 - (self.SPLITS if self.early(item) else 0)


class CrossShared:

    def __init__(self, ctx, nc, Z):
        sb = lambda name, shape, dt=F32: ctx.enter_context(nc.sbuf_tensor(name, shape, dt))
        count = lambda name, per, base: Count(ctx, nc, name, per, base)
        self.ctxT = sb("ctxT", [P, 2, Z.C, Z.S], F32R)
        self.q = sb("q", [P, 2, 2, 2, P], F32R)
        self.wo = sb("wo", [P, Z.NP, Z.D])
        self.RING = 3 * Z.NC + 4
        self.RING_BEFORE = 2 * Z.NC
        self.ring_psum = count("ring_psum", self.RING, self.RING_BEFORE)
        self.ring_out = count("ring_out", self.RING, self.RING_BEFORE)
        self.chi_done = count("chi_done", Z.NC, Z.NC)
        self.q_in = [count(f"q_in{i}", 4 * 16 * Z.NP // 2, 0) for i in range(2)]
        self.stage = Stage(ctx, nc, Z)
        self.wo_in = count("wo_in", 0, 0)


VB = 6


def load_ctx(sp, Z, M, ctx_in, b, n, slot, sem):
    sp.dma_start(M.stage[:, slot:slot + 2], ctx_in[b, n * 2 * P:(n + 1) * 2 * P].rearrange("(n p) d -> p n d", p=P)
                 ).then_inc(sem, 16)


def load_q(sp, Z, X, q_s, b, i):
    for half in range(2):
        for h in range(2):
            sp.dma_start(X.q[half * Z.HD:(half + 1) * Z.HD, i % 2, h].bitcast(F32),
                         q_s[:, i, h * Z.HD:(h + 1) * Z.HD, b * P:(b + 1) * P].rearrange("l d t -> d l t")
                         ).then_inc(X.q_in[i % 2].sem, 16)


def split_parts(Z, M, item, raw):
    if item[0] == "wk":
        return raw.rearrange("p (k n) -> p k n", k=Z.C), M.wk[:, item[1] % 2, 0], M.wk[:, item[1] % 2, 1]
    return raw, M.wv[:, 0, item[2]], M.wv[:, 1, item[2]]


def ctx_transpose(nc, Z, M, X, ps, slot, bank):
    for c in range(Z.C):
        mm = nc.tensor.transpose(ps[:, bank, c * P:(c + 1) * P], M.stage[:, slot, c * P:(c + 1) * P], M.ident[:])
    mm.then_inc(X.ring_psum.sem, 1)


def ctx_hi(nc, Z, X, ps, s, n, bank):
    at = (4 * s + n) * P
    nc.scalar.copy(X.ctxT[:, 0, :, at:at + P], ps[:, bank].rearrange("p (c t) -> p c t", c=Z.C)).then_inc(X.chi_done.sem, 1)


def ctx_lo(nc, Z, X, ps, s, n, bank):
    at = (4 * s + n) * P
    nc.vector.tensor_tensor(X.ctxT[:, 1, :, at:at + P], ps[:, bank].rearrange("p (c t) -> p c t", c=Z.C),
                            X.ctxT[:, 0, :, at:at + P].bitcast(F32), ALU.subtract).then_inc(X.ring_out.sem, 1)


def prepare(nc, Z, M, X, x, ctx_in, Wq, bq, Wk, Wv, bo, q_s):
    NB, C, NP, D, HW, NC = Z.NB, Z.C, Z.NP, Z.D, Z.HW, Z.NC
    TOK = NB * P
    SPLITS = [("wk", 0), ("wk", 1)] + [("wv", 0, c) for c in range(C)]
    XB, QB, CB = 0, 2, 4
    QBUFS = 4
    with ExitStack() as ctx:
        sb = lambda name, shape, dt=F32: ctx.enter_context(nc.sbuf_tensor("a_" + name, shape, dt))
        sem = lambda name: ctx.enter_context(nc.semaphore("a_" + name))
        ps = ctx.enter_context(nc.psum_tensor("a_ps", [P, 8, BANK], F32))
        xs = M.x2[:].rearrange("p (b d) -> p b d", b=NB)
        xn = sb("xn", [P, NB, D])
        xnT = sb("xnT", [P, C, TOK])
        wq = sb("wq", [P, C, HW])
        w = sb("w", [P, len(SPLITS), BANK])
        qhi = sb("qhi", [P, QBUFS, TOK], F32R)
        qlo = sb("qlo", [P, QBUFS, TOK], F32R)
        bqT = sb("bqT", [P, NP])
        bo_b = sb("bo_b", [P, D])
        stats, mv = sb("stats", [P, NB, 6]), sb("mv", [P, NB, 2])
        var, std, rstd = sb("var", [P, NB]), sb("std", [P, NB]), sb("rstd", [P, NB])

        id_ready = sem("id_ready")
        x_in, bq_in, bo_in = sem("x_in"), sem("bq_in"), sem("bo_in")
        wq_in = [sem(f"wq_in{c}") for c in range(C)]
        wk_in, wv_in, ctx_sem = sem("wk_in"), sem("wv_in"), [sem("ctx_in0"), sem("ctx_in1")]
        ln = [sem(n) for n in ("stats_done", "mv_done", "var_done", "std_done", "rstd_done", "xn_done")]
        xT_psum, xT_done = sem("xT_psum"), sem("xT_done")
        q_psum, qhi_done, qlo_done = sem("q_psum"), sem("qhi_done"), sem("qlo_done")
        whi_done, wlo_done = sem("whi_done"), sem("wlo_done")
        q_stored, last_stored = [sem(f"q_stored{i}") for i in range(QBUFS)], sem("last_stored")
        block = ctx.enter_context(nc.Block())

        TURNS = [([], [], [0]), ([0], [0], [1]), ([1], [1, 2], [2]), ([2], [3, 4], [3]), ([3], [5, 6], [4]),
                 ([4], [7, 8], [5]), ([5], [9, 10], [6]), ([], [11], [7]), ([], [12, 13, 14, 15], [])]

        def store_q(eng, j, stored):
            eng.wait_ge(qlo_done, j + 1)
            for hl, src in enumerate((qhi, qlo)):
                eng.dma_start(q_s[hl, j], src[:, j % QBUFS].bitcast(F32)).then_inc(stored, 16)

        @block.sync
        def _(sp):
            sp.dma_start(xs, x.rearrange("b t d -> t b d")).then_inc(x_in, 16)
            for c in range(C):
                sp.dma_start(wq[:, c], Wq[c * P:(c + 1) * P]).then_inc(wq_in[c], 16)
            load_ctx(sp, Z, M, ctx_in, 0, 0, 0, ctx_sem[0])
            for j in range(2):
                sp.dma_start(w[:, j].rearrange("p (k n) -> p k n", k=C),
                             Wk[:, j * P:(j + 1) * P].rearrange("(k p) n -> p k n", p=P)).then_inc(wk_in, 16)
            load_ctx(sp, Z, M, ctx_in, 0, 1, 2, ctx_sem[1])
            sp.dma_start(w[:, 2:], Wv[:, :BANK].rearrange("(c p) n -> p c n", p=P)).then_inc(wv_in, 16)
            for n in range(2, NC // 2):
                sp.wait_ge(X.ring_psum.sem, 2 * (n - 1))
                load_ctx(sp, Z, M, ctx_in, 0, n, 2 * (n % 2), ctx_sem[n % 2])
                if n in (5, 6):
                    sp.wait_ge(q_stored[n - 5], 32)
                    load_q(sp, Z, X, q_s, 0, n - 5)
            for j in range(NP - 2, NP):
                store_q(sp, j, last_stored)
            for i in range(QBUFS):
                sp.wait_ge(q_stored[i], 32 * len(range(i, NP - 2, QBUFS)))
            sp.wait_ge(last_stored, 64)

        @block.gpsimd
        def _(pool):
            pool.dma_start(bqT[:], bq.rearrange("(j p) -> p j", p=P), allow_slow_non_contiguous=True).then_inc(bq_in, 16)
            pool.dma_start(bo_b[:], bo.rearrange("(a d) -> a d", a=1).broadcast_to([P, D])).then_inc(bo_in, 16)
            make_identity(nc, pool, M.ident, id_ready)

            pool.wait_ge(bo_in, 16)
            for b in range(NB):
                pool.wait_ge(ln[5], b + 1)
                nc.gpsimd.tensor_tensor(xs[:, b], xs[:, b], bo_b[:], ALU.add)
            for j in range(NP - 2):
                store_q(pool, j, q_stored[j % QBUFS])

        @block.tensor
        def _(pe):
            pe.wait_ge(id_ready, 2)
            for b in range(NB):
                pe.wait_ge(ln[5], b + 1)
                if b >= 2:
                    pe.wait_ge(xT_done, b - 1)
                for c in range(C):
                    mm = nc.tensor.transpose(ps[:, XB + b % 2, c * P:(c + 1) * P], xn[:, b, c * P:(c + 1) * P], M.ident[:])
                mm.then_inc(xT_psum, 1)
            for _, chunks, pairs in TURNS:
                for n in chunks:
                    if n % 2 == 0:
                        pe.wait_ge(ctx_sem[n // 2 % 2], 16 * (n // 4 + 1))
                    if n >= 4:
                        pe.wait_ge(X.ring_out.sem, n - 3)
                    ctx_transpose(nc, Z, M, X, ps, n % 4, CB + n % 4)
                for j in pairs:
                    if j == 0:
                        pe.wait_ge(xT_done, NB)
                        for c in range(C):
                            pe.wait_ge(wq_in[c], 16)
                    if j >= 2:
                        pe.wait_ge(qlo_done, j - 1)
                    for c in range(C):
                        mm = nc.tensor.matmul(ps[:, QB + j % 2, :TOK], wq[:, c, j * P:(j + 1) * P], xnT[:, c, :],
                                              start=c == 0, stop=c == C - 1)
                    mm.then_inc(q_psum, 1)

        @block.scalar
        def _(act):
            act.wait_ge(ln[2], 1)
            nc.scalar.activation(std[:], var[:], ACT.Sqrt).then_inc(ln[3], 1)
            act.wait_ge(bq_in, 16)
            for units, chunks, pairs in TURNS:
                for n in chunks:
                    act.wait_ge(X.ring_psum.sem, n + 1)
                    ctx_hi(nc, Z, X, ps, n // 4, n % 4, CB + n % 4)
                for j in pairs:
                    act.wait_ge(q_psum, j + 1)
                    if j >= QBUFS:
                        act.wait_ge(q_stored[j % QBUFS], 32 * (j // QBUFS))
                    nc.scalar.activation(qhi[:, j % QBUFS], ps[:, QB + j % 2, :TOK], ACT.Identity,
                                         bias=bqT[:, j:j + 1]).then_inc(qhi_done, 1)
                for m in units:
                    act.wait_ge(*(wk_in, 32) if SPLITS[m][0] == "wk" else (wv_in, 16))
                    raw, hi, _ = split_parts(Z, M, SPLITS[m], w[:, m])
                    nc.scalar.copy(hi, raw).then_inc(whi_done, 1)

        @block.vector
        def _(dve):
            layer_norm_stats(nc, dve, xs, lambda b: dve.wait_ge(x_in, 16), stats, mv, ln, NB)
            layer_norm_apply(nc, dve, xs, xn, (mv, var, std, rstd), ln, NB)
            for b in range(NB):
                dve.wait_ge(xT_psum, b + 1)
                nc.vector.tensor_copy(xnT[:, :, b * P:(b + 1) * P],
                                      ps[:, XB + b % 2].rearrange("p (c t) -> p c t", c=C)).then_inc(xT_done, 1)
            dve.wait_ge(bq_in, 16)
            for units, chunks, pairs in TURNS:
                for n in chunks:
                    dve.wait_ge(X.chi_done.sem, n + 1)
                    ctx_lo(nc, Z, X, ps, n // 4, n % 4, CB + n % 4)
                for j in pairs:
                    dve.wait_ge(qhi_done, j + 1)
                    nc.vector.scalar_tensor_tensor(qlo[:, j % QBUFS], ps[:, QB + j % 2, :TOK], bqT[:, j:j + 1],
                                                   qhi[:, j % QBUFS].bitcast(F32), ALU.add, ALU.subtract).then_inc(qlo_done, 1)
                for m in units:
                    dve.wait_ge(whi_done, m + 1)
                    raw, hi, lo = split_parts(Z, M, SPLITS[m], w[:, m])
                    nc.vector.tensor_tensor(lo, raw, hi.bitcast(F32), ALU.subtract).then_inc(wlo_done, 1)


def layer_norm_stats(nc, dve, xs, ready, stats, mv, sems, NB):
    stats_done, mv_done = sems[:2]
    for b in range(NB):
        ready(b)
        nc.vector.bn_stats(stats[:, b], xs[:, b]).then_inc(stats_done, 1)
    for b in range(NB):
        dve.wait_ge(stats_done, b + 1)
        nc.vector.bn_aggr(mv[:, b], stats[:, b]).then_inc(mv_done, 1)


def layer_norm_apply(nc, dve, xs, xn, tiles, sems, NB):
    mv, var, std, rstd = tiles
    _, mv_done, var_done, std_done, rstd_done, xn_done = sems
    dve.wait_ge(mv_done, NB)
    nc.vector.tensor_scalar(var[:], mv[:, :, 1], EPS, None, ALU.add).then_inc(var_done, 1)
    dve.wait_ge(std_done, 1)
    nc.vector.reciprocal(rstd[:], std[:]).then_inc(rstd_done, 1)
    dve.wait_ge(rstd_done, 1)
    for b in range(NB):
        nc.vector.tensor_scalar(xn[:, b], xs[:, b], mv[:, b, 0:1], rstd[:, b:b + 1],
                                ALU.subtract, ALU.mult).then_inc(xn_done, 1)


def cross_attention(nc, Z, M, X, ctx_in, Wk, bk, Wv, bv, Wo, q_s, late_loads):
    NB, C, NP, S, SB, NC, D, HD, HALF = Z.NB, Z.C, Z.NP, Z.S, Z.SB, Z.NC, Z.D, Z.HD, Z.HALF
    SCALE = HD ** -0.5
    STEPS = NP * SB
    LAG_SCORE, LAG_EXP, LAG_WEIGH = 1, 5, 6
    LAST = STEPS + LAG_WEIGH
    ROUNDS = 2 * SB
    KB, QB, TB, OB = 0, 2, 3, 5

    FIRST = LAST + 1 - STEPS
    v = lambda half, first, last: [("v", half, c) for c in range(first, last)]
    chunks = lambda first, last: [("ctx", n // 4, n % 4) for n in range(first, last)]
    issued = {t: [] for t in range(FIRST, LAST + 1)}
    for c in range(0, NC, 4):
        issued[HALF * SB + 3 + c // 4] = v(1, c, c + 4)
    issued[HALF * SB + 8] = [("wo", 0, 4)]
    issued[STEPS - 3] = chunks(0, 2)
    issued[STEPS - 2] = chunks(2, 6)
    issued[STEPS - 1] = chunks(6, 8) + [("wo", 4, 6)] + chunks(8, 10)
    issued[STEPS + 1] = chunks(10, 12)
    issued[STEPS + 2] = chunks(12, 16) + v(0, 0, 3)
    issued[STEPS + 3] = [("wo", 6, 7)] + v(0, 3, 6)
    issued[STEPS + 4] = v(0, 6, 9)
    issued[STEPS + 5] = v(0, 9, 12)
    issued[STEPS + 6] = v(0, 12, 14) + [("wo", 7, 8)]
    issued[FIRST] = v(0, 14, 16)
    RING = X.RING
    of_next = lambda item, t: t >= FIRST and (item[0] == "ctx" or (item[0] == "v" and item[1] == 0 and t >= STEPS))
    ring_at, last_at, skipped = {}, {}, 0
    for at, (t, item) in enumerate((t, item) for t in issued for item in issued[t]):
        ring_at[item] = at - (RING if item[0] == "v" and of_next(item, t) else 0)
        last_at[item] = ring_at[item] if item[0] == "v" else at - skipped
        skipped += of_next(item, t)
    assert len(ring_at) == RING and RING % 2 == 0
    assert X.RING_BEFORE == NC + sum(item[0] != "ctx" for t in range(STEPS, LAST + 1) for item in issued[t])
    ctx_index = lambda s, n: ring_at[("ctx", s, n)]

    def ring_items(b, t, more):
        if t < FIRST:
            return [((b, 0) if item[0] == "v" else None, item, ring_at[item] - (RING if item[0] == "wo" else 0))
                    for item in issued.get(t + STEPS, []) if item[0] != "ctx"]
        return [((b, int(item[0] == "v" and of_next(item, t))), item, (ring_at if more else last_at)[item])
                for item in issued[t] if more or not of_next(item, t)]

    def parted(t, items):
        n = 2 if t in (STEPS - 2, STEPS - 1, STEPS + 2) and items and items[0][1][0] == "ctx" else 0
        return items[:n], items[n:]

    T = X.stage
    splits = {t: [] for t in range(FIRST, LAST + 1)}
    splits[FIRST].append(("wk", 2))
    for i in range(3, NP):
        splits[SB * (i - 1) + 1].append(("wk", i))
    for c in range(C):
        splits[2 * SB + 1 + c].append(("wv", 1, c))
    splits[STEPS - 6] += [("wv", 0, 0), ("wv", 0, 1)]
    splits[STEPS - 5] += [("wv", 0, 2)]
    splits[STEPS - 4] += [("wk", 0)]
    splits[STEPS] += [("wv", 0, 3), ("wk", 1)]
    assert [x for t in splits for x in splits[t]] == list(T.split_at)

    def step_splits(t, more):
        return [item for item in splits.get(t, []) if more or not T.early(item)]

    def own(b, n):
        return ((b, 0), n) if n < STEPS else ((b, 1), n - STEPS)

    def exists(n, more):
        return 0 <= n and (n < STEPS or more)

    def run(eng, step):
        for t in range(FIRST):
            step(0, t, True)
        with eng.Fori(0, NB - 1) as b:
            for t in range(FIRST, LAST + 1):
                step(b, t, True)
        for t in range(FIRST, LAST + 1):
            step(NB - 1, t, False)

    with ExitStack() as ctx:
        sb = lambda name, shape, dt=F32: ctx.enter_context(nc.sbuf_tensor("b_" + name, shape, dt))
        ps = ctx.enter_context(nc.psum_tensor("b_ps", [P, 8, BANK], F32))
        ctxT, wk, wv, q, wo, ident = X.ctxT, M.wk, M.wv, X.q, X.wo, M.ident
        V = sb("V", [P, NC, BANK])
        kst = sb("kst", [P, 2, 2, BANK], F32R)
        prob = sb("prob", [P, 2, 2, S])
        pT = sb("pT", [P, 2, 4, P])
        attnT = sb("attnT", [P, NP, P])
        bkT = sb("bkT", [P, NP])
        bvT = sb("bvT", [P, NP])
        mx = sb("mx", [P, 2, 2, SB])
        mt = sb("mt", [P, 2])
        negm = sb("negm", [P, 2, 2])
        sums = sb("sums", [P, 2, 2, SB])
        total = sb("total", [P, 2])
        rinv = sb("rinv", [P, 2, 2])
        rb = sb("rb", [P, P])
        scaled = sb("scaled", [P, P])

        sem = lambda name, per: Count(ctx, nc, "b_" + name, per)

        k_psum = sem("k_psum", STEPS)
        qk_psum = sem("qk_psum", 2 * STEPS)
        t_psum = sem("t_psum", NP * ROUNDS)
        pv_done = sem("pv_done", NP * ROUNDS)
        r_psum = sem("r_psum", NP)
        khi_done = sem("khi_done", 2 * STEPS)
        exp_done = sem("exp_done", 2 * STEPS)
        te_done = sem("te_done", NP * ROUNDS // 2)
        klo_done = sem("klo_done", 2 * STEPS)
        qk_out = sem("qk_out", 2 * STEPS)
        mt_done = sem("mt_done", NP)
        negm_done = sem("negm_done", NP)
        to_done = sem("to_done", NP * ROUNDS // 2)
        total_done = sem("total_done", NP)
        rinv_done = sem("rinv_done", NP)
        rb_done = sem("rb_done", NP)
        o_free = sem("o_free", NP)
        attn_done = sem("attn_done", NP)
        stats_done = sem("stats_done", 1)
        bias_in = ctx.enter_context(nc.semaphore("b_bias_in"))

        ring_psum, ring_out, chi_done = X.ring_psum, X.ring_out, X.chi_done

        def start(eng, *counts):
            for s in counts:
                eng.sem_inc(s.sem, 1)

        block = ctx.enter_context(nc.Block())

        @block.sync
        def _(sp):
            sp.dma_start(bkT[:], bk.rearrange("(j p) -> p j", p=P), allow_slow_non_contiguous=True).then_inc(bias_in, 16)
            sp.dma_start(bvT[:], bv.rearrange("(j p) -> p j", p=P), allow_slow_non_contiguous=True).then_inc(bias_in, 16)
            sp.dma_start(wo[:], Wo.rearrange("(j p) n -> p j n", p=P)).then_inc(X.wo_in.sem, 16)
            def free_slots(batch, item):
                at, width = T.pos[item], 2 if item[0] == "ctx" else 1
                for p in range(at - STAGE_SLOTS, at - STAGE_SLOTS + width):
                    old, ago = T.owner[p], 1 if p < 0 else 0
                    if old[0] == "ctx":
                        reach(sp, ring_psum, batch, ctx_index(old[1] // 2, old[1] % 2 * 2 + 1) + 1 - ago * RING)
                    else:
                        reach(sp, T.lo_done, batch, T.split_at[old] + 1 - ago * T.SPLITS)

            def load_stage(b, item):
                free_slots((b, 0), item)
                slot = T.slot(item)
                if item[0] == "ctx":
                    load_ctx(sp, Z, M, ctx_in, b + 1, item[1], slot, T.filled[slot].sem)
                elif item[0] == "wk":
                    src = Wk[:, item[1] * P:(item[1] + 1) * P].rearrange("(k p) n -> p k n", p=P)
                    sp.dma_start(M.stage[:, slot].rearrange("p (k n) -> p k n", k=C), src).then_inc(T.filled[slot].sem, 16)
                else:
                    _, g, c = item
                    sp.dma_start(M.stage[:, slot], Wv[c * P:(c + 1) * P, g * BANK:(g + 1) * BANK]
                                 ).then_inc(T.filled[slot].sem, 16)

            q_after = {("wv", 1, 1): 2, ("wv", 1, 2): 3, ("wk", 5): 4, ("wk", 7): 5, ("wv", 0, 1): 6, ("wv", 0, 2): 7,
                       ("ctx", 1): NP, ("ctx", 5): NP + 1}
            for b in range(NB):
                more = b < NB - 1
                for item in T.items:
                    if more or not T.early(item):
                        load_stage(b, item)
                    i = q_after.get(item)
                    if i is not None and (more or i < NP):
                        reach(sp, qk_psum, (b, 0), 2 * SB * (i - 1))
                        load_q(sp, Z, X, q_s, b + i // NP, i % NP)
            reach(sp, ring_psum, (NB - 1, 0), ring_at["v", 1, NC - 1] + 1)
            late_loads(sp, 0)
            reach(sp, T.lo_done, (NB - 1, 0), T.split_at["wk", NP - 1] + 1)
            late_loads(sp, 2)
            reach(sp, k_psum, (NB - 1, 0), STEPS)
            late_loads(sp, 1)

        @block.tensor
        def _(pe):
            def v_chunk(c, bank):
                pairs = [(0, 0), (0, 1), (1, 0)]
                for m, (a, w) in enumerate(pairs):
                    for k in range(C):
                        mm = nc.tensor.matmul(ps[:, bank], ctxT[:, a, k, c * P:(c + 1) * P], wv[:, w, k],
                                              start=m == 0 and k == 0, stop=m == 2 and k == C - 1)
                mm.then_inc(ring_psum.sem, 1)

            def project(t, first, last):
                i, s = divmod(t, SB)
                terms = [(a, w, k) for a, w in ((0, 0), (1, 0), (0, 1)) for k in range(C)]
                for m in range(first, last):
                    a, w, k = terms[m]
                    mm = nc.tensor.matmul(ps[:, KB + t % 2], wk[:, i % 2, w, k], ctxT[:, a, k, s * BANK:(s + 1) * BANK],
                                          start=m == 0, stop=m == len(terms) - 1)
                if last == len(terms):
                    mm.then_inc(k_psum.sem, 1)

            def score(b, t, h):
                i = t // SB
                if t % SB == 0 and h == 0:
                    reach(pe, X.q_in[i % 2], b, 64 * (i // 2 + 1))
                reach(pe, klo_done, b, 2 * t + h + 1)
                reach(pe, qk_out, b, 2 * t + h)
                for l in range(2):
                    mm = nc.tensor.matmul(ps[:, QB], q[:, i % 2, h, l], kst[:, t % 2, h], start=l == 0, stop=l == 1)
                mm.then_inc(qk_psum.sem, 1)

            def transpose_round(b, i, r):
                n = i * ROUNDS + r
                reach(pe, exp_done, b, 2 * (i * SB + r // 2) + 2)
                reach(pe, (te_done, to_done)[r % 2], b, n // 2)
                for m in range(4):
                    c, h = 2 * r + m // 2, m % 2
                    mm = nc.tensor.transpose(ps[:, TB + r % 2, m * P:(m + 1) * P],
                                             prob[:, i % 2, h, c * P:(c + 1) * P], ident[:])
                mm.then_inc(t_psum.sem, 1)

            def weigh_round(b, i, r):
                n = i * ROUNDS + r
                if r == 0:
                    reach(pe, o_free, b, i)
                reach(pe, (te_done, to_done)[r % 2], b, n // 2 + 1)
                reach(pe, ring_out, b, ring_at["v", i // HALF, 2 * r + 1] + 1)
                for m in range(4):
                    c, h = 2 * r + m // 2, m % 2
                    col = (i % HALF * 2 + h) * HD
                    mm = nc.tensor.matmul(ps[h * HD:(h + 1) * HD, OB, 0:P], V[:, c, col:col + HD], pT[:, r % 2, m],
                                          start=c == 0, stop=c == NC - 1)
                mm.then_inc(pv_done.sem, 1)

            def spread_rinv(b, i):
                reach(pe, rinv_done, b, i + 1)
                reach(pe, pv_done, b, (i + 1) * ROUNDS)
                for h in range(2):
                    mm = nc.tensor.matmul(ps[h * HD:(h + 1) * HD, OB, P:2 * P],
                                          rinv[:, i % 2, h:h + 1].broadcast_to([P, HD]), ident[:], start=True, stop=True)
                mm.then_inc(r_psum.sem, 1)

            def ring_item(b, item, at):
                if b is None:
                    reach(pe, ring_psum, (0, 0), at)
                    pe.sem_inc(ring_psum.sem, 1)
                    return
                kind, g, n = item
                bank = VB + at % 2
                reach(pe, ring_out, b, at - 1)
                if kind == "v":
                    if n == 0:
                        reach(pe, T.lo_done, b, T.split_count(("wv", g, C - 1)))
                    if g == 0 and n % 4 == 0:
                        reach(pe, ring_out, b, ctx_index(n // 4, 3) + 1 - RING)
                    v_chunk(n, bank)
                elif kind == "ctx":
                    half = ("ctx", 2 * g + n // 2)
                    if n % 2 == 0:
                        reach(pe, T.filled[T.slot(half)], b, T.count[half])
                    ctx_transpose(nc, Z, M, X, ps, T.slot(half) + n % 2, bank)
                else:
                    pe.wait_ge(X.wo_in.sem, 16)
                    reach(pe, attn_done, b, n)
                    for i in range(g, n):
                        mm = nc.tensor.matmul(ps[:, bank], attnT[:, i], wo[:, i], start=i == g, stop=i == n - 1)
                    mm.then_inc(ring_psum.sem, 1)

            start(pe, k_psum, qk_psum, t_psum, pv_done, r_psum)
            def step(b, t, more):
                w, e = t - LAG_WEIGH, t - LAG_SCORE
                ahead = not more and t > STEPS
                if exists(w, more):
                    batch, n = own(b, w)
                    if not ahead:
                        transpose_round(batch, n // SB, n % SB * 2)
                        transpose_round(batch, n // SB, n % SB * 2 + 1)
                begin, items = parted(t, ring_items(b, t, more))
                for item in begin:
                    ring_item(*item)
                if exists(t, more):
                    batch, n = own(b, t)
                    if n < SB:
                        reach(pe, ring_out, batch, ctx_index(n, 3) + 1 - RING)
                    if n % SB == 0:
                        reach(pe, T.lo_done, batch, T.split_count(("wk", n // SB)))
                    reach(pe, klo_done, batch, 2 * (n - 1))
                    project(n, 0, 6)
                if exists(e, more):
                    score(*own(b, e), 0)
                if exists(t, more):
                    project(n, 6, 3 * C)
                if exists(e, more):
                    score(*own(b, e), 1)
                if exists(w, more):
                    batch, n = own(b, w)
                    for half in range(2):
                        weigh_round(batch, n // SB, n % SB * 2 + half)
                        if not more and t >= STEPS:
                            if n + 1 < STEPS:
                                transpose_round(batch, (n + 1) // SB, (n + 1) % SB * 2 + half)
                            for item in items[:(len(items) + 1) // 2]:
                                ring_item(*item)
                            items = items[(len(items) + 1) // 2:]
                    if n % SB == SB - 1:
                        spread_rinv(batch, n // SB)
                for item in items:
                    ring_item(*item)

            run(pe, step)

        @block.scalar
        def _(act):
            def split_hi(b, item):
                slot = T.slot(item)
                reach(act, T.filled[slot], b, T.count[item])
                if item[0] == "wk":
                    reach(act, k_psum, b, SB * (item[1] - 1 if item[1] >= 2 else NP - 1 + item[1]))
                else:
                    reach(act, ring_psum, b, ring_at["v", 1 - item[1], NC - 1] + 1)
                raw, hi, _ = split_parts(Z, M, item, M.stage[:, slot])
                nc.scalar.copy(hi, raw).then_inc(T.hi_done.sem, 1)

            def chunks_hi(items):
                for batch, (kind, g, n), at in items:
                    if kind == "ctx":
                        reach(act, ring_psum, batch, at + 1)
                        ctx_hi(nc, Z, X, ps, g, n, VB + at % 2)

            start(act, khi_done, exp_done, te_done, T.hi_done)
            act.wait_ge(bias_in, 32)
            def step(b, t, more):
                w = t - LAG_WEIGH
                if exists(w, more):
                    batch, m = own(b, w)
                    n = 2 * m
                    reach(act, t_psum, batch, n + 1)
                    reach(act, pv_done, batch, n - 1)
                    nc.scalar.copy(pT[:, 0], ps[:, TB].rearrange("p (m t) -> p m t", m=4)).then_inc(te_done.sem, 1)
                begin, rest = parted(t, ring_items(b, t, more))
                chunks_hi(begin)
                e = t - LAG_EXP
                if exists(e, more):
                    batch, m = own(b, e)
                    i, s = divmod(m, SB)
                    if s == 0:
                        reach(act, negm_done, batch, i + 1)
                        reach(act, rinv_done, batch, i - 1)
                    for h in range(2):
                        p = prob[:, i % 2, h, s * BANK:(s + 1) * BANK]
                        nc.scalar.activation(p, p, ACT.Exp, bias=negm[:, i % 2, h:h + 1], scale=SCALE,
                                             accum_out=sums[:, i % 2, h, s:s + 1]).then_inc(exp_done.sem, 1)
                if exists(t, more):
                    batch, m = own(b, t)
                    reach(act, k_psum, batch, m + 1)
                    reach(act, qk_psum, batch, 2 * (m - 1))
                    for h in range(2):
                        rows = slice(h * HD, (h + 1) * HD)
                        nc.scalar.activation(kst[rows, m % 2, h], ps[rows, KB + m % 2], ACT.Identity,
                                             bias=bkT[rows, m // SB:m // SB + 1]).then_inc(khi_done.sem, 1)
                chunks_hi(rest)
                for item in step_splits(t, more):
                    split_hi((b, 0), item)

            run(act, step)

        @block.vector
        def _(dve):
            start(dve, klo_done, qk_out, mt_done, negm_done, to_done, total_done, rinv_done, rb_done, o_free, attn_done,
                  stats_done, T.lo_done)
            dve.wait_ge(bias_in, 32)
            def ring_out_items(b, items):
                for batch, (kind, g, n), at in items:
                    if batch is None:
                        reach(dve, ring_out, (0, 0), at)
                        dve.sem_inc(ring_out.sem, 1)
                        continue
                    bank = VB + at % 2
                    if kind == "ctx":
                        reach(dve, chi_done, batch, 4 * g + n + 1)
                        ctx_lo(nc, Z, X, ps, g, n, bank)
                        continue
                    reach(dve, ring_psum, batch, at + 1)
                    if kind == "v":
                        reach(dve, pv_done, batch, (HALF * g - 1) * ROUNDS + n // 2 + 1)
                        nc.vector.tensor_copy(V[:, n], ps[:, bank]).then_inc(ring_out.sem, 1)
                    else:
                        reach(dve, ring_out, batch, at)
                        rows = M.x2[:, bass.ds(b * D, D)]
                        nc.vector.tensor_tensor(rows, ps[:, bank], rows, ALU.add).then_inc(ring_out.sem, 1)
                        if n == NP:
                            reach(dve, ring_out, batch, at + 1)
                            nc.vector.bn_stats(M.stats[:, bass.ds(b * 6, 6)], rows).then_inc(stats_done.sem, 1)

            def step(b, t, more):
                w = t - LAG_WEIGH
                if w >= SB and w % SB == 0:
                    i, batch = w // SB - 1, (b, 0)
                    reach(dve, r_psum, batch, i + 1)
                    if i == 0:
                        reach(dve, ring_psum, batch, 0)
                    nc.vector.tensor_copy(rb[:], ps[:, OB, P:2 * P]).then_inc(rb_done.sem, 1)
                    reach(dve, rb_done, batch, i + 1)
                    reach(dve, attn_done, batch, i)
                    nc.vector.tensor_tensor(scaled[:], ps[:, OB, 0:P], rb[:], ALU.mult).then_inc(o_free.sem, 1)
                    reach(dve, o_free, batch, i + 1)
                    nc.vector.tensor_scalar(attnT[:, i], scaled[:], bvT[:, i:i + 1], None, ALU.add).then_inc(attn_done.sem, 1)
                if exists(w, more):
                    batch, m = own(b, w)
                    n = 2 * m + 1
                    reach(dve, t_psum, batch, n + 1)
                    reach(dve, pv_done, batch, n - 1)
                    nc.vector.tensor_copy(pT[:, 1], ps[:, TB + 1].rearrange("p (m t) -> p m t", m=4)).then_inc(to_done.sem, 1)
                if exists(w, more) and w % SB == SB - 1:
                    i = m // SB
                    reach(dve, exp_done, batch, 2 * SB * (i + 1))
                    nc.vector.tensor_reduce(total[:], sums[:, i % 2], AX.X, ALU.add).then_inc(total_done.sem, 1)
                    reach(dve, total_done, batch, i + 1)
                    reach(dve, r_psum, batch, i - 1)
                    nc.vector.reciprocal(rinv[:, i % 2], total[:]).then_inc(rinv_done.sem, 1)
                    reach(dve, rinv_done, batch, i + 1)
                begin, rest = parted(t, ring_items(b, t, more))
                ring_out_items(b, begin)
                e = t - LAG_SCORE
                if exists(e, more):
                    batch, e = own(b, e)
                    i, s = divmod(e, SB)
                    for h in range(2):
                        reach(dve, qk_psum, batch, 2 * e + h + 1)
                        reach(dve, t_psum, batch, ROUNDS * (i - 2) + 2 * (s + 1))
                        if s == 0:
                            reach(dve, negm_done, batch, i - 1)
                        nc.vector.tensor_scalar(prob[:, i % 2, h, s * BANK:(s + 1) * BANK], ps[:, QB], 1.0, None,
                                                ALU.mult, ALU.max, accum_out=mx[:, i % 2, h, s:s + 1]).then_inc(qk_out.sem, 1)
                    if s == SB - 1:
                        reach(dve, qk_out, batch, 2 * (e + 1))
                        nc.vector.tensor_reduce(mt[:], mx[:, i % 2], AX.X, ALU.max).then_inc(mt_done.sem, 1)
                        reach(dve, mt_done, batch, i + 1)
                        nc.vector.tensor_scalar(negm[:, i % 2], mt[:], -SCALE, None, ALU.mult).then_inc(negm_done.sem, 1)
                        reach(dve, negm_done, batch, i + 1)
                if exists(t, more):
                    batch, m = own(b, t)
                    for h in range(2):
                        rows, other = slice(h * HD, (h + 1) * HD), slice((1 - h) * HD, (2 - h) * HD)
                        reach(dve, khi_done, batch, 2 * m + h + 1)
                        nc.vector.scalar_tensor_tensor(kst[other, m % 2, h], ps[rows, KB + m % 2],
                                                       bkT[rows, m // SB:m // SB + 1], kst[rows, m % 2, h].bitcast(F32),
                                                       ALU.add, ALU.subtract).then_inc(klo_done.sem, 1)
                ring_out_items(b, rest)
                for item in step_splits(t, more):
                    reach(dve, T.hi_done, (b, 0), T.split_at[item] + 1)
                    raw, hi, lo = split_parts(Z, M, item, M.stage[:, T.slot(item)])
                    nc.vector.tensor_tensor(lo, raw, hi.bitcast(F32), ALU.subtract).then_inc(T.lo_done.sem, 1)

            run(dve, step)


SELF_HD = 32


def load_rows(sp, Z, M, qkv_w, fc_w, part):
    G = P // SELF_HD
    for t in ((0, 1), (2,), ())[part]:
        for r in range(G):
            sp.dma_start(M.w_rows[r * SELF_HD:(r + 1) * SELF_HD, t * G:(t + 1) * G],
                         qkv_w.rearrange("(g r t d) c -> r t d g c", g=G, r=G, t=3)[r, t]).then_inc(M.rows_in[part], 16)
    if part == 2:
        sp.dma_start(M.w_rows[:, 3 * G:], fc_w.rearrange("(m p) c -> p m c", p=P)).then_inc(M.rows_in[part], 16)


def load_tile(sp, Z, M, projections, m):
    t, eg = divmod(m, 4)
    for i in range(4):
        if t < 3:
            dst = M.w_tiles[:, m % 4, i].rearrange("p (e h) -> p e h", e=4)
            src = projections[t][eg * 4:(eg + 1) * 4, i * P:(i + 1) * P].rearrange("e p h -> p e h")
        else:
            dst, src = M.w_tiles[:, m % 4, i], projections[t][eg * 4 + i]
        sp.dma_start(dst, src).then_inc(M.tile_in[m % 4], 16)


def self_attention(nc, Z, M, head_mask, qkv_b, fc_b, gates, projections):
    NB, C, D = Z.NB, Z.C, Z.D
    H, HD = 16, SELF_HD
    G = P // HD
    TILES = 4 * G
    ORDER = [t * G + g for g in range(G) for t in range(2)] + list(range(2 * G, TILES))
    TOK = NB * P
    U = NB * G
    LAG = 4
    BUFS = 6
    WB, XB, LB, PB, AB, VB, FB = 0, 4, 0, 2, 4, 6, 7
    with ExitStack() as ctx:
        sb = lambda name, shape, dt=F32: ctx.enter_context(nc.sbuf_tensor("c_" + name, shape, dt))
        sem = lambda name: ctx.enter_context(nc.semaphore("c_" + name))
        ps = ctx.enter_context(nc.psum_tensor("c_ps", [P, 8, BANK], F32))
        x2 = M.x2[:].rearrange("p (b d) -> p b d", b=NB)
        ident = M.ident
        whi, wlo = sb("whi", [P, C, 4 * D], F32R), sb("wlo", [P, C, 4 * D], F32R)
        fb_b = sb("fb_b", [P, D])
        bv_b = sb("bv_b", [P, H, HD])
        hm_b = sb("hm_b", [P, H])
        bqk = sb("bqk", [P, 2, G])
        hmT = sb("hmT", [P, 2, G])
        xn = sb("xn", [P, NB, D])
        xhi, xlo = sb("xhi", [P, C, TOK], F32R), sb("xlo", [P, C, TOK], F32R)
        qkT = sb("qkT", [P, 2, G, TOK])
        v = sb("v", [P, NB, H, HD])
        vb = sb("vb", [P, 2, H, HD])
        prob = sb("prob", [P, BUFS, G, P])
        negm = sb("negm", [P, U, G])
        sums = sb("sums", [P, U, G])
        rinv = sb("rinv", [P, U, G])
        pT = sb("pT", [P, 2 * G, G, P])
        aohi, aolo = sb("aohi", [P, 2, C, P], F32R), sb("aolo", [P, 2, C, P], F32R)
        stats, mv = M.stats[:].rearrange("p (b s) -> p b s", b=NB), M.mv[:].rearrange("p (b s) -> p b s", b=NB)
        var, std, rstd = sb("var", [P, NB]), sb("std", [P, NB]), sb("rstd", [P, NB])

        small_in, rows_small_in = sem("small_in"), sem("rows_small_in")
        ln = [sem(n) for n in LN_STEPS]
        wt_psum, whi_done, wlo_done = sem("wt_psum"), sem("whi_done"), sem("wlo_done")
        xT_psum, xhi_done, xlo_done = sem("xT_psum"), sem("xhi_done"), sem("xlo_done")
        hm_done, qk_psum, qk_done = sem("hm_done"), sem("qk_psum"), sem("qk_done")
        egate_done, gate_done = sem("egate_done"), sem("gate_done")
        v_psum, vb_done, v_done = sem("v_psum"), sem("vb_done"), sem("v_done")
        l_psum, max_done, exp_done = sem("l_psum"), sem("max_done"), sem("exp_done")
        rinv_done, norm_done = sem("rinv_done"), sem("norm_done")
        t_psum, t_done, pv_psum = sem("t_psum"), sem("t_done"), sem("pv_psum")
        aohi_done, aolo_done = sem("aohi_done"), sem("aolo_done")
        fc_psum, x1b_done, x2_done = sem("fc_psum"), sem("x1b_done"), sem("x2_done")
        block = ctx.enter_context(nc.Block())
        SMALL = 16 * 4

        @block.sync
        def _(sp):
            for r in range(G):
                rows = slice(r * HD, (r + 1) * HD)
                for t in range(2):
                    sp.dma_start(bqk[rows, t], qkv_b.rearrange("(g r t d) -> r t d g", g=G, r=G, t=3)[r, t],
                                   allow_slow_non_contiguous=True).then_inc(rows_small_in, 16)
                sp.dma_start(hmT[rows, 1], head_mask.rearrange("(g r) -> r g", g=G)[r:r + 1].broadcast_to([HD, G]),
                               allow_slow_non_contiguous=True).then_inc(rows_small_in, 16)
            for m, rows in enumerate((2 * G, 2 * G, 3 * G, 4 * G)):
                sp.wait_ge(wt_psum, rows)
                load_tile(sp, Z, M, projections, m)

        @block.gpsimd
        def _(pool):
            pool.dma_start(fb_b[:], fc_b.rearrange("(a d) -> a d", a=1).broadcast_to([P, D])).then_inc(small_in, 16)
            pool.dma_start(hm_b[:], head_mask.rearrange("(a d) -> a d", a=1).broadcast_to([P, H])).then_inc(small_in, 16)
            bias = qkv_b.rearrange("(a h t d) -> a h t d", a=1, t=3, d=HD)
            pool.dma_start(bv_b[:], bias[:, :, 2].broadcast_to([P, H, HD])).then_inc(small_in, 16)
            pool.dma_start(M.gate[:, 0], gates.rearrange("(a e) -> a e", a=1).broadcast_to([P, Z.E])).then_inc(small_in, 16)
            pool.wait_ge(small_in, SMALL)
            for b in range(NB):
                pool.wait_ge(ln[5], b + 1)
                nc.gpsimd.tensor_tensor(x2[:, b], x2[:, b], fb_b[:], ALU.add).then_inc(x1b_done, 1)
            for u in range(U):
                pool.wait_ge(rinv_done, u + 1)
                p = prob[:, u % BUFS]
                nc.gpsimd.tensor_tensor(p, p, rinv[:, u, :, None].broadcast_to([P, G, P]), ALU.mult).then_inc(norm_done, 1)

        @block.tensor
        def _(pe):
            def weight_tile(m):
                if m in (0, 2 * G, 3 * G):
                    part = max(m // G - 1, 0)
                    pe.wait_ge(M.rows_in[part], (16 * 2 * G, 16 * G, 16)[part])
                if m >= 4:
                    pe.wait_ge(wlo_done, m - 3)
                for c in range(C):
                    mm = nc.tensor.transpose(ps[:, WB + m % 4, c * P:(c + 1) * P],
                                             M.w_rows[:, ORDER[m], c * P:(c + 1) * P], ident[:])
                mm.then_inc(wt_psum, 1)

            def passes(out, a, w):
                terms = [(i, j, c) for i, j in ((0, 0), (0, 1), (1, 0)) for c in range(C)]
                for n, (i, j, c) in enumerate(terms):
                    mm = nc.tensor.matmul(out, a(i, c), w(j, c), start=n == 0, stop=n == len(terms) - 1)
                return mm

            W, XT = (whi, wlo), (xhi, xlo)

            def project_qk(j):
                g, t = divmod(j, 2)
                pe.wait_ge(wlo_done, j + 1)
                if j >= 2:
                    pe.wait_ge(qk_done, j - 1)
                tile = (t * G + g) * P
                passes(ps[:, XB + j % 2], lambda i, c: W[i][:, c, tile:tile + P], lambda i, c: XT[i][:, c]
                       ).then_inc(qk_psum, 1)

            def project_v(b):
                pe.wait_ge(wlo_done, 3 * G)
                if b >= 2:
                    pe.wait_ge(vb_done, b - 1)
                passes(ps[:, VB + b % 2], lambda i, c: XT[i][:, c, b * P:(b + 1) * P],
                       lambda i, c: W[i][:, c, 2 * D:3 * D]).then_inc(v_psum, 1)

            def logits(u):
                b, r = divmod(u, G)
                rows = slice(r * HD, (r + 1) * HD)
                if u == 0:
                    pe.wait_ge(qk_done, 2 * G)
                    pe.wait_ge(wlo_done, TILES)
                if u >= 2:
                    pe.wait_ge(exp_done, u - 1)
                for g in range(G):
                    mm = nc.tensor.matmul(ps[:, LB + u % 2, g * P:(g + 1) * P], qkT[rows, 0, g, b * P:(b + 1) * P],
                                          qkT[rows, 1, g, b * P:(b + 1) * P], start=True, stop=True)
                mm.then_inc(l_psum, 1)

            def transpose_probs(u):
                pe.wait_ge(norm_done, u + 1)
                if u >= 2:
                    pe.wait_ge(t_done, u - 1)
                for g in range(G):
                    mm = nc.tensor.transpose(ps[:, PB + u % 2, g * P:(g + 1) * P], prob[:, u % BUFS, g], ident[:])
                mm.then_inc(t_psum, 1)

            def weigh(b):
                pe.wait_ge(t_done, G * (b + 1))
                pe.wait_ge(v_done, b + 1)
                if b >= 2:
                    pe.wait_ge(aolo_done, b - 1)
                for g in range(G):
                    for r in range(G):
                        mm = nc.tensor.matmul(ps[r * HD:(r + 1) * HD, AB + b % 2, g * P:(g + 1) * P], v[:, b, G * g + r],
                                              pT[:, (b * G + r) % (2 * G), g], start=True, stop=True)
                mm.then_inc(pv_psum, 1)

            def out_product(b):
                pe.wait_ge(aolo_done, b + 1)
                pe.wait_ge(*(x2_done, b) if b >= 1 else (vb_done, NB))
                A = (aohi, aolo)
                passes(ps[:, FB], lambda i, c: A[i][:, b % 2, c], lambda i, c: W[i][:, c, 3 * D:]).then_inc(fc_psum, 1)

            for m in range(4):
                weight_tile(m)
            for b in range(NB):
                pe.wait_ge(ln[5], b + 1)
                if b >= 2:
                    pe.wait_ge(xlo_done, b - 1)
                for c in range(C):
                    mm = nc.tensor.transpose(ps[:, XB + b % 2, c * P:(c + 1) * P], xn[:, b, c * P:(c + 1) * P], ident[:])
                mm.then_inc(xT_psum, 1)
            for m in range(4, 2 * G):
                weight_tile(m)
            pe.wait_ge(xlo_done, NB)
            for j in range(2 * G):
                project_qk(j)
                weight_tile(2 * G + j)
            for s in range(U + LAG + 2):
                if s < U:
                    logits(s)
                if s < NB:
                    project_v(s)
                if 0 <= s - LAG < U:
                    transpose_probs(s - LAG)
                if 0 <= s - LAG - 1 < U and (s - LAG - 1) % G == G - 1:
                    weigh((s - LAG - 1) // G)
                b, at = divmod(s - LAG - 1 - G, G)
                if 0 <= b < NB and at == 0:
                    out_product(b)

        @block.scalar
        def _(act):
            def weight_hi(m):
                act.wait_ge(wt_psum, m + 1)
                tile = ORDER[m] * P
                nc.scalar.copy(whi[:, :, tile:tile + P], ps[:, WB + m % 4].rearrange("p (c e) -> p c e", c=C)
                               ).then_inc(whi_done, 1)

            act.wait_ge(ln[2], 1)
            nc.scalar.activation(std[:], var[:], ACT.Sqrt).then_inc(ln[3], 1)
            for m in range(4):
                weight_hi(m)
            for b in range(NB):
                act.wait_ge(xT_psum, b + 1)
                nc.scalar.copy(xhi[:, :, b * P:(b + 1) * P], ps[:, XB + b % 2].rearrange("p (c t) -> p c t", c=C)
                               ).then_inc(xhi_done, 1)
            for m in range(4, TILES):
                weight_hi(m)
            for s in range(U + LAG + 2):
                if s < U:
                    act.wait_ge(max_done, s + 1)
                    if s >= BUFS:
                        act.wait_ge(t_psum, s - BUFS + 1)
                    for g in range(G):
                        ins = nc.scalar.activation(prob[:, s % BUFS, g], ps[:, LB + s % 2, g * P:(g + 1) * P], ACT.Exp,
                                                   bias=negm[:, s, g:g + 1], accum_out=sums[:, s, g:g + 1])
                    ins.then_inc(exp_done, 1)
                u = s - LAG - 1
                if 0 <= u < U and u % G == G - 1:
                    b = u // G
                    act.wait_ge(pv_psum, b + 1)
                    if b >= 2:
                        act.wait_ge(fc_psum, b - 1)
                    nc.scalar.copy(aohi[:, b % 2], ps[:, AB + b % 2].rearrange("p (c q) -> p c q", c=C)).then_inc(aohi_done, 1)
                if s == U:
                    act.wait_ge(small_in, SMALL)
                    nc.scalar.activation(M.gate[:, 1], M.gate[:, 0], ACT.Exp, scale=-1.0).then_inc(egate_done, 1)

        @block.vector
        def _(dve):
            def weight_lo(m):
                dve.wait_ge(whi_done, m + 1)
                tile = ORDER[m] * P
                nc.vector.tensor_tensor(wlo[:, :, tile:tile + P], ps[:, WB + m % 4].rearrange("p (c e) -> p c e", c=C),
                                        whi[:, :, tile:tile + P].bitcast(F32), ALU.subtract).then_inc(wlo_done, 1)

            def v_tile(b):
                dve.wait_ge(v_psum, b + 1)
                if b >= 2:
                    dve.wait_ge(v_done, b - 1)
                nc.vector.tensor_tensor(vb[:, b % 2], ps[:, VB + b % 2].rearrange("p (h d) -> p h d", h=H), bv_b[:],
                                        ALU.add).then_inc(vb_done, 1)
                dve.wait_ge(vb_done, b + 1)
                nc.vector.tensor_tensor(v[:, b], vb[:, b % 2], hm_b[:, :, None].broadcast_to([P, H, HD]),
                                        ALU.mult).then_inc(v_done, 1)

            for b in range(NB):
                nc.vector.bn_aggr(mv[:, b], stats[:, b]).then_inc(ln[1], 1)
            layer_norm_apply(nc, dve, x2, xn, (mv, var, std, rstd), ln, NB)
            for m in range(4):
                weight_lo(m)
            for b in range(NB):
                dve.wait_ge(xhi_done, b + 1)
                nc.vector.tensor_tensor(xlo[:, :, b * P:(b + 1) * P], ps[:, XB + b % 2].rearrange("p (c t) -> p c t", c=C),
                                        xhi[:, :, b * P:(b + 1) * P].bitcast(F32), ALU.subtract).then_inc(xlo_done, 1)
            for m in range(4, 2 * G):
                weight_lo(m)
            dve.wait_ge(small_in, SMALL)
            dve.wait_ge(rows_small_in, 16 * 3 * G)
            nc.vector.tensor_scalar(hmT[:, 0], hmT[:, 1], HD ** -0.5, None, ALU.mult).then_inc(hm_done, 1)
            dve.wait_ge(hm_done, 1)
            for j in range(2 * G):
                g, t = divmod(j, 2)
                dve.wait_ge(qk_psum, j + 1)
                nc.vector.tensor_scalar(qkT[:, t, g], ps[:, XB + j % 2], bqk[:, t, g:g + 1], hmT[:, t, g:g + 1],
                                        ALU.add, ALU.mult).then_inc(qk_done, 1)
                weight_lo(2 * G + j)
            for s in range(U + LAG + 2):
                if s < U:
                    dve.wait_ge(l_psum, s + 1)
                    nc.vector.tensor_reduce(negm[:, s], ps[:, LB + s % 2].rearrange("p (g k) -> p g k", g=G), AX.X, ALU.max,
                                            negate=True).then_inc(max_done, 1)
                if 1 <= s <= U:
                    dve.wait_ge(exp_done, s)
                    nc.vector.reciprocal(rinv[:, s - 1], sums[:, s - 1]).then_inc(rinv_done, 1)
                if s < NB:
                    v_tile(s)
                u = s - LAG
                if 0 <= u < U:
                    dve.wait_ge(t_psum, u + 1)
                    if u >= 2 * G:
                        dve.wait_ge(pv_psum, u // G - 1)
                    nc.vector.tensor_copy(pT[:, u % (2 * G)], ps[:, PB + u % 2].rearrange("p (g q) -> p g q", g=G)
                                          ).then_inc(t_done, 1)
                u = s - LAG - 1
                if 0 <= u < U and u % G == G - 1:
                    b = u // G
                    dve.wait_ge(aohi_done, b + 1)
                    nc.vector.tensor_tensor(aolo[:, b % 2], ps[:, AB + b % 2].rearrange("p (c q) -> p c q", c=C),
                                            aohi[:, b % 2].bitcast(F32), ALU.subtract).then_inc(aolo_done, 1)
                b, at = divmod(s - LAG - 1 - G, G)
                if 0 <= b < NB and at == 0:
                    dve.wait_ge(fc_psum, b + 1)
                    dve.wait_ge(x1b_done, b + 1)
                    nc.vector.tensor_tensor(x2[:, b], ps[:, FB], x2[:, b], ALU.add).then_inc(x2_done, 1)
                    dve.wait_ge(x2_done, b + 1)
                    nc.vector.bn_stats(stats[:, b], x2[:, b]).then_inc(M.ln[0], 1)
                    dve.wait_ge(M.ln[0], b + 1)
                    nc.vector.bn_aggr(mv[:, b], stats[:, b]).then_inc(M.ln[1], 1)
                if s == U + 1:
                    dve.wait_ge(egate_done, 1)
                    nc.vector.tensor_scalar(M.gate[:, 2], M.gate[:, 1], 1.0, None, ALU.add).then_inc(gate_done, 1)
                    dve.wait_ge(gate_done, 1)
                    nc.vector.reciprocal(M.gate[:, 3], M.gate[:, 2]).then_inc(gate_done, 1)


def expert_attention(nc, Z, M, sim_matrix, projections, out):
    NB, C, D = Z.NB, Z.C, Z.D
    E, HD = projections[0].shape[0], projections[0].shape[2]
    EG = BANK // HD
    NG = E // EG
    TILES = 3 * NG
    ALL = 4 * NG
    TOK = NB * P
    SCALE = HD ** -0.5
    NORM_EPS = 1e-12
    NEG = -3e38
    ATTEND = 2 * NG
    YB = 2
    HB = (0, 1, 6, 7)
    SIMB, GATEB, SB_, PTB = 5, 0, 6, 7
    OUTS = [(m, b, e) for m in range(TILES, ALL) for pair in range(0, NB, 2) for e in range(EG) for b in (pair, pair + 1)]
    with ExitStack() as ctx:
        sb = lambda name, shape, dt=F32: ctx.enter_context(nc.sbuf_tensor("d_" + name, shape, dt))
        sem = lambda name: ctx.enter_context(nc.semaphore("d_" + name))
        ps = ctx.enter_context(nc.psum_tensor("d_ps", [P, 8, BANK], F32))
        x2 = M.x2[:].rearrange("p (b d) -> p b d", b=NB)
        raw, ident, ln, mv = M.w_tiles, M.ident, M.ln, M.mv[:].rearrange("p (b s) -> p b s", b=NB)
        whi = sb("whi", [P, 2, C, BANK], F32R)
        wlo = sb("wlo", [P, 2, C, BANK], F32R)
        xn = sb("xn", [P, NB, D])
        hhi = sb("hhi", [P, C, TOK], F32R)
        hlo = sb("hlo", [P, C, TOK], F32R)
        acc = sb("acc", [P, 3, NB, EG, HD])
        qkv = sb("qkv", [P, 3, NB, HD])
        qkT = sb("qkT", [P, 2, TOK])
        prob = sb("prob", [P, NB, P])
        probT = sb("probT", [P, NB, P])
        aohi, aolo = sb("aohi", [P, NB, P], F32R), sb("aolo", [P, NB, P], F32R)
        cmask = sb("cmask", [P, P])
        sm = sb("sm", [P, C, E])
        sm_split = sb("sm_split", [P, C, 2 * E], F32R)
        sq = sb("sq", [P, C, E])
        ones = sb("ones", [P, P])
        junk = sb("junk", [P, D])
        norm = sb("norm", [P, 4, NB + E])
        lgs, lg0 = sb("lgs", [P, NB, E]), sb("lg0", [P, NB, E])
        lg = sb("lg", [P, NB, E])
        rev = sb("rev", [P, E])
        g = sb("g", [P, 16, NB, E])
        g1 = sb("g1", [P, 8, NB])
        rw = sb("rw", [P, NB, E])
        mx, nmx, sums, rinv = sb("mx", [P, NB]), sb("nmx", [P, NB]), sb("sums", [P, NB]), sb("rinv", [P, NB])
        var, std, rstd = sb("var", [P, NB]), sb("std", [P, NB]), sb("rstd", [P, NB])

        small_in, const_done, sq_done = sem("small_in"), sem("const_done"), sem("sq_done")
        hT_psum, hhi_done, hlo_done = sem("hT_psum"), sem("hhi_done"), sem("hlo_done")
        smhi_done, smlo_done = sem("smhi_done"), sem("smlo_done")
        whi_done, wlo_done = sem("whi_done"), sem("wlo_done")
        sim_psum, gate_psum, root_done, gexp_done = sem("sim_psum"), sem("gate_psum"), sem("root_done"), sem("gexp_done")
        chain = sem("chain")
        square_done, norm_done, gsub_done = sem("square_done"), sem("norm_done"), sem("gsub_done")
        y_psum, y_used = sem("y_psum"), sem("y_used")
        qkv_done, qkT_psum, qkT_done = sem("qkv_done"), sem("qkT_psum"), sem("qkT_done")
        s_psum, max_done, exp_done, prob_done = sem("s_psum"), sem("max_done"), sem("exp_done"), sem("prob_done")
        pT_psum, pT_done, ao_psum = sem("pT_psum"), sem("pT_done"), sem("ao_psum")
        aohi_done, aolo_done = sem("aohi_done"), sem("aolo_done")
        o_psum, o_used, stored = sem("o_psum"), sem("o_used"), sem("stored")
        block = ctx.enter_context(nc.Block())

        @block.sync
        def _(sp):
            for m in range(4, ALL):
                sp.wait_ge(wlo_done, m - 3)
                load_tile(sp, Z, M, projections, m)
            for b in range(NB):
                sp.wait_ge(o_used, max(n for n, o in enumerate(OUTS) if o[1] == b) + 1)
                sp.dma_start(out[b], x2[:, b]).then_inc(stored, 16)
            sp.wait_ge(stored, 16 * NB)

        @block.gpsimd
        def _(pool):
            pool.dma_start(sm[:], sim_matrix.rearrange("(c p) e -> p c e", p=P)).then_inc(small_in, 16)
            nc.gpsimd.memset(ones[:], 1.0).then_inc(const_done, 1)
            nc.gpsimd.memset(cmask[:], 0.0).then_inc(const_done, 1)
            nc.gpsimd.iota(rev[:], pattern=[[-1, E]], base=E, channel_multiplier=0,
                           allow_small_or_imprecise_dtypes=True).then_inc(const_done, 1)
            pool.wait_ge(const_done, 3)
            nc.gpsimd.affine_select(out=cmask[:], in_=cmask[:], compare_op=ALU.is_ge, fill=NEG, base=0,
                                    pattern=[[-1, P]], channel_multiplier=1).then_inc(const_done, 1)
            for m in range(TILES + 1, ALL):
                pool.wait_ge(whi_done, m + 1)
                nc.gpsimd.tensor_tensor(wlo[:, m % 2], raw[:, m % 4], whi[:, m % 2].bitcast(F32), ALU.subtract
                                        ).then_inc(wlo_done, 1)

        @block.tensor
        def _(pe):
            def product(m, b):
                n = m * NB + b
                if n >= 4:
                    pe.wait_ge(y_used, (n - 3) * EG)
                elif YB + n == SIMB:
                    pe.wait_ge(norm_done, 1)
                pe.wait_ge(whi_done, m + 1)
                pe.wait_ge(hhi_done, b + 1)
                terms = [(hh, ww, c) for hh, ww in ((hhi, whi), (hlo, whi), (hhi, wlo)) for c in range(C)]
                for i, (hh, ww, c) in enumerate(terms):
                    if i == C:
                        pe.wait_ge(hlo_done, b + 1)
                    if i == 2 * C:
                        pe.wait_ge(wlo_done, m + 1)
                    mm = nc.tensor.matmul(ps[:, YB + n % 4], hh[:, c, b * P:(b + 1) * P], ww[:, m % 2, c],
                                          start=i == 0, stop=i == len(terms) - 1)
                mm.then_inc(y_psum, 1)

            def gate_logits():
                pe.wait_ge(hlo_done, NB)
                pe.wait_ge(smlo_done, 1)
                terms = [(hh, c) for hh in (hhi, hlo) for c in range(C)]
                for b in range(NB):
                    for i, (hh, c) in enumerate(terms):
                        mm = nc.tensor.matmul(ps[:, GATEB, b * 2 * E:(b + 1) * 2 * E], hh[:, c, b * P:(b + 1) * P],
                                              sm_split[:, c], start=i == 0, stop=i == len(terms) - 1)
                mm.then_inc(gate_psum, 1)

            def transpose_qk():
                for t in range(2):
                    pe.wait_ge(qkv_done, t + 1)
                    for b in range(NB):
                        mm = nc.tensor.transpose(ps[:, t, b * P:(b + 1) * P], qkv[:, t, b], ident[:])
                    mm.then_inc(qkT_psum, 1)

            def scores():
                pe.wait_ge(qkT_done, 2)
                for b in range(NB):
                    mm = nc.tensor.matmul(ps[:, SB_, b * P:(b + 1) * P], qkT[:, 0, b * P:(b + 1) * P],
                                          qkT[:, 1, b * P:(b + 1) * P], start=True, stop=True)
                mm.then_inc(s_psum, 1)

            def transpose_probs():
                for b in range(NB):
                    pe.wait_ge(prob_done, b + 1)
                    mm = nc.tensor.transpose(ps[:, PTB, b * P:(b + 1) * P], prob[:, b], ident[:])
                mm.then_inc(pT_psum, 1)

            def attend(b):
                pe.wait_ge(pT_done, 1)
                pe.wait_ge(qkv_done, 2 + b + 1)
                nc.tensor.matmul(ps[:, HB[b], :P], qkv[:, 2, b], probT[:, b], start=True, stop=True).then_inc(ao_psum, 1)

            def output(n):
                m, b, e = OUTS[n]
                pe.wait_ge(*(y_used, (TILES * NB + n - 3) * EG) if n < 4 else (o_used, n - 3))
                if e == 0:
                    pe.wait_ge(wlo_done, m + 1)
                pe.wait_ge(aolo_done, b + 1)
                terms = ((aohi, whi), (aolo, whi), (aohi, wlo))
                for i, (aa, ww) in enumerate(terms):
                    mm = nc.tensor.matmul(ps[:, YB + n % 4], aa[:, b], ww[:, m % 2, e], start=i == 0, stop=i == 2)
                mm.then_inc(o_psum, 1)

            for b in range(NB):
                pe.wait_ge(ln[5], b + 1)
                for c in range(C):
                    mm = nc.tensor.transpose(ps[:, HB[b], c * P:(c + 1) * P], xn[:, b, c * P:(c + 1) * P], ident[:])
                mm.then_inc(hT_psum, 1)
            pe.wait_ge(const_done, 4)
            pe.wait_ge(sq_done, 1)
            for c in range(C):
                mm = nc.tensor.matmul(ps[:, SIMB, :E], ones[:], sq[:, c], start=c == 0, stop=c == C - 1)
            mm.then_inc(sim_psum, 1)
            after = {(0, 0): gate_logits, (ATTEND, 1): transpose_qk, (ATTEND, 3): scores, (ATTEND + 2, 1): transpose_probs}
            for m in range(TILES):
                for b in range(NB):
                    product(m, b)
                    if (m, b) in after:
                        after[m, b]()
                    if m == TILES - 1 and b >= 1:
                        attend(b - 1)
            for n in range(len(OUTS)):
                output(n)
                if n == 1:
                    attend(NB - 1)

        @block.scalar
        def _(act):
            def weight_hi(m):
                act.wait_ge(M.tile_in[m % 4], 16 * 4 * (m // 4 + 1))
                if m >= TILES + 2:
                    act.wait_ge(o_psum, (m - 1 - TILES) * EG * NB)
                elif m >= 2:
                    act.wait_ge(y_psum, (m - 1) * NB)
                nc.scalar.copy(whi[:, m % 2], raw[:, m % 4]).then_inc(whi_done, 1)

            act.wait_ge(ln[2], 1)
            nc.scalar.activation(std[:], var[:], ACT.Sqrt).then_inc(ln[3], 1)
            weight_hi(0)
            act.wait_ge(small_in, 16)
            nc.scalar.copy(sm_split[:, :, :E], sm[:]).then_inc(smhi_done, 1)
            for b in range(NB):
                act.wait_ge(hT_psum, b + 1)
                nc.scalar.copy(hhi[:, :, b * P:(b + 1) * P], ps[:, HB[b]].rearrange("p (c t) -> p c t", c=C)
                               ).then_inc(hhi_done, 1)
            for b in range(NB):
                if b >= 1:
                    act.wait_ge(square_done, b)
                nc.scalar.activation(junk[:], xn[:, b], ACT.Square, accum_out=norm[:, 0, b:b + 1]).then_inc(square_done, 1)
            act.wait_ge(norm_done, 2)
            nc.scalar.activation(norm[:, 2], norm[:, 1], ACT.Sqrt).then_inc(root_done, 1)
            weight_hi(1)
            act.wait_ge(gsub_done, 1)
            nc.scalar.activation(g[:, 11], g[:, 10], ACT.Exp).then_inc(gexp_done, 1)
            for m in range(2, ALL):
                if m == ATTEND + 3:
                    for b in range(NB):
                        act.wait_ge(max_done, b + 1)
                        nc.scalar.activation(prob[:, b], prob[:, b], ACT.Exp, bias=nmx[:, b:b + 1], scale=SCALE,
                                             accum_out=sums[:, b:b + 1]).then_inc(exp_done, 1)
                if m == TILES:
                    act.wait_ge(pT_psum, 1)
                    nc.scalar.copy(probT[:], ps[:, PTB].rearrange("p (b t) -> p b t", b=NB)).then_inc(pT_done, 1)
                if m == TILES + 1:
                    for b in range(NB):
                        act.wait_ge(ao_psum, b + 1)
                        nc.scalar.copy(aohi[:, b], ps[:, HB[b], :P]).then_inc(aohi_done, 1)
                weight_hi(m)

        @block.vector
        def _(dve):
            V = nc.vector
            count = [0]

            def step(ins):
                count[0] += 1
                ins.then_inc(chain, 1)
                dve.wait_ge(chain, count[0])

            def weight_lo(m):
                dve.wait_ge(whi_done, m + 1)
                V.tensor_tensor(wlo[:, m % 2], raw[:, m % 4], whi[:, m % 2].bitcast(F32), ALU.subtract).then_inc(wlo_done, 1)

            def tokens_lo(b):
                dve.wait_ge(hhi_done, b + 1)
                V.tensor_tensor(hlo[:, :, b * P:(b + 1) * P], ps[:, HB[b]].rearrange("p (c t) -> p c t", c=C),
                                hhi[:, :, b * P:(b + 1) * P].bitcast(F32), ALU.subtract).then_inc(hlo_done, 1)

            layer_norm_apply(nc, dve, x2, xn, (mv, var, std, rstd), ln, NB)
            dve.wait_ge(small_in, 16)
            V.tensor_tensor(sq[:], sm[:], sm[:], ALU.mult).then_inc(sq_done, 1)
            tokens_lo(0)
            weight_lo(0)
            dve.wait_ge(smhi_done, 1)
            V.tensor_tensor(sm_split[:, :, E:], sm[:], sm_split[:, :, :E].bitcast(F32), ALU.subtract).then_inc(smlo_done, 1)
            for b in range(1, NB):
                tokens_lo(b)
            dve.wait_ge(sim_psum, 1)
            V.tensor_scalar(norm[:, 1, NB:], ps[:, SIMB, :E], NORM_EPS, None, ALU.add).then_inc(norm_done, 1)
            dve.wait_ge(square_done, NB)
            V.tensor_scalar(norm[:, 1, :NB], norm[:, 0, :NB], NORM_EPS, None, ALU.add).then_inc(norm_done, 1)
            dve.wait_ge(root_done, 1)
            step(V.reciprocal(norm[:, 3], norm[:, 2]))
            weight_lo(1)
            dve.wait_ge(gate_psum, 1)
            step(V.tensor_reduce(lgs[:], ps[:, GATEB, :NB * 2 * E].rearrange("p (b i e) -> p b e i", b=NB, i=2), AX.X, ALU.add))
            for b in range(NB):
                ins = V.scalar_tensor_tensor(lg0[:, b], lgs[:, b], norm[:, 3, b:b + 1],
                                             norm[:, 3, NB:], ALU.mult, ALU.mult)
            step(ins)
            step(V.tensor_tensor(lg[:], lg0[:], M.gate[:, 3, None, :].broadcast_to([P, NB, E]), ALU.subtract))
            wide = lambda a: a[:, :, None].broadcast_to([P, NB, E])
            revb = rev[:, None, :].broadcast_to([P, NB, E])
            dve.wait_ge(const_done, 4)
            left, top = lg[:], []
            for k in range(2):
                o = 3 * k
                step(V.tensor_reduce(g1[:, 2 * k], left, AX.X, ALU.max))
                step(V.tensor_tensor(g[:, o], left, wide(g1[:, 2 * k]), ALU.is_equal))
                step(V.tensor_tensor(g[:, o + 1], g[:, o], revb, ALU.mult))
                step(V.tensor_reduce(g1[:, 2 * k + 1], g[:, o + 1], AX.X, ALU.max))
                step(V.tensor_tensor(g[:, o + 2], revb, wide(g1[:, 2 * k + 1]), ALU.is_equal))
                top.append(g[:, o + 2])
                if k == 0:
                    step(V.scalar_tensor_tensor(g[:, 6], g[:, 2], -16.0, lg[:], ALU.mult, ALU.add))
                    left = g[:, 6]
            step(V.tensor_tensor(g[:, 7], top[0], top[1], ALU.add))
            step(V.tensor_scalar(g[:, 8], lg[:], 0.0, None, ALU.is_gt))
            step(V.tensor_scalar(g1[:, 4], g1[:, 0], 0.0, None, ALU.is_le))
            step(V.tensor_tensor(g[:, 9], g[:, 7], wide(g1[:, 4]), ALU.mult))
            step(V.tensor_tensor(g[:, 13], g[:, 8], g[:, 9], ALU.add))
            step(V.tensor_scalar(g[:, 12], lg[:], 0.0, None, ALU.max))
            step(V.tensor_reduce(g1[:, 5], g[:, 12], AX.X, ALU.max))
            V.tensor_tensor(g[:, 10], g[:, 12], wide(g1[:, 5]), ALU.subtract).then_inc(gsub_done, 1)
            dve.wait_ge(gexp_done, 1)
            step(V.tensor_tensor(g[:, 14], g[:, 11], g[:, 13], ALU.mult))
            step(V.tensor_reduce(g1[:, 6], g[:, 14], AX.X, ALU.add))
            step(V.reciprocal(g1[:, 7], g1[:, 6]))
            step(V.tensor_tensor(rw[:], g[:, 14], wide(g1[:, 7]), ALU.mult))

            def use_product(m, b):
                t, eg = divmod(m, NG)
                n = m * NB + b
                dve.wait_ge(y_psum, n + 1)
                if eg > 0:
                    dve.wait_ge(y_used, EG * (n - NB + 1))
                for j in range(EG):
                    e = eg * EG + j
                    y, w = ps[:, YB + n % 4, j * HD:(j + 1) * HD], rw[:, b, e:e + 1]
                    if eg == 0:
                        ins = V.tensor_scalar(acc[:, t, b, j], y, w, None, ALU.mult)
                    else:
                        ins = V.scalar_tensor_tensor(acc[:, t, b, j], y, w, acc[:, t, b, j], ALU.mult, ALU.add)
                    ins.then_inc(y_used, 1)

            def attention_lo(b):
                dve.wait_ge(aohi_done, b + 1)
                V.tensor_tensor(aolo[:, b], ps[:, HB[b], :P], aohi[:, b].bitcast(F32), ALU.subtract).then_inc(aolo_done, 1)

            def copy_qkT():
                for t in range(2):
                    dve.wait_ge(qkT_psum, t + 1)
                    V.tensor_copy(qkT[:, t], ps[:, t]).then_inc(qkT_done, 1)

            def score_maxima():
                dve.wait_ge(s_psum, 1)
                step(V.tensor_tensor(prob[:], ps[:, SB_].rearrange("p (b t) -> p b t", b=NB),
                                     cmask[:, None, :].broadcast_to([P, NB, P]), ALU.add))
                step(V.tensor_reduce(mx[:], prob[:], AX.X, ALU.max))
                V.tensor_scalar(nmx[:], mx[:], -SCALE, None, ALU.mult).then_inc(max_done, NB)

            def normalise():
                dve.wait_ge(exp_done, NB)
                step(V.reciprocal(rinv[:], sums[:]))
                for b in range(NB):
                    V.tensor_scalar(prob[:, b], prob[:, b], rinv[:, b:b + 1], None, ALU.mult).then_inc(prob_done, 1)

            after = {(ATTEND, 2): copy_qkT, (ATTEND + 1, 0): score_maxima, (ATTEND + 1, 3): normalise}
            for m in range(TILES):
                t, eg = divmod(m, NG)
                for b in range(NB):
                    use_product(m, b)
                    if (m, b) in after:
                        after[m, b]()
                    if m == TILES - 1:
                        dve.wait_ge(y_used, EG * (m * NB + b + 1))
                        V.tensor_reduce(qkv[:, t, b], acc[:, t, b].rearrange("p j h -> p h j"), AX.X, ALU.add
                                        ).then_inc(qkv_done, 1)
                        if b >= 1:
                            attention_lo(b - 1)
                if m < TILES - 1:
                    weight_lo(m + 2)
                if eg == NG - 1 and t < 2:
                    dve.wait_ge(y_used, EG * NB * (m + 1))
                    V.tensor_reduce(qkv[:, t], acc[:, t].rearrange("p b j h -> p b h j"), AX.X, ALU.add).then_inc(qkv_done, 1)
            for n, (m, b, e) in enumerate(OUTS):
                dve.wait_ge(o_psum, n + 1)
                before = [i for i in range(n) if OUTS[i][1] == b]
                if before:
                    dve.wait_ge(o_used, before[-1] + 1)
                w = (m - TILES) * EG + e
                V.scalar_tensor_tensor(x2[:, b], ps[:, YB + n % 4], rw[:, b, w:w + 1], x2[:, b],
                                       ALU.mult, ALU.add).then_inc(o_used, 1)
                if n == 1:
                    attention_lo(NB - 1)


NAMES = ['x', 'ctx_1024', 'L0_xattn_Wq', 'L0_xattn_bq', 'L0_xattn_Wk', 'L0_xattn_bk', 'L0_xattn_Wv', 'L0_xattn_bv',
         'L0_xattn_Wo', 'L0_xattn_bo', 'L0_attn_head_mask', 'L0_attn_qkv_w', 'L0_attn_qkv_b', 'L0_attn_fc_w',
         'L0_attn_fc_b', 'L0_ffn_sim_matrix', 'L0_ffn_gates', 'L0_ffn_q_proj', 'L0_ffn_k_proj', 'L0_ffn_v_proj',
         'L0_ffn_o_proj']


def perceiver_layer(nc, x, ctx_1024, Wq, bq, Wk, bk, Wv, bv, Wo, bo, head_mask, qkv_w, qkv_b, fc_w, fc_b,
                    sim_matrix, gates, q_proj, k_proj, v_proj, o_proj, out):
    Z = Shapes(x, ctx_1024, gates)
    scratch = lambda name, shape: nc.dram_tensor(name, shape, F32, kind="Internal").ap()
    q_s = scratch("q_s", [2, Z.NP, P, Z.NB * P])
    projections = (q_proj, k_proj, v_proj, o_proj)
    with ExitStack() as ctx:
        M = Shared(ctx, nc, Z)
        with ExitStack() as inner:
            X = CrossShared(inner, nc, Z)
            prepare(nc, Z, M, X, x, ctx_1024, Wq, bq, Wk, Wv, bo, q_s)
            cross_attention(nc, Z, M, X, ctx_1024, Wk, bk, Wv, bv, Wo, q_s,
                            lambda sp, part: load_rows(sp, Z, M, qkv_w, fc_w, part))
        self_attention(nc, Z, M, head_mask, qkv_b, fc_b, gates, projections)
        expert_attention(nc, Z, M, sim_matrix, projections, out)


def kernel(**inputs):
    import numpy as np
    import concourse.bacc as bacc
    from concourse.bass_utils import run_bass_kernel_spmd

    nc = bacc.Bacc("TRN2", target_bir_lowering=False, num_devices=1)
    arrays, args = {}, []
    for name in NAMES:
        a = np.ascontiguousarray(inputs[name])
        arrays[f"in_{name}"] = a
        args.append(nc.dram_tensor(f"in_{name}", a.shape, mybir.dt.from_np(a.dtype), kind="ExternalInput").ap())
    out = nc.dram_tensor("out", inputs["x"].shape, F32, kind="ExternalOutput").ap()
    perceiver_layer(nc, *args, out)
    r = run_bass_kernel_spmd(nc, [arrays], core_ids=[0])
    return r.results[0]["out"]
```
